# Optimizing a Trainium2 kernel written in Bass

```python
import numpy as np
import jax
import jax.numpy as jnp

def _softmax(x, axis=-1):
    return jax.nn.softmax(x, axis=axis)

def _gelu(x):
    return jax.nn.gelu(x, approximate=True)

def _silu(x):
    return jax.nn.silu(x)

def _sigmoid(x):
    return jax.nn.sigmoid(x)

def _layernorm(x, axis=-1, eps=1e-05):
    m = jnp.mean(x, axis=axis, keepdims=True)
    v = jnp.var(x, axis=axis, keepdims=True)
    return (x - m) / jnp.sqrt(v + eps)

def _scatter_add(tgt, idx, src, axis=0):
    return tgt.at[idx].add(src)

def _segment_sum(src, seg, n):
    return jax.ops.segment_sum(src, seg, n)
kernel_name = 'mk_conv_seq_d2_conv_nhwc768_r4_295d19'

def setup_inputs(seed: int=0):
    np.random.seed(seed)
    _w = jnp.asarray

    def _rec_inputs():
        import jax
        import jax.numpy as jnp
        _gk = jax.random.key(seed)
        x = -0.0008768 + 1.001 * jax.random.normal(jax.random.fold_in(_gk, 1), (1, 48, 48, 192), jnp.float32)
        return x
    x = _rec_inputs()

    def _L0_conv_setup():
        import jax, jax.numpy as jnp
        import numpy as np
        NUM_HEADS = 12
        LN_EPS = 1e-05

        def layernorm(x, g, b):
            mu = jnp.mean(x, axis=-1, keepdims=True)
            var = jnp.var(x, axis=-1, keepdims=True)
            return (x - mu) * jax.lax.rsqrt(var + LN_EPS) * g + b

        def _block(x, qkv_w, qkv_b, proj_w, proj_b, rel_pos_h, rel_pos_w, ln1_g, ln1_b, ln2_g, ln2_b, mlp_w1, mlp_b1, mlp_w2, mlp_b2):
            B, H, W, C = x.shape
            nh = NUM_HEADS
            hd = C // nh
            scale = hd ** (-0.5)
            shortcut = x
            xn = layernorm(x, ln1_g, ln1_b)
            qkv = xn.reshape(B, H * W, C) @ qkv_w + qkv_b
            qkv = qkv.reshape(B, H * W, 3, nh, hd).transpose(2, 0, 3, 1, 4)
            qkv = qkv.reshape(3, B * nh, H * W, hd)
            q, k, v = (qkv[0], qkv[1], qkv[2])
            attn = jnp.einsum('bqc,bkc->bqk', q * scale, k)
            coords = jnp.arange(H)[:, None] - jnp.arange(H)[None, :] + (H - 1)
            Rh = rel_pos_h[coords]
            Rw = rel_pos_w[coords]
            r_q = q.reshape(B * nh, H, W, hd)
            rel_h = jnp.einsum('bhwc,hkc->bhwk', r_q, Rh)
            rel_w = jnp.einsum('bhwc,wkc->bhwk', r_q, Rw)
            attn = (attn.reshape(B * nh, H, W, H, W) + rel_h[:, :, :, :, None] + rel_w[:, :, :, None, :]).reshape(B * nh, H * W, H * W)
            attn = jax.nn.softmax(attn, axis=-1)
            out = jnp.einsum('bqk,bkc->bqc', attn, v)
            out = out.reshape(B, nh, H, W, hd).transpose(0, 2, 3, 1, 4).reshape(B, H, W, C)
            out = out @ proj_w + proj_b
            x = shortcut + out
            xn2 = layernorm(x, ln2_g, ln2_b)
            h = jax.nn.gelu(xn2 @ mlp_w1 + mlp_b1, approximate=False)
            return x + (h @ mlp_w2 + mlp_b2)
        key = jax.random.key(seed)
        ks = jax.random.split(key, 16)
        B, H, W, C = (1, 48, 48, 192)
        hd = C // NUM_HEADS
        mlp_dim = 4 * C
        L = 2 * H - 1
        s = 0.02
        return {'x': jax.random.normal(ks[0], (B, H, W, C), jnp.float32), 'qkv_w': jax.random.normal(ks[1], (C, 3 * C), jnp.float32) * s, 'qkv_b': jnp.zeros((3 * C,), jnp.float32), 'proj_w': jax.random.normal(ks[2], (C, C), jnp.float32) * s, 'proj_b': jnp.zeros((C,), jnp.float32), 'rel_pos_h': jax.random.normal(ks[3], (L, hd), jnp.float32) * s, 'rel_pos_w': jax.random.normal(ks[4], (L, hd), jnp.float32) * s, 'ln1_g': jnp.ones((C,), jnp.float32), 'ln1_b': jnp.zeros((C,), jnp.float32), 'ln2_g': jnp.ones((C,), jnp.float32), 'ln2_b': jnp.zeros((C,), jnp.float32), 'mlp_w1': jax.random.normal(ks[5], (C, mlp_dim), jnp.float32) * s, 'mlp_b1': jnp.zeros((mlp_dim,), jnp.float32), 'mlp_w2': jax.random.normal(ks[6], (mlp_dim, C), jnp.float32) * s, 'mlp_b2': jnp.zeros((C,), jnp.float32)}
    _L0_conv_all = _L0_conv_setup()
    _L0_conv_in = {k: v for k, v in _L0_conv_all.items() if k in ('qkv_w', 'qkv_b', 'proj_w', 'proj_b', 'rel_pos_h', 'rel_pos_w', 'ln1_g', 'ln1_b', 'ln2_g', 'ln2_b', 'mlp_w1', 'mlp_b1', 'mlp_w2', 'mlp_b2')}
    del _L0_conv_all

    def _L1_conv_setup():
        import jax, jax.numpy as jnp
        import numpy as np
        DIM = 192
        NB = 8
        BS = DIM // NB
        HID = 4 * DIM
        LAM = 0.01
        SCALE = 0.02

        def layernorm(x, g, b, eps=1e-05):
            m = x.mean(axis=-1, keepdims=True)
            v = ((x - m) ** 2).mean(axis=-1, keepdims=True)
            return (x - m) / jnp.sqrt(v + eps) * g + b

        def softshrink(x, lam):
            return jnp.sign(x) * jnp.maximum(jnp.abs(x) - lam, 0.0)

        def cmul_add(ar, ai, w, b):
            wr, wi = (w[..., 0], w[..., 1])
            outr = jnp.einsum('bxyki,kio->bxyko', ar, wr) - jnp.einsum('bxyki,kio->bxyko', ai, wi) + b[..., 0]
            outi = jnp.einsum('bxyki,kio->bxyko', ai, wr) + jnp.einsum('bxyki,kio->bxyko', ar, wi) + b[..., 1]
            return (outr, outi)

        def afno2d(x, w1, b1, w2, b2):
            bias = x
            B, H, W, C = x.shape
            Wf = W // 2 + 1
            total_modes = H // 2 + 1
            kept = int(total_modes * 1.0)
            xf = jnp.fft.rfft2(x.astype(jnp.float32), axes=(1, 2), norm='ortho')
            xf = xf.reshape(B, H, Wf, NB, BS)
            xs = xf[:, total_modes - kept:total_modes + kept, :kept]
            xr, xi = (jnp.real(xs), jnp.imag(xs))
            o1r, o1i = cmul_add(xr, xi, w1, b1)
            o1r, o1i = (jax.nn.relu(o1r), jax.nn.relu(o1i))
            o2r, o2i = cmul_add(o1r, o1i, w2, b2)
            o2r, o2i = (softshrink(o2r, LAM), softshrink(o2i, LAM))
            full = jnp.zeros((B, H, Wf, NB, BS), dtype=xf.dtype)
            full = full.at[:, total_modes - kept:total_modes + kept, :kept].set(o2r + 1j * o2i)
            out = jnp.fft.irfft2(full.reshape(B, H, Wf, C), s=(H, W), axes=(1, 2), norm='ortho')
            return out.astype(x.dtype) + bias
        key = jax.random.key(seed)
        ks = jax.random.split(key, 12)
        B, H, W = (2, 90, 45)
        x = jax.random.normal(ks[0], (B, H, W, DIM), dtype=jnp.float32)
        w1 = SCALE * jax.random.normal(ks[1], (NB, BS, BS, 2), dtype=jnp.float32)
        b1 = SCALE * jax.random.normal(ks[2], (NB, BS, 2), dtype=jnp.float32)
        w2 = SCALE * jax.random.normal(ks[3], (NB, BS, BS, 2), dtype=jnp.float32)
        b2 = SCALE * jax.random.normal(ks[4], (NB, BS, 2), dtype=jnp.float32)
        g1 = jnp.ones((DIM,), jnp.float32)
        be1 = jnp.zeros((DIM,), jnp.float32)
        g2 = jnp.ones((DIM,), jnp.float32)
        be2 = jnp.zeros((DIM,), jnp.float32)
        lim1 = 1.0 / np.sqrt(DIM)
        lim2 = 1.0 / np.sqrt(HID)
        fc1_w = jax.random.uniform(ks[5], (DIM, HID), jnp.float32, -lim1, lim1)
        fc1_b = jax.random.uniform(ks[6], (HID,), jnp.float32, -lim1, lim1)
        fc2_w = jax.random.uniform(ks[7], (HID, DIM), jnp.float32, -lim2, lim2)
        fc2_b = jax.random.uniform(ks[8], (DIM,), jnp.float32, -lim2, lim2)
        return {'x': x, 'g1': g1, 'be1': be1, 'g2': g2, 'be2': be2, 'w1': w1, 'b1': b1, 'w2': w2, 'b2': b2, 'fc1_w': fc1_w, 'fc1_b': fc1_b, 'fc2_w': fc2_w, 'fc2_b': fc2_b}
    _L1_conv_all = _L1_conv_setup()
    _L1_conv_in = {k: v for k, v in _L1_conv_all.items() if k in ('g1', 'be1', 'g2', 'be2', 'w1', 'b1', 'w2', 'b2', 'fc1_w', 'fc1_b', 'fc2_w', 'fc2_b')}
    del _L1_conv_all
    return {'x': x, 'L0_conv_qkv_w': _L0_conv_in['qkv_w'], 'L0_conv_qkv_b': _L0_conv_in['qkv_b'], 'L0_conv_proj_w': _L0_conv_in['proj_w'], 'L0_conv_proj_b': _L0_conv_in['proj_b'], 'L0_conv_rel_pos_h': _L0_conv_in['rel_pos_h'], 'L0_conv_rel_pos_w': _L0_conv_in['rel_pos_w'], 'L0_conv_ln1_g': _L0_conv_in['ln1_g'], 'L0_conv_ln1_b': _L0_conv_in['ln1_b'], 'L0_conv_ln2_g': _L0_conv_in['ln2_g'], 'L0_conv_ln2_b': _L0_conv_in['ln2_b'], 'L0_conv_mlp_w1': _L0_conv_in['mlp_w1'], 'L0_conv_mlp_b1': _L0_conv_in['mlp_b1'], 'L0_conv_mlp_w2': _L0_conv_in['mlp_w2'], 'L0_conv_mlp_b2': _L0_conv_in['mlp_b2'], 'L1_conv_g1': _L1_conv_in['g1'], 'L1_conv_be1': _L1_conv_in['be1'], 'L1_conv_g2': _L1_conv_in['g2'], 'L1_conv_be2': _L1_conv_in['be2'], 'L1_conv_w1': _L1_conv_in['w1'], 'L1_conv_b1': _L1_conv_in['b1'], 'L1_conv_w2': _L1_conv_in['w2'], 'L1_conv_b2': _L1_conv_in['b2'], 'L1_conv_fc1_w': _L1_conv_in['fc1_w'], 'L1_conv_fc1_b': _L1_conv_in['fc1_b'], 'L1_conv_fc2_w': _L1_conv_in['fc2_w'], 'L1_conv_fc2_b': _L1_conv_in['fc2_b']}

def reference(x, L0_conv_qkv_w, L0_conv_qkv_b, L0_conv_proj_w, L0_conv_proj_b, L0_conv_rel_pos_h, L0_conv_rel_pos_w, L0_conv_ln1_g, L0_conv_ln1_b, L0_conv_ln2_g, L0_conv_ln2_b, L0_conv_mlp_w1, L0_conv_mlp_b1, L0_conv_mlp_w2, L0_conv_mlp_b2, L1_conv_g1, L1_conv_be1, L1_conv_g2, L1_conv_be2, L1_conv_w1, L1_conv_b1, L1_conv_w2, L1_conv_b2, L1_conv_fc1_w, L1_conv_fc1_b, L1_conv_fc2_w, L1_conv_fc2_b):
    import jax
    import jax.numpy as jnp

    def _L0_conv_ref(x, qkv_w, qkv_b, proj_w, proj_b, rel_pos_h, rel_pos_w, ln1_g, ln1_b, ln2_g, ln2_b, mlp_w1, mlp_b1, mlp_w2, mlp_b2):
        import jax, jax.numpy as jnp
        import numpy as np
        NUM_HEADS = 12
        LN_EPS = 1e-05

        def layernorm(x, g, b):
            mu = jnp.mean(x, axis=-1, keepdims=True)
            var = jnp.var(x, axis=-1, keepdims=True)
            return (x - mu) * jax.lax.rsqrt(var + LN_EPS) * g + b

        def _block(x, qkv_w, qkv_b, proj_w, proj_b, rel_pos_h, rel_pos_w, ln1_g, ln1_b, ln2_g, ln2_b, mlp_w1, mlp_b1, mlp_w2, mlp_b2):
            B, H, W, C = x.shape
            nh = NUM_HEADS
            hd = C // nh
            scale = hd ** (-0.5)
            shortcut = x
            xn = layernorm(x, ln1_g, ln1_b)
            qkv = xn.reshape(B, H * W, C) @ qkv_w + qkv_b
            qkv = qkv.reshape(B, H * W, 3, nh, hd).transpose(2, 0, 3, 1, 4)
            qkv = qkv.reshape(3, B * nh, H * W, hd)
            q, k, v = (qkv[0], qkv[1], qkv[2])
            attn = jnp.einsum('bqc,bkc->bqk', q * scale, k)
            coords = jnp.arange(H)[:, None] - jnp.arange(H)[None, :] + (H - 1)
            Rh = rel_pos_h[coords]
            Rw = rel_pos_w[coords]
            r_q = q.reshape(B * nh, H, W, hd)
            rel_h = jnp.einsum('bhwc,hkc->bhwk', r_q, Rh)
            rel_w = jnp.einsum('bhwc,wkc->bhwk', r_q, Rw)
            attn = (attn.reshape(B * nh, H, W, H, W) + rel_h[:, :, :, :, None] + rel_w[:, :, :, None, :]).reshape(B * nh, H * W, H * W)
            attn = jax.nn.softmax(attn, axis=-1)
            out = jnp.einsum('bqk,bkc->bqc', attn, v)
            out = out.reshape(B, nh, H, W, hd).transpose(0, 2, 3, 1, 4).reshape(B, H, W, C)
            out = out @ proj_w + proj_b
            x = shortcut + out
            xn2 = layernorm(x, ln2_g, ln2_b)
            h = jax.nn.gelu(xn2 @ mlp_w1 + mlp_b1, approximate=False)
            return x + (h @ mlp_w2 + mlp_b2)
        return _block(x, qkv_w, qkv_b, proj_w, proj_b, rel_pos_h, rel_pos_w, ln1_g, ln1_b, ln2_g, ln2_b, mlp_w1, mlp_b1, mlp_w2, mlp_b2)

    def _L1_conv_ref(x, g1, be1, g2, be2, w1, b1, w2, b2, fc1_w, fc1_b, fc2_w, fc2_b):
        import jax, jax.numpy as jnp
        import numpy as np
        DIM = 192
        NB = 8
        BS = DIM // NB
        HID = 4 * DIM
        LAM = 0.01
        SCALE = 0.02

        def layernorm(x, g, b, eps=1e-05):
            m = x.mean(axis=-1, keepdims=True)
            v = ((x - m) ** 2).mean(axis=-1, keepdims=True)
            return (x - m) / jnp.sqrt(v + eps) * g + b

        def softshrink(x, lam):
            return jnp.sign(x) * jnp.maximum(jnp.abs(x) - lam, 0.0)

        def cmul_add(ar, ai, w, b):
            wr, wi = (w[..., 0], w[..., 1])
            outr = jnp.einsum('bxyki,kio->bxyko', ar, wr) - jnp.einsum('bxyki,kio->bxyko', ai, wi) + b[..., 0]
            outi = jnp.einsum('bxyki,kio->bxyko', ai, wr) + jnp.einsum('bxyki,kio->bxyko', ar, wi) + b[..., 1]
            return (outr, outi)

        def afno2d(x, w1, b1, w2, b2):
            bias = x
            B, H, W, C = x.shape
            Wf = W // 2 + 1
            total_modes = H // 2 + 1
            kept = int(total_modes * 1.0)
            xf = jnp.fft.rfft2(x.astype(jnp.float32), axes=(1, 2), norm='ortho')
            xf = xf.reshape(B, H, Wf, NB, BS)
            xs = xf[:, total_modes - kept:total_modes + kept, :kept]
            xr, xi = (jnp.real(xs), jnp.imag(xs))
            o1r, o1i = cmul_add(xr, xi, w1, b1)
            o1r, o1i = (jax.nn.relu(o1r), jax.nn.relu(o1i))
            o2r, o2i = cmul_add(o1r, o1i, w2, b2)
            o2r, o2i = (softshrink(o2r, LAM), softshrink(o2i, LAM))
            full = jnp.zeros((B, H, Wf, NB, BS), dtype=xf.dtype)
            full = full.at[:, total_modes - kept:total_modes + kept, :kept].set(o2r + 1j * o2i)
            out = jnp.fft.irfft2(full.reshape(B, H, Wf, C), s=(H, W), axes=(1, 2), norm='ortho')
            return out.astype(x.dtype) + bias
        residual = x
        h = layernorm(x, g1, be1)
        h = afno2d(h, w1, b1, w2, b2)
        h = h + residual
        residual = h
        m = layernorm(h, g2, be2)
        m = jax.nn.gelu(m @ fc1_w + fc1_b, approximate=False) @ fc2_w + fc2_b
        return m + residual

    def _gn(v, G=32, eps=1e-05):
        B_, H_, W_, C_ = v.shape
        g = v.reshape(B_, H_, W_, G, C_ // G)
        m = jnp.mean(g, axis=(1, 2, 4), keepdims=True)
        s = jnp.var(g, axis=(1, 2, 4), keepdims=True)
        return ((g - m) / jnp.sqrt(s + eps)).reshape(v.shape)

    def _ln_c(v, eps=1e-06):
        m = jnp.mean(v, axis=-1, keepdims=True)
        s = jnp.var(v, axis=-1, keepdims=True)
        return (v - m) / jnp.sqrt(s + eps)

    def _ln_t(v, eps=1e-05):
        m = jnp.mean(v, axis=-1, keepdims=True)
        s = jnp.var(v, axis=-1, keepdims=True)
        return (v - m) / jnp.sqrt(s + eps)

    def _to_tokens(v):
        B_, H_, W_, C_ = v.shape
        return v.reshape(B_, H_ * W_, C_)

    def _from_tokens(t, like):
        return t.reshape(like.shape)
    x = _L0_conv_ref(x, L0_conv_qkv_w, L0_conv_qkv_b, L0_conv_proj_w, L0_conv_proj_b, L0_conv_rel_pos_h, L0_conv_rel_pos_w, L0_conv_ln1_g, L0_conv_ln1_b, L0_conv_ln2_g, L0_conv_ln2_b, L0_conv_mlp_w1, L0_conv_mlp_b1, L0_conv_mlp_w2, L0_conv_mlp_b2)
    x = _L1_conv_ref(x, L1_conv_g1, L1_conv_be1, L1_conv_g2, L1_conv_be2, L1_conv_w1, L1_conv_b1, L1_conv_w2, L1_conv_b2, L1_conv_fc1_w, L1_conv_fc1_b, L1_conv_fc2_w, L1_conv_fc2_b)
    return x

_drawn_inputs = setup_inputs


def setup_inputs(seed=0):
    import zlib

    import numpy as np

    out = dict(_drawn_inputs(seed))
    spreads = {'L0_conv_qkv_b': (0.0, 0.281),
     'L0_conv_proj_b': (0.0, 0.1),
     'L0_conv_ln1_g': (1.0, 0.6),
     'L0_conv_ln1_b': (0.0, 0.8),
     'L0_conv_ln2_g': (1.0, 0.6),
     'L0_conv_ln2_b': (0.0, 0.8),
     'L0_conv_mlp_b1': (0.0, 0.28),
     'L0_conv_mlp_b2': (0.0, 0.1),
     'L1_conv_g1': (1.0, 0.2),
     'L1_conv_be1': (0.0, 0.1),
     'L1_conv_g2': (1.0, 0.6),
     'L1_conv_be2': (0.0, 0.8)}
    factors = {'L0_conv_qkv_w': 7.229,
     'L0_conv_rel_pos_h': 8.0,
     'L0_conv_rel_pos_w': 8.0,
     'L1_conv_w1': 8.0,
     'L1_conv_b1': 8.0,
     'L1_conv_w2': 8.0,
     'L1_conv_b2': 6.074,
     'L1_conv_fc1_b': 7.341,
     'L1_conv_fc2_b': 5.241}
    for name, (base, spread) in spreads.items():
        noise = np.random.default_rng([zlib.crc32(name.encode()), seed]).standard_normal(out[name].shape)
        drawn = base * np.exp(spread * noise) if base else spread * noise
        out[name] = jnp.asarray(drawn.astype(out[name].dtype))
    for name, factor in factors.items():
        out[name] = (out[name] * factor).astype(out[name].dtype)
    return out
```

```python
from contextlib import ExitStack

import concourse.bass as bass
from concourse import mybir

F32 = mybir.dt.float32
F16 = mybir.dt.float16
ALU = mybir.AluOpType
ACT = mybir.ActivationFunctionType
AX = mybir.AxisListType.X
ds = bass.ds

S = 48
N = S * S
C = 192
C2 = C // 2
NH = 12
HD = C // NH
SCALE = HD ** -0.5
T = 96
NT = N // T
CT = 4
NC = NT // CT
CW = CT * T
HID = 4 * C
HM = HID // 128
KT = N // 128
QW = 2 * CW
NQ = N // QW
STEPS = NQ * KT
MW = 512
MP = -(-N // MW)
MAXU = KT * MP
NG = 6
KF = S // 2 + 1
NB = 8
BS = C // NB
R3 = S // 3
NV = 9
QR = 3 * HD + 4 * R3
LAM = 0.01
KG = 5
EPS = 1e-5


def rounds(eng, count, body):
    body(0)
    with eng.Fori(1, count) as c:
        body(c)


def wait_used(eng, sem, count):
    if not (isinstance(count, int) and count == 0):
        eng.wait_ge(sem, count)


def norm_chunk(dve, nc, src, stats, mv, rstd, dst, sem, n, dst_free):
    dve.nop(nofuse=True)
    for t in range(CT):
        ins = nc.vector.bn_stats(stats[:, t, :], src[:, t, :])
    ins.then_inc(sem["stats"], 1)
    dve.wait_ge(sem["stats"], n + 1)
    dve.nop(nofuse=True)
    for t in range(CT):
        ins = nc.vector.bn_aggr(mv[:, t, :], stats[:, t, :])
    ins.then_inc(sem["mean"], 1)
    dve.wait_ge(sem["mean"], n + 1)
    nc.vector.tensor_scalar(rstd[:, 0, :], mv[:, :, 1], EPS, None, ALU.add).then_inc(sem["var"], 1)
    dve.wait_ge(sem["rstd"], n + 1)
    dst_free()
    for t in range(CT):
        ins = nc.vector.tensor_scalar(dst[:, t, :], src[:, t, :], mv[:, t, 0:1], rstd[:, 1, t:t + 1],
                                      ALU.subtract, ALU.mult)
    ins.then_inc(sem["out"], 1)


def norm_root(pool, nc, rstd, sem, n):
    pool.wait_ge(sem["var"], n + 1)
    nc.gpsimd.tensor_tensor(rstd[:, 1, :], rstd[:, 0, :], rstd[:, 2, :], ALU.pow).then_inc(sem["rstd"], 1)


def build(nc, d, out):
    ctx = ExitStack()
    with ctx:
        def sb(name, shape, dt=F32, where=ctx):
            return where.enter_context(nc.sbuf_tensor(name, shape, dt))

        def sem(name):
            return ctx.enter_context(nc.semaphore(name))

        def norm_sems(name):
            return {k: sem(f"{name}_{k}") for k in ("stats", "mean", "var", "rstd", "out")}

        kq_d = nc.dram_tensor("kq_d", (2, 2, C, N), F16).ap()
        q_d = nc.dram_tensor("q_d", (2, NH, 128, N), F16).ap()
        m_d = nc.dram_tensor("m_d", (2, N), F16).ap()
        u1_d = nc.dram_tensor("u1_d", (S, 2, KF, C), F32).ap()
        u2_d = nc.dram_tensor("u2_d", (S, 2, KF, C), F32).ap()

        attn = sb("attn", [T, NT, C])
        v_all = sb("v_all", [128, NH, KT, HD])
        w_qkv = sb("w_qkv", [C2 + 1, 2, 3 * C])
        w_proj = sb("w_proj", [C2, 2, C])
        w_up = [sb("w_up0", [C2, 2, HID])]
        w_dn = [sb("w_dn0", [128, HM, C])]
        b_up = [sb(f"b_up{i}", [128, HM]) for i in range(2)]
        gain = [sb(f"gain{i}", [C2, 2]) for i in range(3)]
        shift = [sb(f"shift{i}", [C2, 2]) for i in range(3)]
        rows = sb("rows", [T, 5, C])
        ident = sb("ident", [128, 128])
        mask = sb("mask", [128, 3])
        sel = sb("sel", [128, 2, HD + 1])
        dft_w = sb("dft_w", [T, 4 * KF])
        idft_w = sb("idft_w", [4 * KF, T])
        dft_h = sb("dft_h", [2 * S, 2, 2 * S])
        f_w = sb("f_w", [C2, 2, 2, 2, C2])
        f_wn = sb("f_wn", [C2, 2, C2])
        f_b1 = sb("f_b1", [C2, 2, 2])
        f_b2 = sb("f_b2", [2 * S, C])
        xin = sb("xin", [T, CT, C])
        xh = sb("xh", [T, CT, C])
        xnt = sb("xnt", [C2 + 1, 2, CW])
        xnk = sb("xnk", [C2 + 1, 2, CW])
        stats = sb("stats", [T, CT, 6])
        mv = sb("mv", [T, CT, 2])
        rstd = sb("rstd", [T, 3, CT])

        tmp16 = sb("tmp16", [128, 2, 2 * NG * S], F16)
        mx_p = sb("mx_p", [128, KT, MP])
        mx = sb("mx", [128, KT])
        mneg = sb("mneg", [KT, 128], F16)
        rden = sb("rden", [T, 2 * CT])
        esel = sb("esel", [S, 2 * HD], F16)

        with ExitStack() as r:
            khl = sb("khl", [C2, 2, 4, 2, CW], F16, r)
            rel = [sb(f"rel{i}", [S, S, S], F32, r) for i in range(2)]
            rel_hi = [sb(f"rel_hi{i}", [S, S, S], F16, r) for i in range(2)]
        with ExitStack() as r:
            stage = [sb(f"stage{i}", [128, NG, N], F16, r) for i in range(2)]
        with ExitStack() as r:
            x1 = sb("x1", [T, NT, C], F32, r)
            xnt_all = sb("xnt_all", [C2, 2, N], F32, r)
            r3 = sb("r3", [T, NT, C], F32, r)
        qc, ka, kc = (sb(n, [128, 2, N], F16) for n in ("qc", "ka", "kc"))
        qv = sb("qv", [128, 2, NV, QW], F16)

        with ExitStack() as r:
            q48 = sb("q48", [128, NH, N], F16, r)
            stat = [sb(f"stat{i}", [128, S, 128], F16, r) for i in range(2)]
        with ExitStack() as r:
            v_ext = sb("v_ext", [128, 2, KT, 32], F32, r)
            prob = sb("prob", [128, 4, QW], F32, r)
            o_sb = sb("o_sb", [128, 2, CW], F32, r)
            at_c = sb("at_c", [T, CT, C], F32, r)
            at_t = sb("at_t", [C2, 2, CW], F32, r)
            xb = sb("xb", [T, CT, C], F32, r)
        f_x = sb("f_x", [C2, 2, KG, 2, S])
        f_a = sb("f_a", [C2, 2, KG, 2, S])
        f_r = sb("f_r", [C2, 2, KG, 2, S])
        f_y = sb("f_y", [2 * S, KG, C])
        f_c = sb("f_c", [2 * S, KG, C])
        f_o = sb("f_o", [2 * S, KG, C])
        f_u = sb("f_u", [2 * S, KG, C])
        h1 = sb("h1", [T, CT, C])
        w_up.append(sb("w_up1", [C2, 2, HID]))
        w_dn.append(sb("w_dn1", [128, HM, C]))
        hid = sb("hid", [128, HM, CW])
        u_sb = sb("u_sb", [4 * KF, CT, C])
        y_sb = sb("y_sb", [T, CT, C])
        f_in = sb("f_in", [2 * S, 2, KG, C])

        ps = ctx.enter_context(nc.psum_tensor("ps", [128, 8, 512], F32))

        consts = sem("consts")
        fw_zero = sem("fw_zero")
        fw_neg = sem("fw_neg")
        w1_in = sem("w1_in")
        exponent = sem("exponent")
        ones_row = sem("ones_row")
        rel_in = sem("rel_in")
        zeroed = sem("zeroed")
        stat_sel = sem("stat_sel")
        rel_h16 = sem("rel_h16")
        stat_done = sem("stat_done")
        x_in = sem("x_in")
        ln1 = norm_sems("ln1")
        t1_ps = sem("t1_ps")
        xnt_ok = sem("xnt_ok")
        kq_ps = sem("kq_ps")
        kq_hi = sem("kq_hi")
        kq_lo = sem("kq_lo")
        v_ps = sem("v_ps")
        v_ok = sem("v_ok")
        kq_out = [sem("kq_out0"), sem("kq_out1")]
        q48_in = sem("q48_in")
        op_ps = sem("op_ps")
        op_hi = sem("op_hi")
        op_out = sem("op_out")
        q_out = [sem("q_out0"), sem("q_out1")]
        onehot_in = sem("onehot_in")
        c_in = [sem("c_in0"), sem("c_in1")]
        k_in = [sem("k_in0"), sem("k_in1")]
        qv_in = [sem("qv_in0"), sem("qv_in1")]
        wk_ok = sem("wk_ok")
        rel_pair = sem("rel_pair")
        v_one = sem("v_one")
        v_in = sem("v_in")
        unit_ps = sem("unit_ps")
        unit_ok = sem("unit_ok")
        mx_red = sem("mx_red")
        m_out = sem("m_out")
        s_ps = sem("s_ps")
        p_ok = sem("p_ok")
        pv_ps = sem("pv_ps")
        o_ok = sem("o_ok")
        den_ok = sem("den_ok")
        at_ok = sem("at_ok")
        at_ps = sem("at_ps")
        att_ok = sem("att_ok")
        xr_in = sem("xr_in")
        xb_ok = sem("xb_ok")
        pr_ps = sem("pr_ps")
        x1_ok = sem("x1_ok")
        ln2 = norm_sems("ln2")
        t2_ps = sem("t2_ps")
        xn2_ok = sem("xn2_ok")
        up0 = {k: sem(f"mlp0_{k}") for k in ("up_ps", "act", "dn_ps", "sum", "out")}
        up1 = {k: sem(f"mlp1_{k}") for k in ("up_ps", "act", "dn_ps", "sum", "out")}
        ln3 = norm_sems("ln3")
        h1_mul = sem("h1_mul")
        h1_ok = sem("h1_ok")
        r3_ok = sem("r3_ok")
        fw_ps = sem("fw_ps")
        u_ok = sem("u_ok")
        u_out = sem("u_out")
        f_in_ok = [sem("f_in0"), sem("f_in1")]
        fh_ps = sem("fh_ps")
        fx_ok = sem("fx_ok")
        f1_ps = sem("f1_ps")
        fa_ok = sem("fa_ok")
        fr_ok = sem("fr_ok")
        f2_ps = sem("f2_ps")
        fy_ok = sem("fy_ok")
        fc_ok = sem("fc_ok")
        fo_ok = sem("fo_ok")
        fi_ps = sem("fi_ps")
        fu_ok = sem("fu_ok")
        fu_out = sem("fu_out")
        u2_in = sem("u2_in")
        iw_ps = sem("iw_ps")
        x3_ok = sem("x3_ok")
        ln4 = norm_sems("ln4")
        t4_ps = sem("t4_ps")
        xn4_ok = sem("xn4_ok")
        y_out = sem("y_out")

        block = ctx.enter_context(nc.Block())
        x_t = d["x"].rearrange("(t p) c -> p t c", p=T)
        out_t = out.rearrange("(t p) c -> p t c", p=T)
        NCONST = [0]

        def load(eng, dst, src):
            eng.dma_start(dst, src, allow_slow_non_contiguous=True).then_inc(consts, 16)
            NCONST[0] += 16

        def wait_consts(eng):
            eng.wait_ge(consts, ALL_CONSTS)

        ALL_CONSTS = 16 * (2 + 4 + 2 + 1 + 4 + 2 + 5 + 4 + 1 + 2 + 2 * NB)

        def units(with_max):
            at = {x: [] for x in range(2 * STEPS + 1)}
            if with_max:
                for u in range(MAXU):
                    at[u * MAX_END // MAXU].append(("max", u))
                at[MAX_END + 2].append(("mt", 0))
            at[2 * KT + 8].append(("norm", 0))
            at[4 * KT + 8].append(("norm", 1))
            at[2 * STEPS].append(("norm", 2))
            return at

        def flat(with_max):
            return [u for s, us in sorted(units(with_max).items()) for u in us]

        MAX_END = 2 * STEPS - 14
        U_FIRST = MAXU + 1
        U_HEAD = len(flat(True))
        U_MT = flat(True).index(("mt", 0)) + 1
        PAIRS = STEPS // 2

        def norm_at(q, n):
            last = isinstance(n, int) and n == NH - 1
            return flat(not last).index(("norm", q)) + 1

        def s4(p, s):
            return (p * STEPS + s) % 4

        def piece(u):
            w0 = (u % MP) * MW
            return u // MP, w0, min(MW, N - w0)

        @block.sync
        def _(sp):
            load(sp, w_qkv[0:C2, :, :], d["L0_conv_qkv_w"].rearrange("(k p) n -> p k n", p=C2))
            load(sp, w_qkv[C2:C2 + 1, 1, :], d["L0_conv_qkv_b"])
            for i, nm in enumerate(("L0_conv_ln1", "L0_conv_ln2")):
                load(sp, gain[i][:, :], d[nm + "_g"].rearrange("(k p) -> p k", p=C2))
                load(sp, shift[i][:, :], d[nm + "_b"].rearrange("(k p) -> p k", p=C2))
            load(sp, ident[:, :], d["c_ident"])
            load(sp, mask[:, :], d["c_mask"])

            def chunk(c, par):
                wait_used(sp, ln1["out"], c)
                sp.dma_start(xin[:, :, :], x_t[:, ds(c * CT, CT), :]).then_inc(x_in, 16)
                sp.wait_ge(kq_lo, c * 4 + 4)
                for i in range(4):
                    dst = kq_d[i // 2, :, (i % 2) * C2:(i % 2 + 1) * C2, ds(c * CW, CW)]
                    sp.dma_start(dst.rearrange("l p t -> p l t"), khl[:, par, i, :, :]).then_inc(kq_out[par], 16)

            def round_1(i):
                chunk(2 * i, 0)
                chunk(2 * i + 1, 1)

            rounds(sp, NC // 2, round_1)
            for p in range(2):
                sp.wait_ge(kq_out[p], 64 * NC // 2)
            sp.wait_ge(zeroed, 1 + 2 * NC)
            for r, part in enumerate((0, 1, 0)):
                sp.dma_start(q48[r * HD:(r + 1) * HD, :, :],
                             kq_d[1, part].rearrange("(n c) t -> c n t", c=HD)).then_inc(q48_in, 16)
            for s in range(4):
                g, ab = s // 2, s % 2
                sp.wait_ge(op_out, (s + 1) * S // 2)
                sp.dma_start(q_d[ab, g * NG:(g + 1) * NG].rearrange("n p t -> p n t"),
                             stage[s % 2][:, :, :]).then_inc(q_out[s % 2], 16)
            sp.dma_start(w_up[1][:, :, :], d["L1_conv_fc1_w"].rearrange("(k p) n -> p k n", p=C2)).then_inc(w1_in, 16)
            sp.dma_start(w_dn[1][:, :, :], d["L1_conv_fc2_w"].rearrange("(k p) n -> p k n", p=128)).then_inc(w1_in, 16)
            for p in range(2):
                sp.wait_ge(q_out[p], 32)
            for p in range(2):
                sp.dma_start(ka[3 * HD:QR + 1, p, :], d["c_onehot"]).then_inc(onehot_in, 16)
                sp.dma_start(kc[HD:HD + 2 * S, p, :], d["c_onehot_c"]).then_inc(onehot_in, 16)

            def load_c(n, p):
                parts = [(qc[0:HD, p, :], q_d[0, ds(n, 1), 0:HD, :]),
                         (kc[0:HD, p, :], kq_d[0, 0:1, ds(n * HD, HD), :])]
                for i in range(3):
                    r = HD + i * R3
                    parts.append((qc[r:r + R3, p, :], q_d[0, ds(n, 1), 2 * HD + 2 * i * R3:2 * HD + (2 * i + 1) * R3, :]))
                    r += S
                    parts.append((qc[r:r + R3, p, :], q_d[1, ds(n, 1), HD + 2 * i * R3:HD + (2 * i + 1) * R3, :]))
                for dst, src in parts:
                    sp.dma_start(dst, src.rearrange("o p t -> (o p) t")).then_inc(c_in[p], 16)

            def load_k(n, p):
                for r, part in enumerate((0, 0, 1)):
                    sp.dma_start(ka[r * HD:(r + 1) * HD, p, :],
                                 kq_d[0, part:part + 1, ds(n * HD, HD), :].rearrange("o p t -> (o p) t"))\
                      .then_inc(k_in[p], 16)

            def load_qv(n, q, b):
                def rows(ab, r0, r1):
                    return q_d[ab, ds(n, 1), r0:r1, q * QW:(q + 1) * QW].rearrange("o p t -> p o t")

                v3 = qv[:, b, :, :].rearrange("p (i j) t -> p i j t", j=3)
                parts = [(qv[0:2 * HD, b, :, :], rows(0, 0, 2 * HD).to_broadcast([2 * HD, NV, QW])),
                         (qv[2 * HD:3 * HD, b, :, :], rows(1, 0, HD).to_broadcast([HD, NV, QW]))]
                for i in range(3):
                    r = 3 * HD
                    parts.append((v3[r:r + 2 * R3, i, :, :],
                                  rows(0, 2 * HD + 2 * i * R3, 2 * HD + 2 * (i + 1) * R3).to_broadcast([2 * R3, 3, QW])))
                    r += 2 * R3
                    parts.append((v3[r:r + 2 * R3, :, i, :],
                                  rows(1, HD + 2 * i * R3, HD + 2 * (i + 1) * R3).to_broadcast([2 * R3, 3, QW])))
                for dst, src in parts:
                    sp.dma_start(dst, src).then_inc(qv_in[b], 16)

            def load_m(p, q, b):
                sp.dma_start(qv[QR:QR + 1, b, :, :],
                             m_d[p:p + 1, q * QW:(q + 1) * QW].unsqueeze(1).to_broadcast([1, NV, QW])).then_inc(qv_in[b], 16)

            def store_m(n, p, unit):
                sp.wait_ge(unit_ok, unit)
                sp.dma_start(m_d[p].rearrange("(k t) -> k t", t=128), mneg[:, :]).then_inc(m_out, 16)
                sp.wait_ge(m_out, 16 * (n + 1))

            def period(n, p, more_c):
                for q in range(1, NQ):
                    wait_used(sp, s_ps, n * STEPS + (q - 1) * KT)
                    load_qv(n, q, (p + q) % 2)
                    load_m(p, q, (p + q) % 2)
                load_k(n + 1, 1 - p)
                sp.wait_ge(s_ps, n * STEPS + (NQ - 1) * KT)
                load_qv(n + 1, 0, 1 - p)
                store_m(n + 1, 1 - p, n * U_HEAD + U_FIRST + U_MT)
                load_m(1 - p, 0, 1 - p)
                if more_c:
                    load_c(n + 2, p)

            load_c(0, 0)
            load_k(0, 0)
            load_qv(0, 0, 0)
            load_c(1, 1)
            store_m(0, 0, U_FIRST)
            load_m(0, 0, 0)

            def two_periods(i):
                period(2 * i, 0, True)
                period(2 * i + 1, 1, True)

            rounds(sp, NH // 2 - 1, two_periods)
            period(NH - 2, 0, False)
            for q in range(1, NQ):
                sp.wait_ge(s_ps, (NH - 1) * STEPS + (q - 1) * KT)
                load_qv(NH - 1, q, (1 + q) % 2)
                load_m(1, q, (1 + q) % 2)

            def round_3(c):
                wait_used(sp, xb_ok, c)
                sp.dma_start(xin[:, :, :], x_t[:, ds(c * CT, CT), :]).then_inc(xr_in, 16)

            rounds(sp, NC, round_3)
            u1_t = u1_d.rearrange("(t a) r k c -> (a r k) t c", a=2)
            u2_t = u2_d.rearrange("(t a) r k c -> (a r k) t c", a=2)
            def round_4(c):
                sp.wait_ge(u_ok, c + 1)
                sp.dma_start(u1_t[:, ds(c * CT, CT), :], u_sb[:, :, :]).then_inc(u_out, 16)

            rounds(sp, NC, round_4)
            sp.wait_ge(u_out, 16 * NC)

            def f_load(g, p):
                for r in range(2):
                    sp.dma_start(f_in[r * S:(r + 1) * S, p, :, :],
                                 u1_d[:, r, ds(g * KG, KG), :]).then_inc(f_in_ok[p], 16)

            def f_store(g):
                sp.wait_ge(fu_ok, g + 1)
                for r in range(2):
                    sp.dma_start(u2_d[:, r, ds(g * KG, KG), :],
                                 f_u[r * S:(r + 1) * S, :, :]).then_inc(fu_out, 16)

            G = KF // KG
            f_load(0, 0)
            f_load(1, 1)
            for g in range(G):
                f_store(g)
                if g + 2 < G:
                    sp.wait_ge(fh_ps, g + 1)
                    f_load(g + 2, g % 2)
            sp.wait_ge(fu_out, 32 * G)
            def round_5(c):
                wait_used(sp, iw_ps, c)
                sp.dma_start(u_sb[:, :, :], u2_t[:, ds(c * CT, CT), :]).then_inc(u2_in, 16)

            rounds(sp, NC, round_5)
            def round_6(c):
                sp.wait_ge(up1["out"], c + 1)
                sp.dma_start(out_t[:, ds(c * CT, CT), :], y_sb[:, :, :]).then_inc(y_out, 16)

            rounds(sp, NC, round_6)
            sp.wait_ge(y_out, 16 * NC)

        @block.gpsimd
        def _(pool):
            nc.gpsimd.memset(rstd[:, 2, :], -0.5).then_inc(exponent, 1)
            pool.wait_ge(exponent, 1)
            nc.gpsimd.memset(xnk[C2:C2 + 1, :, :], 1.0)
            nc.gpsimd.memset(xnt[C2:C2 + 1, :, :], 1.0).then_inc(ones_row, 1)
            pool.wait_ge(ones_row, 1)
            nc.gpsimd.memset(stat[0][:, :, :].bitcast(F32), 0.0)
            nc.gpsimd.memset(stat[1][:, :, :].bitcast(F32), 0.0).then_inc(zeroed, 1)
            nc.gpsimd.memset(f_w[:, :, :, :, :], 0.0).then_inc(fw_zero, 1)
            pool.wait_ge(zeroed, 1)
            pool.wait_ge(rel_in, 48)
            nc.gpsimd.tensor_copy(stat[0][0:S, :, 0:2 * HD],
                                  esel[:, :].unsqueeze(1).to_broadcast([S, S, 2 * HD]))
            nc.gpsimd.tensor_copy(stat[1][0:S, :, 0:HD],
                                  esel[:, 0:HD].unsqueeze(1).to_broadcast([S, S, HD])).then_inc(stat_sel, 1)
            for c in range(NC):
                norm_root(pool, nc, rstd, ln1, c)
                hs = slice(c * (NH // NC), (c + 1) * (NH // NC))
                pool.wait_ge(ln1["rstd"], c + 1)
                nc.gpsimd.memset(q48[32:64, hs, :].bitcast(F32), 0.0).then_inc(zeroed, 1)
                pool.wait_ge(zeroed, 2 * c + 2)
                nc.gpsimd.memset(q48[64:128, hs, :].bitcast(F32), 0.0).then_inc(zeroed, 1)
                pool.wait_ge(zeroed, 2 * c + 3)
            pool.wait_ge(op_ps, 2 * S)
            nc.gpsimd.memset(v_ext[:, :, :, HD:HD + 1], 1.0)
            nc.gpsimd.memset(v_ext[:, :, :, HD + 1:32], 0.0).then_inc(v_one, 1)
            pool.wait_ge(v_ok, 3 * NC)

            def copy_v(n, p):
                nc.gpsimd.tensor_copy(v_ext[:, p, :, 0:HD],
                                      v_all[:, ds(n, 1), :, :].rearrange("p o j c -> p (o j) c")).then_inc(v_in, 1)

            copy_v(0, 0)
            copy_v(1, 1)
            with pool.Fori(1, NH // 2) as i:
                for p in range(2):
                    pool.wait_ge(pv_ps, (2 * i + p - 1) * PAIRS)
                    copy_v(2 * i + p, p)

            wait_consts(pool)
            def round_7(c):
                pool.wait_ge(xr_in, 16 * (c + 1))
                wait_used(pool, x1_ok, c)
                nc.gpsimd.tensor_tensor(xb[:, :, :], xin[:, :, :],
                                        rows[:, 0:1, :].to_broadcast([T, CT, C]), ALU.add).then_inc(xb_ok, 1)
                norm_root(pool, nc, rstd, ln2, c)

            rounds(pool, NC, round_7)
            def round_8(c):
                norm_root(pool, nc, rstd, ln3, c)
                pool.wait_ge(ln3["out"], c + 1)
                wait_used(pool, fw_ps, c)
                nc.gpsimd.tensor_tensor(h1[:, :, :], xh[:, :, :],
                                        rows[:, 2:3, :].to_broadcast([T, CT, C]), ALU.mult).then_inc(h1_mul, 1)
                pool.wait_ge(h1_mul, c + 1)
                nc.gpsimd.tensor_tensor(h1[:, :, :], h1[:, :, :],
                                        rows[:, 3:4, :].to_broadcast([T, CT, C]), ALU.add).then_inc(h1_ok, 1)
                pool.wait_ge(h1_ok, c + 1)
                nc.gpsimd.tensor_tensor(r3[:, ds(c * CT, CT), :], h1[:, :, :], y_sb[:, :, :],
                                        ALU.add).then_inc(r3_ok, 1)

            rounds(pool, NC, round_8)

            def round_9(c):
                norm_root(pool, nc, rstd, ln4, c)

            rounds(pool, NC, round_9)

        @block.scalar
        def _(act):
            act.dma_start(rel[0][:, :, :], d["c_rel_h"]).then_inc(rel_in, 16)
            act.dma_start(rel[1][:, :, :], d["c_rel_w"]).then_inc(rel_in, 16)
            act.dma_start(esel[:, :], d["c_esel"]).then_inc(rel_in, 16)
            load(act, w_proj[:, :, :], d["L0_conv_proj_w"].rearrange("(k p) n -> p k n", p=C2))
            for i, (up, dn, bu) in enumerate((("L0_conv_mlp_w1", "L0_conv_mlp_w2", "L0_conv_mlp_b1"),
                                              ("L1_conv_fc1_w", "L1_conv_fc2_w", "L1_conv_fc1_b"))):
                if i == 0:
                    load(act, w_up[i][:, :, :], d[up].rearrange("(k p) n -> p k n", p=C2))
                    load(act, w_dn[i][:, :, :], d[dn].rearrange("(k p) n -> p k n", p=128))
                load(act, b_up[i][:, :], d[bu].rearrange("(m p) -> p m", p=128))
            load(act, gain[2][:, :], d["L1_conv_g2"].rearrange("(k p) -> p k", p=C2))
            load(act, shift[2][:, :], d["L1_conv_be2"].rearrange("(k p) -> p k", p=C2))
            for i, nm in enumerate(("L0_conv_proj_b", "L0_conv_mlp_b2", "L1_conv_g1", "L1_conv_be1", "L1_conv_fc2_b")):
                load(act, rows[:, i, :], d[nm].rearrange("(o c) -> o c", o=1).to_broadcast([T, C]))
            load(act, sel[:, :, :], d["c_sel"])
            load(act, dft_w[:, :], d["c_dft_w"])
            load(act, idft_w[:, :], d["c_idft_w"])
            load(act, dft_h[:, :, :], d["c_dft_h"])
            load(act, f_b1[:, :, :].rearrange("p r k -> p (r k)"), d["f_b1"].rearrange("r (k p) -> p (r k)", p=C2))
            for r in range(2):
                load(act, f_b2[r * S:(r + 1) * S, :], d["f_b2"][r:r + 1, :].to_broadcast([S, C]))
            act.wait_ge(fw_zero, 1)
            for layer in range(2):
                for b in range(NB):
                    p0 = (b % 4) * BS
                    load(act, f_w[p0:p0 + BS, layer, b // 4, :, p0:p0 + BS],
                         d["f_w"][layer, :, b].rearrange("r k o -> k r o"))
            act.wait_ge(rel_in, 48)
            for i in range(2):
                nc.scalar.activation(rel_hi[i][:, :, :], rel[i][:, :, :], ACT.Copy).then_inc(rel_h16, 1)
            wait_consts(act)
            nc.scalar.activation(w_qkv[0:C2, :, C:2 * C], w_qkv[0:C2, :, C:2 * C], ACT.Copy, scale=SCALE)
            nc.scalar.activation(w_qkv[C2:C2 + 1, 1, C:2 * C], w_qkv[C2:C2 + 1, 1, C:2 * C], ACT.Copy,
                                 scale=SCALE).then_inc(wk_ok, 1)
            nc.scalar.activation(f_wn[:, :, :], f_w[:, 0, :, 1, :], ACT.Copy, scale=-1.0).then_inc(fw_neg, 1)

            def in_key_order(x):
                return x.rearrange("p (j a b) -> p a j b", j=3, b=R3)

            def chunk(c, par, before):
                act.wait_ge(t1_ps, c + 1)
                wait_used(act, v_ps, c)
                for k in range(2):
                    nc.scalar.activation(xnt[0:C2, k, :], ps[0:C2, k, 0:CW], ACT.Identity,
                                         bias=shift[0][:, k:k + 1], scale=gain[0][:, k:k + 1])
                    nc.scalar.activation(in_key_order(xnk[0:C2, k, :]),
                                         ps[0:C2, k, 0:CW].rearrange("p (a j b) -> p a j b", j=3, b=R3),
                                         ACT.Identity, bias=shift[0][:, k:k + 1],
                                         scale=gain[0][:, k:k + 1]).then_inc(xnt_ok, 1)
                wait_used(act, kq_out[par], 64 * before)
                for i in range(4):
                    act.wait_ge(kq_ps, 4 * c + i + 1)
                    hi, x = khl[:, par, i, 0, :], ps[0:C2, 2 + i, 0:CW]
                    nc.scalar.activation(hi, x, ACT.Copy).then_inc(kq_hi, 1)

            def round_10(i):
                chunk(2 * i, 0, i)
                chunk(2 * i + 1, 1, i)

            rounds(act, NC // 2, round_10)

            def op_hi_of(i, ab, par, first):
                act.wait_ge(op_ps, i + 1)
                if not first:
                    act.wait_ge(op_out, i - 1)
                nc.scalar.activation(tmp16[:, par, :].rearrange("p (a b) -> p a b", a=2),
                                     ps[:, 2 * par:2 * par + 2, 0:NG * S], ACT.Copy,
                                     scale=mask[:, ab:ab + 1]).then_inc(op_hi, 1)

            op_hi_of(0, 0, 0, True)
            op_hi_of(1, 0, 1, True)
            for s in range(4):
                with act.Fori(s * S // 4 + (s == 0), (s + 1) * S // 4) as i:
                    op_hi_of(2 * i, s % 2, 0, False)
                    op_hi_of(2 * i + 1, s % 2, 1, False)

            def period(n, p, first):
                for s in range(STEPS):
                    act.wait_ge(s_ps, n * STEPS + s + 1)
                    if not (first and s < 4):
                        act.wait_ge(pv_ps, n * PAIRS + (s - 4) // 2 + 1)
                    nc.scalar.activation(prob[:, s4(p, s), :].rearrange("p (a b) -> p a b", a=2),
                                         ps[:, 2 + 2 * (s % 2):4 + 2 * (s % 2), 0:CW],
                                         ACT.Exp).then_inc(p_ok, 1)
                    for q in range(NQ):
                        if s == (q + 1) * KT + 1:
                            out_group(n, q, p, first)
                out_group(n, NQ - 1, p, first)

            def out_group(n, q, p, first):
                par = (NQ * p + q) % 2
                act.wait_ge(pv_ps, n * PAIRS + (q + 1) * (KT // 2))
                if q == 2:
                    act.wait_ge(unit_ps, n * U_HEAD + U_FIRST + norm_at(0, n))
                elif not first:
                    act.wait_ge(unit_ps, (n - 1) * U_HEAD + U_FIRST + norm_at(q + 1, None))
                nc.scalar.activation(o_sb[:, par, :], ps[:, 6 + par, 0:CW], ACT.Copy).then_inc(o_ok, 1)

            period(0, 0, True)
            period(1, 1, False)
            with act.Fori(1, NH // 2 - 1) as i:
                period(2 * i, 0, False)
                period(2 * i + 1, 1, False)
            period(NH - 2, 0, False)
            period(NH - 1, 1, False)

            act.wait_ge(unit_ok, U_FIRST + (NH - 1) * U_HEAD + NQ)
            def round_11(c):
                wait_used(act, at_ps, c)
                nc.scalar.activation(at_c[:, :, :], attn[:, ds(c * CT, CT), :], ACT.Copy).then_inc(at_ok, 1)
                act.wait_ge(at_ps, c + 1)
                wait_used(act, pr_ps, c)
                nc.scalar.activation(at_t[:, :, :], ps[0:C2, 0:2, 0:CW], ACT.Copy).then_inc(att_ok, 1)
                act.wait_ge(t2_ps, c + 1)
                for k in range(2):
                    nc.scalar.activation(xnt_all[:, k, ds(c * CW, CW)], ps[0:C2, 4 + k, 0:CW], ACT.Identity,
                                         bias=shift[1][:, k:k + 1], scale=gain[1][:, k:k + 1]).then_inc(xn2_ok, 1)

            rounds(act, NC, round_11)

            def gelus(c, i, sems):
                wait_used(act, sems["dn_ps"], c)
                for m in range(HM):
                    act.wait_ge(sems["up_ps"], c * HM + m + 1)
                    nc.scalar.activation(hid[:, m, :], ps[:, m % 4, 0:CW], ACT.Gelu,
                                         bias=b_up[i][:, m:m + 1]).then_inc(sems["act"], 1)

            def spectrum(c):
                act.wait_ge(fw_ps, c + 1)
                wait_used(act, u_out, 16 * c)
                nc.scalar.activation(u_sb[:, :, :].rearrange("p (a b) c -> p a (b c)", a=2),
                                     ps[0:4 * KF, 6:8, 0:2 * C], ACT.Copy).then_inc(u_ok, 1)

            gelus(0, 0, up0)
            with act.Fori(1, NC) as c:
                gelus(c, 0, up0)
                spectrum(c - 1)
            spectrum(NC - 1)

            for g in range(KF // KG):
                act.wait_ge(fh_ps, g + 1)
                act.wait_ge(f1_ps, g)
                nc.scalar.activation(f_x[:, :, :, :, :].rearrange("p a k r h -> p a (k r h)"),
                                     ps[0:C2, 0:2, 0:KG * 2 * S], ACT.Copy).then_inc(fx_ok, 1)
                act.wait_ge(f1_ps, g + 1)
                act.wait_ge(f2_ps, g)
                for k in range(2):
                    for r in range(2):
                        ins = nc.scalar.activation(
                            f_a[:, k, :, r, :],
                            ps[0:C2, 2 + k, r * KG * S:(r + 1) * KG * S].rearrange("p (k h) -> p k h", h=S),
                            ACT.Relu, bias=f_b1[:, r, k:k + 1])
                ins.then_inc(fa_ok, 1)
                act.wait_ge(fi_ps, g + 1)
                act.wait_ge(fu_out, 32 * g)
                nc.scalar.activation(f_u[:, 0:4, :].rearrange("p (a b) c -> p a (b c)", a=2),
                                     ps[0:2 * S, 0:2, 0:2 * C], ACT.Copy)
                nc.scalar.activation(f_u[:, 4, :], ps[0:2 * S, 7, 0:C], ACT.Copy).then_inc(fu_ok, 1)

            def round_12(c):
                act.wait_ge(t4_ps, c + 1)
                for k in range(2):
                    nc.scalar.activation(xnt_all[:, k, ds(c * CW, CW)], ps[0:C2, 4 + k, 0:CW], ACT.Identity,
                                         bias=shift[2][:, k:k + 1], scale=gain[2][:, k:k + 1]).then_inc(xn4_ok, 1)

            rounds(act, NC, round_12)
            def round_13(c):
                gelus(c, 1, up1)

            rounds(act, NC, round_13)

        @block.tensor
        def _(pe):
            def mm(o, l, r, start=True, stop=True):
                return nc.tensor.matmul(o, l, r, start=start, stop=stop)

            def transposes(src, bank):
                for k in range(2):
                    for t in range(CT):
                        ins = nc.tensor.transpose(ps[0:C2, bank + k, t * T:(t + 1) * T],
                                                  src[:, t, k * C2:(k + 1) * C2], ident[0:T, 0:T])
                return ins

            wait_consts(pe)
            pe.wait_ge(ones_row, 1)
            pe.wait_ge(wk_ok, 1)
            def round_14(c):
                pe.wait_ge(ln1["out"], c + 1)
                wait_used(pe, xnt_ok, 2 * c)
                transposes(xh, 0).then_inc(t1_ps, 1)
                pe.wait_ge(xnt_ok, 2 * c + 2)
                for i in range(4):
                    wait_used(pe, kq_lo, 4 * c)
                    col = (C if i < 2 else 0) + (i % 2) * C2
                    xn = xnk if i < 2 else xnt
                    mm(ps[0:C2, 2 + i, 0:CW], w_qkv[0:C2, 0, col:col + C2], xn[0:C2, 0, :], stop=False)
                    mm(ps[0:C2, 2 + i, 0:CW], w_qkv[:, 1, col:col + C2], xn[:, 1, :],
                       start=False).then_inc(kq_ps, 1)
                wait_used(pe, v_ok, 3 * c)
                for j in range(3):
                    o = ps[:, 6 + j // 2, (j % 2) * C:(j % 2 + 1) * C]
                    mm(o, xnk[0:C2, 0, j * 128:(j + 1) * 128], w_qkv[0:C2, 0, 2 * C:3 * C], stop=False)
                    ins = mm(o, xnk[:, 1, j * 128:(j + 1) * 128], w_qkv[:, 1, 2 * C:3 * C], start=False)
                ins.then_inc(v_ps, 1)

            rounds(pe, NC, round_14)

            pe.wait_ge(q48_in, 48)
            pe.wait_ge(stat_done, 4)
            pe.wait_ge(stat_sel, 1)
            pe.wait_ge(v_ok, 3 * NC)
            pe.wait_ge(kq_lo, 4 * NC)

            def op_tile(s, i, tile, par, first):
                g, ab = s // 2, s % 2
                if not first:
                    pe.wait_ge(op_out, tile - 1)
                for j in range(2):
                    r = 2 * i + j
                    if ab == 0:
                        q = q48[:, g * NG:(g + 1) * NG, ds(r * S, S)]
                    else:
                        q = q48[:, g * NG:(g + 1) * NG, :].rearrange("p n (h w) -> p n w h", w=S)[:, :, ds(r, 1), :]
                        q = q.rearrange("p n o h -> p n (o h)")
                    ins = mm(ps[:, 2 * par + j, 0:NG * S].rearrange("p (n w) -> p n w", n=NG),
                             stat[ab][:, ds(r, 1), :].rearrange("p o m -> p (o m)"), q)
                ins.then_inc(op_ps, 1)

            for s in range(4):
                base = s * S // 2
                if s == 0:
                    op_tile(0, 0, 0, 0, True)
                    op_tile(0, 1, 1, 1, True)
                with pe.Fori(1 if s == 0 else 0, S // 4) as i:
                    op_tile(s, 2 * i, 2 * i + base, 0, False)
                    op_tile(s, 2 * i + 1, 2 * i + 1 + base, 1, False)

            pe.wait_ge(op_out, 2 * S)
            pe.wait_ge(onehot_in, 64)

            def ring_wait(count):
                pe.wait_ge(unit_ok, count)

            def max_unit(k, slot, p):
                qt, w0, w = piece(k)
                mm(ps[:, slot, 0:w], qc[0:HD + 2 * S, p, qt * 128:(qt + 1) * 128],
                   kc[0:HD + 2 * S, p, w0:w0 + w]).then_inc(unit_ps, 1)

            def mt_unit(slot, reduced):
                pe.wait_ge(mx_red, reduced)
                nc.tensor.transpose(ps[0:KT, slot, 0:128], mx[:, :], ident[:, :]).then_inc(unit_ps, 1)

            pe.wait_ge(c_in[0], 128)
            for k in range(MAXU):
                if k >= 2:
                    ring_wait(k - 1)
                max_unit(k, k % 2, 0)
            ring_wait(MAXU - 1)
            mt_unit(MAXU % 2, 1)

            pe.wait_ge(v_one, 1)

            def scores(n, p, s, j):
                k0 = (s % KT) * 128
                if j == 0 and (s >= 2 or not (isinstance(n, int) and n == 0)):
                    pe.wait_ge(p_ok, n * STEPS + s - 1)
                o = ps[:, 2 + 2 * (s % 2) + j, 0:CW]
                v = (2 - s % KT // 6) * 3 + 2 - s % 3
                q = s // KT
                if s % KT == 0 and j == 0:
                    pe.wait_ge(qv_in[(p + q) % 2], 144 * (3 * n_half(n, p) + (3 * p + q) // 2 + 1))
                ins = mm(o, ka[0:QR + 1, p, k0:k0 + 128], qv[0:QR + 1, (p + q) % 2, v, j * CW:(j + 1) * CW])
                if j == 1:
                    ins.then_inc(s_ps, 1)

            def values(n, p, s):
                q, acc = s // KT, 6 + (NQ * p + s // KT) % 2
                pe.wait_ge(p_ok, n * STEPS + s + 2)
                if s % KT == 0 and not (isinstance(n, int) and n == 0 and q < 2):
                    pe.wait_ge(o_ok, n * NQ + q - 1)
                for e in range(2):
                    for j in range(2):
                        r = 32 * (2 * e + j)
                        ins = nc.tensor.matmul(ps[r:r + 32, acc, 0:CW], v_ext[:, p, (s + e) % KT, :],
                                               prob[:, s4(p, s + e), j * CW:(j + 1) * CW],
                                               start=(s % KT == 0), stop=(s % KT == KT - 2),
                                               tile_position=(0, r))
                ins.then_inc(pv_ps, 1)

            def norm_unit(n, p, q, slot):
                par = (NQ * p + q) % 2
                pe.wait_ge(o_ok, n * NQ + q + 1)
                for t in range(2 * CT):
                    ins = mm(ps[0:T, slot, t * (HD + 1):(t + 1) * (HD + 1)],
                             o_sb[:, par, (t % CT) * T:(t % CT + 1) * T], sel[:, t // CT, :])
                ins.then_inc(unit_ps, 1)

            def period(n, p, with_max):
                at, u = units(with_max), 0
                pe.wait_ge(k_in[p], 48 * (n_half(n, p) + 1))
                pe.wait_ge(v_in, n + 1)

                def slot_units(x):
                    nonlocal u
                    for kind, k in at[x]:
                        if kind == "max" and k == 0:
                            pe.wait_ge(c_in[1 - p], 128 * c_count(n, p))
                        ring_wait(n * U_HEAD + U_FIRST + u - 1)
                        slot = (U_FIRST + p * U_HEAD + u) % 2
                        if kind == "max":
                            max_unit(k, slot, 1 - p)
                        elif kind == "mt":
                            mt_unit(slot, n + 2)
                        else:
                            norm_unit(n, p, k, slot)
                        u += 1

                for s in range(0, STEPS, 2):
                    scores(n, p, s, 0)
                    scores(n, p, s, 1)
                    slot_units(2 * s)
                    scores(n, p, s + 1, 0)
                    slot_units(2 * s + 1)
                    scores(n, p, s + 1, 1)
                    slot_units(2 * s + 2)
                    if s >= 2:
                        values(n, p, s - 2)
                    slot_units(2 * s + 3)
                values(n, p, STEPS - 2)
                slot_units(2 * STEPS)

            def n_half(n, p):
                return halves[0] if halves[0] is not None else n // 2

            def c_count(n, p):
                return n_half(n, p) + (1 if p == 0 else 2)

            halves = [None]
            period(0, 0, True)
            period(1, 1, True)
            with pe.Fori(1, NH // 2 - 1) as i:
                halves[0] = i
                period(2 * i, 0, True)
                period(2 * i + 1, 1, True)
            halves[0] = None
            period(NH - 2, 0, True)
            period(NH - 1, 1, False)

            pe.wait_ge(unit_ok, U_FIRST + (NH - 1) * U_HEAD + NQ)
            pe.wait_ge(o_ok, NH * NQ)
            def round_15(c):
                pe.wait_ge(at_ok, c + 1)
                wait_used(pe, att_ok, c)
                transposes(at_c, 0).then_inc(at_ps, 1)
                pe.wait_ge(att_ok, c + 1)
                wait_used(pe, x1_ok, c)
                for t in range(CT):
                    for k in range(2):
                        ins = mm(ps[0:T, 2 + t // 2, (t % 2) * C:(t % 2 + 1) * C],
                                 at_t[:, k, t * T:(t + 1) * T], w_proj[:, k, :], start=(k == 0), stop=(k == 1))
                ins.then_inc(pr_ps, 1)
                pe.wait_ge(ln2["out"], c + 1)
                wait_used(pe, xn2_ok, 2 * c)
                transposes(xh, 4).then_inc(t2_ps, 1)

            rounds(pe, NC, round_15)

            def up(c, i, sems):
                for m in range(HM):
                    if m >= 4:
                        pe.wait_ge(sems["act"], c * HM + m - 3)
                    else:
                        wait_used(pe, sems["act"], c * HM)
                    for k in range(2):
                        ins = mm(ps[:, m % 4, 0:CW], w_up[i][:, k, m * 128:(m + 1) * 128],
                                 xnt_all[:, k, ds(c * CW, CW)], start=(k == 0), stop=(k == 1))
                    ins.then_inc(sems["up_ps"], 1)

            def down(c, i, sems):
                pe.wait_ge(sems["act"], (c + 1) * HM)
                wait_used(pe, sems["sum"], c)
                for t in range(CT):
                    for m in range(HM):
                        ins = mm(ps[0:T, 4 + t // 2, (t % 2) * C:(t % 2 + 1) * C],
                                 hid[:, m, t * T:(t + 1) * T], w_dn[i][:, m, :],
                                 start=(m == 0), stop=(m == HM - 1))
                ins.then_inc(sems["dn_ps"], 1)

            def dft(c):
                pe.wait_ge(h1_ok, c + 1)
                wait_used(pe, u_ok, c)
                for j in range(2):
                    ins = mm(ps[0:4 * KF, 6 + j, 0:2 * C], dft_w[:, :],
                             h1[:, 2 * j:2 * j + 2, :].rearrange("p t c -> p (t c)"))
                ins.then_inc(fw_ps, 1)

            pe.wait_ge(x1_ok, NC)
            pe.wait_ge(xn2_ok, 2 * NC)
            up(0, 0, up0)
            down(0, 0, up0)
            with pe.Fori(1, NC) as c:
                up(c, 0, up0)
                dft(c - 1)
                down(c, 0, up0)
            dft(NC - 1)

            pe.wait_ge(fw_neg, 1)
            for g in range(KF // KG):
                p = g % 2
                pe.wait_ge(f_in_ok[p], 32 * (g // 2 + 1))
                pe.wait_ge(fu_ok, g)
                pe.wait_ge(u_ok, NC)
                for k in range(2):
                    for f in range(KG):
                        ins = mm(ps[0:C2, k, f * 2 * S:(f + 1) * 2 * S], f_in[:, p, f, k * C2:(k + 1) * C2],
                                 dft_h[:, 0, :])
                ins.then_inc(fh_ps, 1)
                pe.wait_ge(fx_ok, g + 1)
                pe.wait_ge(fa_ok, g)
                for k in range(2):
                    for r in range(2):
                        o = ps[0:C2, 2 + k, r * KG * S:(r + 1) * KG * S].rearrange("p (k h) -> p k h", h=S)
                        w_r, w_i = f_w[:, 0, k, 0, :], f_w[:, 0, k, 1, :]
                        mm(o, w_r, f_x[:, k, :, r, :], stop=False)
                        ins = mm(o, f_wn[:, k, :] if r == 0 else w_i, f_x[:, k, :, 1 - r, :], start=False)
                ins.then_inc(f1_ps, 1)
                pe.wait_ge(fr_ok, g + 1)
                pe.wait_ge(fy_ok, g)
                for f in range(KG):
                    for k in range(2):
                        o = ps[0:2 * S, 4 + f // 2, (f % 2) * C + k * C2:(f % 2) * C + (k + 1) * C2]
                        mm(o, f_a[:, k, f, :, :].rearrange("p r h -> p (r h)"), f_w[:, 1, k, 0, :], stop=False)
                        ins = mm(o, f_r[:, k, f, :, :].rearrange("p r h -> p (r h)"), f_w[:, 1, k, 1, :],
                                 start=False)
                ins.then_inc(f2_ps, 1)
                pe.wait_ge(fo_ok, g + 1)
                for j, bank in enumerate((0, 1, 7)):
                    w = min(2, KG - 2 * j)
                    ins = mm(ps[0:2 * S, bank, 0:w * C], dft_h[:, 1, :],
                             f_o[:, 2 * j:2 * j + w, :].rearrange("p f c -> p (f c)"))
                ins.then_inc(fi_ps, 1)

            pe.wait_ge(fu_ok, KF // KG)
            pe.wait_ge(fy_ok, KF // KG)
            def round_16(c):
                pe.wait_ge(u2_in, 16 * (c + 1))
                wait_used(pe, x3_ok, c)
                for j in range(2):
                    ins = mm(ps[0:T, 2 + j, 0:2 * C], idft_w[:, :],
                             u_sb[:, 2 * j:2 * j + 2, :].rearrange("p t c -> p (t c)"))
                ins.then_inc(iw_ps, 1)
                pe.wait_ge(ln4["out"], c + 1)
                wait_used(pe, xn4_ok, 2 * c)
                transposes(xh, 4).then_inc(t4_ps, 1)

            rounds(pe, NC, round_16)
            pe.wait_ge(x3_ok, NC)
            pe.wait_ge(xn4_ok, 2 * NC)
            pe.wait_ge(w1_in, 32)
            def round_17(c):
                up(c, 1, up1)
                down(c, 1, up1)

            rounds(pe, NC, round_17)

        @block.vector
        def _(dve):
            dve.wait_ge(rel_h16, 2)
            dve.wait_ge(zeroed, 1)
            wait_consts(dve)
            for i in range(2):
                nc.vector.scalar_tensor_tensor(out=rel_hi[i][:, :, :], in0=rel_hi[i][:, :, :],
                                               scalar=mask[0:S, 2:3], in1=rel[i][:, :, :],
                                               op0=ALU.mult, op1=ALU.add).then_inc(rel_pair, 1)
            dve.wait_ge(rel_pair, 2)
            for i, c0 in ((0, 2 * HD), (1, HD)):
                o = stat[i][0:S, :, c0:c0 + 2 * S].rearrange("p x (i l r) -> p x i l r", l=2, r=R3)
                for l in range(2):
                    nc.vector.tensor_copy(o[:, :, :, l, :], rel_hi[i][:, :, :].rearrange("p x (i r) -> p x i r", r=R3))\
                      .then_inc(stat_done, 1)

            def chunk(c, par):
                dve.wait_ge(x_in, 16 * (c + 1))
                norm_chunk(dve, nc, xin, stats, mv, rstd, xh, ln1, c,
                           lambda: wait_used(dve, t1_ps, c))
                for i in range(4):
                    dve.wait_ge(kq_hi, 4 * c + i + 1)
                    lo, hi, x = khl[:, par, i, 1, :], khl[:, par, i, 0, :], ps[0:C2, 2 + i, 0:CW]
                    nc.vector.tensor_tensor(lo, x, hi, ALU.subtract).then_inc(kq_lo, 1)
                dve.wait_ge(v_ps, c + 1)
                for j in range(3):
                    nc.vector.tensor_copy(v_all[:, :, ds(c * 3 + j, 1), :].rearrange("p n o c -> p n (o c)"),
                                          ps[:, 6 + j // 2, (j % 2) * C:(j % 2 + 1) * C]
                                          .rearrange("p (n c) -> p n c", c=HD)).then_inc(v_ok, 1)

            def round_18(i):
                chunk(2 * i, 0)
                chunk(2 * i + 1, 1)

            rounds(dve, NC // 2, round_18)

            def operand(s, i, tile, par):
                g, ab = s // 2, s % 2
                dve.wait_ge(op_hi, tile + 1)
                st = stage[s % 2]
                if ab == 0:
                    o = st[:, :, ds(i * 2 * S, 2 * S)].rearrange("p n (r w) -> p r n w", r=2)
                else:
                    o = st[:, :, :].rearrange("p n (h w) -> p w n h", w=S)[:, ds(i * 2, 2), :, :]
                nc.vector.tensor_tensor(o, ps[:, 2 * par:2 * par + 2, 0:NG * S].rearrange("p r (n w) -> p r n w", n=NG),
                                        tmp16[:, par, :].rearrange("p (r n w) -> p r n w", r=2, n=NG),
                                        ALU.subtract).then_inc(op_out, 1)

            for p in range(2):
                dve.wait_ge(kq_out[p], 64 * NC // 2)
            for s in range(4):
                if s >= 2:
                    dve.wait_ge(q_out[s % 2], 16)
                base = s * S // 2
                with dve.Fori(0, S // 4) as i:
                    operand(s, 2 * i, 2 * i + base, 0)
                    operand(s, 2 * i + 1, 2 * i + 1 + base, 1)

            def max_unit(k, slot, heads):
                qt, w0, w = piece(k)
                nc.vector.tensor_reduce(mx_p[:, qt, k % MP:k % MP + 1], ps[:, slot, 0:w], AX,
                                        ALU.max).then_inc(unit_ok, 1)

            def reduce_max(count, reduced):
                dve.wait_ge(unit_ok, count)
                nc.vector.tensor_reduce(mx[:, :], mx_p[:, :, :], AX, ALU.max).then_inc(mx_red, 1)

            for k in range(MAXU):
                dve.wait_ge(unit_ps, k + 1)
                max_unit(k, k % 2, 1)
            reduce_max(MAXU, 1)
            dve.wait_ge(unit_ps, MAXU + 1)
            nc.vector.tensor_scalar(mneg[:, :], ps[0:KT, MAXU % 2, 0:128], -1.0, None, ALU.mult).then_inc(unit_ok, 1)

            def period(n, p, with_max):
                us = flat(with_max)
                for u, (kind, k) in enumerate(us):
                    slot = (U_FIRST + p * U_HEAD + u) % 2
                    count = n * U_HEAD + U_FIRST + u
                    dve.wait_ge(unit_ps, count + 1)
                    if kind == "max":
                        if k == 0:
                            dve.wait_ge(mx_red, n + 1)
                        max_unit(k, slot, n)
                        if k == MAXU - 1:
                            reduce_max(count + 1, n + 2)
                    elif kind == "mt":
                        dve.wait_ge(m_out, 16 * (n + 1))
                        nc.vector.tensor_scalar(mneg[:, :], ps[0:KT, slot, 0:128], -1.0, None,
                                                ALU.mult).then_inc(unit_ok, 1)
                    else:
                        o = ps[0:T, slot, 0:2 * CT * (HD + 1)].rearrange("p (t c) -> p t c", c=HD + 1)
                        dve.wait_ge(unit_ok, count)
                        nc.vector.reciprocal(rden[:, :], o[:, :, HD]).then_inc(den_ok, 1)
                        dve.wait_ge(den_ok, n * NQ + k + 1)
                        nc.vector.tensor_tensor(attn[:, 2 * CT * k:2 * CT * (k + 1), ds(n * HD, HD)],
                                                o[:, :, 0:HD], rden[:, :].unsqueeze(2).to_broadcast([T, 2 * CT, HD]),
                                                ALU.mult).then_inc(unit_ok, 1)

            with dve.Fori(0, NH // 2 - 1) as i:
                period(2 * i, 0, True)
                period(2 * i + 1, 1, True)
            period(NH - 2, 0, True)
            period(NH - 1, 1, False)

            def round_19(c):
                dve.wait_ge(pr_ps, c + 1)
                dve.wait_ge(xb_ok, c + 1)
                x1_c = x1[:, ds(c * CT, CT), :]
                nc.vector.tensor_tensor(x1_c.rearrange("p (a b) c -> p a (b c)", a=2), ps[0:T, 2:4, 0:2 * C],
                                        xb[:, :, :].rearrange("p (a b) c -> p a (b c)", a=2),
                                        ALU.add).then_inc(x1_ok, 1)
                dve.wait_ge(x1_ok, c + 1)
                norm_chunk(dve, nc, x1_c, stats, mv, rstd, xh, ln2, c,
                           lambda: wait_used(dve, t2_ps, c))

            rounds(dve, NC, round_19)

            def mlp_sum(c, i, sems, res, free):
                dve.wait_ge(sems["dn_ps"], c + 1)
                free()
                two = dict(a=2)
                nc.vector.tensor_tensor(y_sb[:, :, :].rearrange("p (a b) c -> p a (b c)", **two),
                                        ps[0:T, 4:6, 0:2 * C], res.rearrange("p (a b) c -> p a (b c)", **two),
                                        ALU.add).then_inc(sems["sum"], 1)
                dve.wait_ge(sems["sum"], c + 1)
                nc.vector.tensor_tensor(y_sb[:, :, :], y_sb[:, :, :],
                                        rows[:, 1 + 3 * i:2 + 3 * i, :].to_broadcast([T, CT, C]),
                                        ALU.add).then_inc(sems["out"], 1)
                dve.wait_ge(sems["out"], c + 1)

            dve.wait_ge(t2_ps, NC)
            def round_20(c):
                mlp_sum(c, 0, up0, x1[:, ds(c * CT, CT), :], lambda: wait_used(dve, r3_ok, c))
                norm_chunk(dve, nc, y_sb, stats, mv, rstd, xh, ln3, c,
                           lambda: wait_used(dve, h1_mul, c))

            rounds(dve, NC, round_20)

            for g in range(KF // KG):
                dve.wait_ge(fa_ok, g + 1)
                dve.wait_ge(f2_ps, g)
                nc.vector.tensor_scalar(f_r[:, :, :, 0, :], f_a[:, :, :, 1, :], -1.0, None, ALU.mult)
                nc.vector.tensor_copy(f_r[:, :, :, 1, :], f_a[:, :, :, 0, :]).then_inc(fr_ok, 1)
                dve.wait_ge(f2_ps, g + 1)
                nc.vector.tensor_tensor(f_y[:, 0:4, :].rearrange("p (a b) c -> p a b c", a=2),
                                        ps[0:2 * S, 4:6, 0:2 * C].rearrange("p a (b c) -> p a b c", b=2),
                                        f_b2[:, :].unsqueeze(1).unsqueeze(1).to_broadcast([2 * S, 2, 2, C]), ALU.add)
                nc.vector.tensor_tensor(f_y[:, 4, :], ps[0:2 * S, 6, 0:C], f_b2[:, :], ALU.add).then_inc(fy_ok, 1)
                dve.wait_ge(fy_ok, g + 1)
                nc.vector.tensor_scalar(f_c[:, :, :], f_y[:, :, :], -LAM, LAM, ALU.max, ALU.min).then_inc(fc_ok, 1)
                dve.wait_ge(fc_ok, g + 1)
                dve.wait_ge(fi_ps, g)
                nc.vector.tensor_tensor(f_o[:, :, :], f_y[:, :, :], f_c[:, :, :], ALU.subtract).then_inc(fo_ok, 1)

            dve.wait_ge(r3_ok, NC)
            def round_21(c):
                dve.wait_ge(iw_ps, c + 1)
                x3_c = x1[:, ds(c * CT, CT), :]
                nc.vector.tensor_tensor(x3_c.rearrange("p (a b) c -> p a (b c)", a=2), ps[0:T, 2:4, 0:2 * C],
                                        r3[:, ds(c * CT, CT), :].rearrange("p (a b) c -> p a (b c)", a=2),
                                        ALU.add).then_inc(x3_ok, 1)
                dve.wait_ge(x3_ok, c + 1)
                norm_chunk(dve, nc, x3_c, stats, mv, rstd, xh, ln4, c,
                           lambda: wait_used(dve, t4_ps, c))

            rounds(dve, NC, round_21)
            def round_22(c):
                mlp_sum(c, 1, up1, x1[:, ds(c * CT, CT), :], lambda: wait_used(dve, y_out, 16 * c))

            rounds(dve, NC, round_22)

        assert NCONST[0] == ALL_CONSTS, (NCONST[0], ALL_CONSTS)


_FLAT = ("L0_conv_qkv_w", "L0_conv_proj_w", "L0_conv_proj_b", "L0_conv_ln1_g", "L0_conv_ln1_b", "L0_conv_ln2_g",
         "L0_conv_ln2_b", "L0_conv_mlp_w1", "L0_conv_mlp_b1", "L0_conv_mlp_w2", "L0_conv_mlp_b2", "L1_conv_g1",
         "L1_conv_be1", "L1_conv_g2", "L1_conv_be2", "L1_conv_fc1_w", "L1_conv_fc1_b", "L1_conv_fc2_w",
         "L1_conv_fc2_b")


def constants():
    import numpy as np

    r = np.arange(S)
    c = {"c_ident": np.eye(128, dtype=np.float32)}
    mask = np.zeros((128, 3), np.float32)
    mask[HD:2 * HD, 0] = 1.0
    for i in range(3):
        mask[2 * HD + (2 * i + 1) * R3:2 * HD + (2 * i + 2) * R3, 0] = 1.0
        mask[HD + (2 * i + 1) * R3:HD + (2 * i + 2) * R3, 1] = 1.0
    mask[2 * HD:3 * HD, 2] = -1.0
    c["c_mask"] = mask
    rh = S - 1 - (np.arange(6)[:, None, None, None] * 8 + np.arange(8)[:, None]) + np.zeros((6, 3, 8, R3), int)
    rw = S - 1 - (np.arange(3)[:, None, None] * R3 + np.arange(R3)) + np.zeros((6, 3, 8, R3), int)
    rh, rw = rh.reshape(N), rw.reshape(N)
    x = np.arange(R3)[:, None]
    row, col = rh % R3 == x, rw % R3 == x
    c["c_onehot"] = np.concatenate([row, row, col, col, np.ones((1, N))]).astype(np.float16)
    c["c_onehot_c"] = np.concatenate([rh == r[:, None], rw == r[:, None]]).astype(np.float16)
    esel = np.zeros((S, 2 * HD), np.float16)
    for j in range(HD):
        for a in range(2):
            for b in range(2):
                esel[a * HD + j, b * HD + j] = 1.0
    c["c_esel"] = esel
    sel = np.zeros((128, 2, HD + 1), np.float32)
    for half in range(2):
        for e in range(2):
            for j in range(HD + 1):
                sel[32 * (2 * e + half) + j, half, j] = 1.0
    c["c_sel"] = sel
    ang = 2 * np.pi * (np.outer(r, np.arange(KF)) % S) / S
    dw, iw = np.zeros((2, S, 2, 2, KF)), np.zeros((2, 2, KF, 2, S))
    wt = np.where((np.arange(KF) == 0) | (np.arange(KF) == S // 2), 1.0, 2.0)[:, None]
    for a in range(2):
        dw[a, :, a, 0], dw[a, :, a, 1] = np.cos(ang), -np.sin(ang)
        iw[a, 0, :, a], iw[a, 1, :, a] = wt * np.cos(ang).T / S, -wt * np.sin(ang).T / S
    c["c_dft_w"] = (dw / S).reshape(T, 4 * KF).astype(np.float32)
    c["c_idft_w"] = iw.reshape(4 * KF, T).astype(np.float32)
    ang = 2 * np.pi * (np.outer(r, r) % S) / S
    co, si = np.cos(ang), np.sin(ang)
    fwd = np.block([[co, -si], [si, co]])
    inv = np.block([[co, si], [-si, co]])
    c["c_dft_h"] = np.stack([fwd, inv], 1).astype(np.float32)
    return c


def kernel(**inputs):
    import numpy as np
    import concourse.bacc as bacc
    from concourse.bass_utils import run_bass_kernel_spmd as run

    nc = bacc.Bacc("TRN2", target_bir_lowering=False, num_devices=1)
    arrays = {"x": np.ascontiguousarray(inputs["x"]).reshape(N, C),
              "L0_conv_qkv_b": np.ascontiguousarray(inputs["L0_conv_qkv_b"]).reshape(1, 3 * C)}
    for name in _FLAT:
        arrays[name] = np.ascontiguousarray(inputs[name])
    for short, name in (("c_rel_h", "L0_conv_rel_pos_h"), ("c_rel_w", "L0_conv_rel_pos_w")):
        table = np.ascontiguousarray(inputs[name])
        win = np.stack([table[i:i + S] for i in range(S)])
        arrays[short] = np.ascontiguousarray(np.concatenate([win.transpose(2, 0, 1)] * 3))
    arrays["f_w"] = np.ascontiguousarray(np.stack([np.ascontiguousarray(inputs[n]).transpose(3, 0, 1, 2)
                                                   for n in ("L1_conv_w1", "L1_conv_w2")]))
    for short, name in (("f_b1", "L1_conv_b1"), ("f_b2", "L1_conv_b2")):
        arrays[short] = np.ascontiguousarray(np.ascontiguousarray(inputs[name]).transpose(2, 0, 1).reshape(2, C))
    arrays.update(constants())
    d = {k: nc.dram_tensor(f"in_{k}", a.shape, mybir.dt.from_np(a.dtype), kind="ExternalInput").ap()
         for k, a in arrays.items()}
    out = nc.dram_tensor("out_0", (N, C), F32, kind="ExternalOutput").ap()
    build(nc, d, out)
    r = run(nc, [{f"in_{k}": a for k, a in arrays.items()}], core_ids=[0])
    return r.results[0]["out_0"].reshape(1, S, S, C)
```

```python
from contextlib import ExitStack

import concourse.bass as bass
from concourse import mybir

F32 = mybir.dt.float32
F16 = mybir.dt.float16
ALU = mybir.AluOpType
ACT = mybir.ActivationFunctionType
AX = mybir.AxisListType.X
ds = bass.ds

S = 48
N = S * S
C = 192
C2 = C // 2
NH = 12
HD = C // NH
SCALE = HD ** -0.5
T = 96
NT = N // T
CT = 4
NC = NT // CT
CW = CT * T
HID = 4 * C
HM = HID // 128
KT = N // 128
QW = 2 * CW
NQ = N // QW
STEPS = NQ * KT
GS = STEPS // NQ
MP = 5
MW = 464
GT = KT // NQ
GU = GT * MP
LEAD = 15
NG = 6
KF = S // 2 + 1
NB = 8
BS = C // NB
R3 = S // 3
NV = 9
QR = 3 * HD + 4 * R3
LAM = 0.01
KG = 5
G = KF // KG
EPS = 1e-5


def rounds(eng, count, body):
    body(0)
    with eng.Fori(1, count) as c:
        body(c)


def chunks(eng, body):
    body(0, True)
    body(1, True)
    with eng.Fori(2, NC - 1) as c:
        body(c, True)
    body(NC - 1, False)


def wait_used(eng, sem, count):
    if not (isinstance(count, int) and count <= 0):
        eng.wait_ge(sem, count)


def norm_chunk(dve, nc, src, stats, mv, rstd, dst, sem, n, dst_free):
    dve.nop(nofuse=True)
    for t in range(CT):
        ins = nc.vector.bn_stats(stats[:, t, :], src[:, t, :])
    ins.then_inc(sem["stats"], 1)
    dve.wait_ge(sem["stats"], n + 1)
    dve.nop(nofuse=True)
    for t in range(CT):
        ins = nc.vector.bn_aggr(mv[:, t, :], stats[:, t, :])
    ins.then_inc(sem["mean"], 1)
    dve.wait_ge(sem["mean"], n + 1)
    nc.vector.tensor_scalar(rstd[:, 0, :], mv[:, :, 1], EPS, None, ALU.add).then_inc(sem["var"], 1)
    dve.wait_ge(sem["rstd"], n + 1)
    dst_free()
    for t in range(CT):
        ins = nc.vector.tensor_scalar(dst[:, t, :], src[:, t, :], mv[:, t, 0:1], rstd[:, 1, t:t + 1],
                                      ALU.subtract, ALU.mult)
    ins.then_inc(sem["out"], 1)


def norm_root(pool, nc, rstd, sem, n):
    pool.wait_ge(sem["var"], n + 1)
    nc.gpsimd.tensor_tensor(rstd[:, 1, :], rstd[:, 0, :], rstd[:, 2, :], ALU.pow).then_inc(sem["rstd"], 1)


def build(nc, d, out):
    ctx = ExitStack()
    with ctx:
        def sb(name, shape, dt=F32, where=ctx):
            return where.enter_context(nc.sbuf_tensor(name, shape, dt))

        def sem(name):
            return ctx.enter_context(nc.semaphore(name))

        def norm_sems(name):
            return {k: sem(f"{name}_{k}") for k in ("stats", "mean", "var", "rstd", "out")}

        kq_d = nc.dram_tensor("kq_d", (2, 2, C, N), F16).ap()
        q_d = nc.dram_tensor("q_d", (2, NH, 128, N), F16).ap()
        m_d = nc.dram_tensor("m_d", (2, QW), F16).ap()
        u1_d = nc.dram_tensor("u1_d", (S, 2, KF, C), F32).ap()
        u2_d = nc.dram_tensor("u2_d", (S, 2, KF, C), F32).ap()

        attn = sb("attn", [T, NT, C])
        v_all = sb("v_all", [128, NH, KT, HD])
        w_qkv = sb("w_qkv", [C2 + 1, 2, 3 * C])
        w_proj = sb("w_proj", [C2, 2, C])
        w_up = [sb("w_up0", [C2, 2, HID])]
        w_dn = [sb("w_dn0", [128, HM, C])]
        b_up = [sb(f"b_up{i}", [128, HM]) for i in range(2)]
        gain = [sb(f"gain{i}", [C2, 2]) for i in range(3)]
        shift = [sb(f"shift{i}", [C2, 2]) for i in range(3)]
        rows = sb("rows", [T, 5, C])
        ident = sb("ident", [128, 128])
        mask = sb("mask", [128, 3])
        sel = sb("sel", [128, 2, HD + 1])
        dft_w = sb("dft_w", [T, 4 * KF])
        idft_w = sb("idft_w", [4 * KF, T])
        dft_h = sb("dft_h", [2 * S, 2, 2 * S])
        f_w = sb("f_w", [C2, 2, 2, 2, C2])
        f_wn = sb("f_wn", [C2, 2, C2])
        f_b1 = sb("f_b1", [C2, 2, 2])
        f_b2 = sb("f_b2", [2 * S, C])
        xin = sb("xin", [T, CT, C])
        xh2 = [sb(f"xh{i}", [T, CT, C]) for i in range(2)]
        stats = sb("stats", [T, CT, 6])
        mv = sb("mv", [T, CT, 2])
        rstd = sb("rstd", [T, 3, CT])

        tmp16 = sb("tmp16", [128, 4, 2 * NG * S], F16)
        mx_p = sb("mx_p", [128, KT, MP])
        mx = sb("mx", [128, KT])
        mneg = sb("mneg", [GT, 128], F16)
        rden = sb("rden", [T, 2 * CT])
        esel = sb("esel", [S, 2 * HD], F16)

        with ExitStack() as r:
            khl = sb("khl", [C2, 2, 4, 2, CW], F16, r)
            rel = [sb(f"rel{i}", [S, S, S], F32, r) for i in range(2)]
            rel_hi = [sb(f"rel_hi{i}", [S, S, S], F16, r) for i in range(2)]
            xnt = [sb(f"xnt{i}", [C2 + 1, 2, CW], F32, r) for i in range(2)]
            xnk = [sb(f"xnk{i}", [C2 + 1, 2, CW], F32, r) for i in range(2)]
            xin2 = [xin, sb("xin1", [T, CT, C], F32, r)]
        with ExitStack() as r:
            stage = [sb(f"stage{i}", [128, NG, N], F16, r) for i in range(2)]
        with ExitStack() as r:
            x1 = sb("x1", [T, NT, C], F32, r)
            xnt_all = sb("xnt_all", [C2, 2, N], F32, r)
            r3 = sb("r3", [T, NT, C], F32, r)
        qc, kc = (sb(n, [128, 2, N], F16) for n in ("qc", "kc"))
        qv = sb("qv", [128, 2, NV, QW], F16)
        ka = sb("ka", [128, 2, N], F16)

        with ExitStack() as r:
            q48 = sb("q48", [128, NH, N], F16, r)
            stat = [sb(f"stat{i}", [128, S, 128], F16, r) for i in range(2)]
        with ExitStack() as r:
            v_ext = sb("v_ext", [128, 2, KT, 32], F32, r)
            prob = sb("prob", [128, 4, QW], F32, r)
            o_sb = sb("o_sb", [128, 2, CW], F32, r)
        f_x = sb("f_x", [C2, 2, KG, 2, S])
        f_a = sb("f_a", [C2, 2, KG, 2, S])
        f_r = sb("f_r", [C2, 2, KG, 2, S])
        f_y = sb("f_y", [2 * S, KG, C])
        f_c = sb("f_c", [2 * S, KG, C])
        f_o = sb("f_o", [2 * S, KG, C])
        f_u = sb("f_u", [2 * S, KG, C])
        h1 = sb("h1", [T, CT, C])
        w_up.append(sb("w_up1", [C2, 2, HID]))
        w_dn.append(sb("w_dn1", [128, HM, C]))
        hid = sb("hid", [128, HM, CW])
        u_sb = sb("u_sb", [4 * KF, CT, C])
        y_sb = sb("y_sb", [T, CT, C])
        f_in = sb("f_in", [2 * S, 2, KG, C])
        at_c = sb("at_c", [T, CT, C])
        at_t = sb("at_t", [C2, 2, CW])
        xb = sb("xb", [T, CT, C])

        ps = ctx.enter_context(nc.psum_tensor("ps", [128, 8, 512], F32))

        first_in = sem("first_in")
        consts = sem("consts")
        fw_zero = sem("fw_zero")
        fw_neg = sem("fw_neg")
        w1_in = sem("w1_in")
        exponent = sem("exponent")
        ones_row = sem("ones_row")
        rel_in = sem("rel_in")
        zeroed = sem("zeroed")
        stat_sel = sem("stat_sel")
        rel_h16 = sem("rel_h16")
        stat_done = sem("stat_done")
        x_in = [sem("x_in0"), sem("x_in1")]
        ln1 = norm_sems("ln1")
        t1_ps = sem("t1_ps")
        xnt_ok = sem("xnt_ok")
        kq_ps = sem("kq_ps")
        kq_hi = sem("kq_hi")
        kq_lo = sem("kq_lo")
        v_ps = sem("v_ps")
        v_ok = sem("v_ok")
        kq_out = [sem("kq_out0"), sem("kq_out1")]
        q48_in = sem("q48_in")
        op_ps = sem("op_ps")
        op_hi = sem("op_hi")
        op_out = sem("op_out")
        q_out = [sem("q_out0"), sem("q_out1")]
        onehot_in = [sem("onehot_in_k"), sem("onehot_in_c")]
        c_in = [sem("c_in0"), sem("c_in1")]
        k_in = [sem("k_in0"), sem("k_in1")]
        qv_in = [sem("qv_in0"), sem("qv_in1")]
        wk_ok = sem("wk_ok")
        rel_pair = sem("rel_pair")
        v_one = sem("v_one")
        v_in = sem("v_in")
        unit_ps = sem("unit_ps")
        unit_ok = sem("unit_ok")
        mx_red = sem("mx_red")
        m_out = sem("m_out")
        s_ps = sem("s_ps")
        p_ok = sem("p_ok")
        pv_ps = sem("pv_ps")
        o_ok = sem("o_ok")
        den_ok = sem("den_ok")
        at_ok = sem("at_ok")
        at_ps = sem("at_ps")
        att_ok = sem("att_ok")
        xr_in = sem("xr_in")
        xb_ok = sem("xb_ok")
        pr_ps = sem("pr_ps")
        x1_ok = sem("x1_ok")
        x1b_ok = sem("x1b_ok")
        ln2 = norm_sems("ln2")
        t2_ps = sem("t2_ps")
        xn2_ok = sem("xn2_ok")
        up0 = {k: sem(f"mlp0_{k}") for k in ("up_ps", "act", "dn_ps", "sum")}
        up1 = {k: sem(f"mlp1_{k}") for k in ("up_ps", "act", "dn_ps", "sum")}
        ln3 = norm_sems("ln3")
        h1_mul = sem("h1_mul")
        h1_ok = sem("h1_ok")
        r3_ok = sem("r3_ok")
        fw_ps = sem("fw_ps")
        u_ok = sem("u_ok")
        u_out = sem("u_out")
        f_in_ok = [sem("f_in0"), sem("f_in1")]
        fh_ps = sem("fh_ps")
        fx_ok = sem("fx_ok")
        f1_ps = sem("f1_ps")
        fa_ok = sem("fa_ok")
        fr_ok = sem("fr_ok")
        f2_ps = sem("f2_ps")
        fy_ok = sem("fy_ok")
        fc_ok = sem("fc_ok")
        fo_ok = sem("fo_ok")
        fi_ps = sem("fi_ps")
        fu_ok = sem("fu_ok")
        fu_out = sem("fu_out")
        u2_in = sem("u2_in")
        iw_ps = sem("iw_ps")
        x3_ok = sem("x3_ok")
        x3b_ok = sem("x3b_ok")
        ln4 = norm_sems("ln4")
        t4_ps = sem("t4_ps")
        xn4_ok = sem("xn4_ok")
        y_out = sem("y_out")

        block = ctx.enter_context(nc.Block())
        x_t = d["x"].rearrange("(t p) c -> p t c", p=T)
        out_t = out.rearrange("(t p) c -> p t c", p=T)
        NCONST = [0]
        FIRST = 16 * 6

        def load(eng, dst, src):
            eng.dma_start(dst, src, allow_slow_non_contiguous=True).then_inc(consts, 16)
            NCONST[0] += 16

        def load_consts(eng):
            load(eng, w_proj[:, :, :], d["L0_conv_proj_w"].rearrange("(k p) n -> p k n", p=C2))
            for i, (up, dn, bu) in enumerate((("L0_conv_mlp_w1", "L0_conv_mlp_w2", "L0_conv_mlp_b1"),
                                              ("L1_conv_fc1_w", "L1_conv_fc2_w", "L1_conv_fc1_b"))):
                if i == 0:
                    load(eng, w_up[i][:, :, :], d[up].rearrange("(k p) n -> p k n", p=C2))
                    load(eng, w_dn[i][:, :, :], d[dn].rearrange("(k p) n -> p k n", p=128))
                load(eng, b_up[i][:, :], d[bu].rearrange("(m p) -> p m", p=128))
            load(eng, gain[1][:, :], d["L0_conv_ln2_g"].rearrange("(k p) -> p k", p=C2))
            load(eng, shift[1][:, :], d["L0_conv_ln2_b"].rearrange("(k p) -> p k", p=C2))
            load(eng, gain[2][:, :], d["L1_conv_g2"].rearrange("(k p) -> p k", p=C2))
            load(eng, shift[2][:, :], d["L1_conv_be2"].rearrange("(k p) -> p k", p=C2))
            for i, nm in enumerate(("L0_conv_proj_b", "L0_conv_mlp_b2", "L1_conv_g1", "L1_conv_be1", "L1_conv_fc2_b")):
                load(eng, rows[:, i, :], d[nm].rearrange("(o c) -> o c", o=1).to_broadcast([T, C]))
            load(eng, sel[:, :, :], d["c_sel"])
            load(eng, dft_w[:, :], d["c_dft_w"])
            load(eng, idft_w[:, :], d["c_idft_w"])
            load(eng, dft_h[:, :, :], d["c_dft_h"])
            load(eng, f_b1[:, :, :].rearrange("p r k -> p (r k)"), d["f_b1"].rearrange("r (k p) -> p (r k)", p=C2))
            for r in range(2):
                load(eng, f_b2[r * S:(r + 1) * S, :], d["f_b2"][r:r + 1, :].to_broadcast([S, C]))
            eng.wait_ge(fw_zero, 1)
            for layer in range(2):
                for b in range(NB):
                    p0 = (b % 4) * BS
                    load(eng, f_w[p0:p0 + BS, layer, b // 4, :, p0:p0 + BS],
                         d["f_w"][layer, :, b].rearrange("r k o -> k r o"))

        def wait_consts(eng):
            eng.wait_ge(consts, ALL_CONSTS)

        ALL_CONSTS = 16 * (2 + 1 + 4 + 2 + 5 + 4 + 1 + 2 + 2 * NB)

        GROUP_K = LEAD % 5 + 5

        def units(first, last):
            at = {x: [] for x in range(2 * STEPS)}
            for x in range(2 * STEPS):
                k = x // 6 * 5 + x % 6 + LEAD
                if x % 6 < 5:
                    if not (last and k // GU >= NQ - 1):
                        at[x].append(("max", k // GU + 1, k % GU))
                elif k % GU == GROUP_K and not (last and k // GU >= NQ):
                    at[x].append(("mt", k // GU, 0))
            for q in range(NQ):
                if not (first and q == 0):
                    at[2 * q * GS + 11].append(("out", q - 1, 0))
            return at

        def is_at(n, head):
            return isinstance(n, int) and n == head

        def units_of(n):
            return units(is_at(n, 0), is_at(n, NH - 1))

        def flat(n):
            return [u for x in range(2 * STEPS) for u in units_of(n)[x]]

        before = [("max", 0, k) for k in range(GU)] + [("max", 1, k) for k in range(LEAD)]
        before.insert(GU + 5, ("mt", 0, 0))
        U_HEAD = len(flat(1))
        U_ALL = len(before) + len(flat(0)) + (NH - 2) * U_HEAD + len(flat(NH - 1)) + 1
        PAIRS = STEPS // 2

        def units_before(n):
            return len(before) + (0 if is_at(n, 0) else n * U_HEAD - 1)

        def units_to(n, kind, group):
            return units_before(n) + [u[:2] for u in flat(n)].index((kind, group)) + 1

        FREE_BANK = 2

        def ring_slot(n, p, u):
            if is_at(n, NH - 1) and flat(n)[u][:2] == ("out", 1):
                return FREE_BANK
            return (len(before) + (0 if is_at(n, 0) else p * U_HEAD - 1) + u) % RING

        def s4(p, s):
            return (p * STEPS + s) % 4

        RING = 3
        assert U_HEAD % RING == 0 and MW * (MP - 1) < N <= MW * MP <= 512 * MP

        AT_SLOT, PROJECT_SLOT, NORM_SLOT = 64, 72, 92

        @block.sync
        def _(sp):
            def load_x(c):
                wait_used(sp, ln1["out"], c - 1)
                sp.dma_start(xin2[c % 2][:, :, :], x_t[:, c * CT:(c + 1) * CT, :]).then_inc(x_in[c % 2], 16)

            def load_q48(c):
                sp.wait_ge(kq_out[c % 2], 64 * (c // 2 + 1))
                for r, part in enumerate((0, 1, 0)):
                    sp.dma_start(q48[r * HD:(r + 1) * HD, :, c * CW:(c + 1) * CW],
                                 kq_d[1, part, :, c * CW:(c + 1) * CW].rearrange("(n c) t -> c n t", c=HD))\
                      .then_inc(q48_in, 16)

            def first(dst, src):
                sp.dma_start(dst, src, allow_slow_non_contiguous=True).then_inc(first_in, 16)

            load_x(0)
            first(w_qkv[0:C2, :, :], d["L0_conv_qkv_w"].rearrange("(k p) n -> p k n", p=C2))
            first(w_qkv[C2:C2 + 1, 1, :], d["L0_conv_qkv_b"])
            first(gain[0][:, :], d["L0_conv_ln1_g"].rearrange("(k p) -> p k", p=C2))
            first(shift[0][:, :], d["L0_conv_ln1_b"].rearrange("(k p) -> p k", p=C2))
            first(ident[:, :], d["c_ident"])
            first(mask[:, :], d["c_mask"])
            load_x(1)
            for c in range(NC):
                if c + 2 < NC:
                    load_x(c + 2)
                sp.wait_ge(kq_lo, c * 4 + 4)
                for i in range(4):
                    dst = kq_d[i // 2, :, (i % 2) * C2:(i % 2 + 1) * C2, c * CW:(c + 1) * CW]
                    sp.dma_start(dst.rearrange("l p t -> p l t"), khl[:, c % 2, i, :, :]).then_inc(kq_out[c % 2], 16)
                if c > 0:
                    load_q48(c - 1)
            load_q48(NC - 1)
            load_consts(sp)
            def load_c(n, p):
                parts = [(qc[0:HD, p, :], q_d[0, ds(n, 1), 0:HD, :]),
                         (kc[0:HD, p, :], kq_d[0, 0:1, ds(n * HD, HD), :])]
                for i in range(3):
                    r = HD + i * R3
                    parts.append((qc[r:r + R3, p, :], q_d[0, ds(n, 1), 2 * HD + 2 * i * R3:2 * HD + (2 * i + 1) * R3, :]))
                    r += S
                    parts.append((qc[r:r + R3, p, :], q_d[1, ds(n, 1), HD + 2 * i * R3:HD + (2 * i + 1) * R3, :]))
                for dst, src in parts:
                    sp.dma_start(dst, src.rearrange("o p t -> (o p) t")).then_inc(c_in[p], 16)

            def load_k(n, p):
                for r, part in enumerate((0, 0, 1)):
                    sp.dma_start(ka[r * HD:(r + 1) * HD, p, :],
                                 kq_d[0, part:part + 1, ds(n * HD, HD), :].rearrange("o p t -> (o p) t"))\
                      .then_inc(k_in[p], 16)

            def load_qv(n, q, b):
                def rows(ab, r0, r1):
                    return q_d[ab, ds(n, 1), r0:r1, q * QW:(q + 1) * QW].rearrange("o p t -> p o t")

                v3 = qv[:, b, :, :].rearrange("p (i j) t -> p i j t", j=3)
                parts = [(qv[0:2 * HD, b, :, :], rows(0, 0, 2 * HD).to_broadcast([2 * HD, NV, QW])),
                         (qv[2 * HD:3 * HD, b, :, :], rows(1, 0, HD).to_broadcast([HD, NV, QW]))]
                for i in range(3):
                    r = 3 * HD
                    parts.append((v3[r:r + 2 * R3, i, :, :],
                                  rows(0, 2 * HD + 2 * i * R3, 2 * HD + 2 * (i + 1) * R3).to_broadcast([2 * R3, 3, QW])))
                    r += 2 * R3
                    parts.append((v3[r:r + 2 * R3, :, i, :],
                                  rows(1, HD + 2 * i * R3, HD + 2 * (i + 1) * R3).to_broadcast([2 * R3, 3, QW])))
                for dst, src in parts:
                    sp.dma_start(dst, src).then_inc(qv_in[b], 16)

            def m_through_dram(n, p, q, count):
                b = (p + q) % 2
                sp.wait_ge(unit_ok, count)
                sp.dma_start(m_d[b].rearrange("(k t) -> k t", t=128), mneg[:, :]).then_inc(m_out, 16)
                sp.wait_ge(m_out, 16 * (n * NQ + q + 1))
                sp.dma_start(qv[QR:QR + 1, b, :, :],
                             m_d[b:b + 1, :].unsqueeze(1).to_broadcast([1, NV, QW])).then_inc(qv_in[b], 16)

            def period(n, p):
                last = is_at(n, NH - 1)
                for q in range(1, NQ):
                    wait_used(sp, s_ps, n * STEPS + (q - 1) * GS)
                    load_qv(n, q, (p + q) % 2)
                    if q == 1 and not last:
                        load_k(n + 1, 1 - p)
                    m_through_dram(n, p, q, units_to(n, "mt", q))
                if last:
                    return
                if not is_at(n, NH - 2):
                    load_c(n + 2, p)
                sp.wait_ge(s_ps, n * STEPS + (NQ - 1) * GS)
                load_qv(n + 1, 0, 1 - p)
                m_through_dram(n + 1, 1 - p, 0, units_to(n, "mt", NQ))

            for s in range(4):
                g, ab = s // 2, s % 2
                if s == 3:
                    sp.wait_ge(q_out[0], 32)
                    for p in range(2):
                        sp.dma_start(kc[HD:HD + 2 * S, p, :], d["c_onehot_c"]).then_inc(onehot_in[1], 16)
                    sp.wait_ge(q_out[1], 16)
                    load_c(0, 0)
                sp.wait_ge(op_out, (s + 1) * S // 2)
                sp.dma_start(q_d[ab, g * NG:(g + 1) * NG].rearrange("n p t -> p n t"),
                             stage[s % 2][:, :, :]).then_inc(q_out[s % 2], 16)

            sp.wait_ge(q_out[1], 32)
            for p in range(2):
                sp.dma_start(ka[3 * HD:QR + 1, p, :], d["c_onehot"]).then_inc(onehot_in[0], 16)
            load_k(0, 0)
            load_qv(0, 0, 0)
            m_through_dram(0, 0, 0, before.index(("mt", 0, 0)) + 1)
            load_c(1, 1)
            sp.dma_start(w_up[1][:, :, :], d["L1_conv_fc1_w"].rearrange("(k p) n -> p k n", p=C2)).then_inc(w1_in, 16)
            sp.dma_start(w_dn[1][:, :, :], d["L1_conv_fc2_w"].rearrange("(k p) n -> p k n", p=128)).then_inc(w1_in, 16)

            def two_periods(i):
                period(2 * i, 0)
                period(2 * i + 1, 1)

            rounds(sp, NH // 2 - 1, two_periods)
            period(NH - 2, 0)
            period(NH - 1, 1)

            def load_xr(c):
                wait_used(sp, xb_ok, c)
                sp.dma_start(xin[:, :, :], x_t[:, ds(c * CT, CT), :]).then_inc(xr_in, 16)

            u1_t = u1_d.rearrange("(t a) r k c -> (a r k) t c", a=2)
            u2_t = u2_d.rearrange("(t a) r k c -> (a r k) t c", a=2)

            def store_u1(c):
                sp.wait_ge(u_ok, c + 1)
                sp.dma_start(u1_t[:, ds(c * CT, CT), :], u_sb[:, :, :]).then_inc(u_out, 16)

            def block0(c, more):
                if more:
                    load_xr(c + 1)
                if not is_at(c, 0):
                    store_u1(c - 1)

            load_xr(0)
            chunks(sp, block0)
            store_u1(NC - 1)
            sp.wait_ge(u_out, 16 * NC)

            def f_load(g):
                for r in range(2):
                    sp.dma_start(f_in[r * S:(r + 1) * S, g % 2, :, :],
                                 u1_d[:, r, ds(g * KG, KG), :]).then_inc(f_in_ok[g % 2], 16)

            def f_store(g):
                sp.wait_ge(fu_ok, g + 1)
                for r in range(2):
                    sp.dma_start(u2_d[:, r, ds(g * KG, KG), :],
                                 f_u[r * S:(r + 1) * S, :, :]).then_inc(fu_out, 16)

            f_load(0)
            f_load(1)
            for g in range(G):
                if g + 2 < G:
                    sp.wait_ge(fh_ps, g + 1)
                    f_load(g + 2)
                f_store(g)
            sp.wait_ge(fu_out, 32 * G)

            def load_u2(c):
                wait_used(sp, iw_ps, c)
                sp.dma_start(u_sb[:, :, :], u2_t[:, ds(c * CT, CT), :]).then_inc(u2_in, 16)

            def block1(c, more):
                if more:
                    load_u2(c + 1)
                sp.wait_ge(up1["sum"], c + 1)
                sp.dma_start(out_t[:, ds(c * CT, CT), :], y_sb[:, :, :]).then_inc(y_out, 16)

            load_u2(0)
            chunks(sp, block1)
            sp.wait_ge(y_out, 16 * NC)

        @block.gpsimd
        def _(pool):
            nc.gpsimd.memset(rstd[:, 2, :], -0.5).then_inc(exponent, 1)
            pool.wait_ge(exponent, 1)
            for i in range(2):
                nc.gpsimd.memset(xnk[i][C2:C2 + 1, :, :], 1.0)
                ins = nc.gpsimd.memset(xnt[i][C2:C2 + 1, :, :], 1.0)
            ins.then_inc(ones_row, 1)
            pool.wait_ge(ones_row, 1)
            nc.gpsimd.memset(f_w[:, :, :, :, :], 0.0).then_inc(fw_zero, 1)
            norm_root(pool, nc, rstd, ln1, 0)
            nc.gpsimd.memset(stat[1][0:S, :, HD + 2 * S:], 0.0).then_inc(zeroed, 1)
            pool.wait_ge(rel_in, 48)
            nc.gpsimd.tensor_copy(stat[0][0:S, :, 0:2 * HD],
                                  esel[:, :].unsqueeze(1).to_broadcast([S, S, 2 * HD]))
            nc.gpsimd.tensor_copy(stat[1][0:S, :, 0:HD],
                                  esel[:, 0:HD].unsqueeze(1).to_broadcast([S, S, HD])).then_inc(stat_sel, 1)
            norm_root(pool, nc, rstd, ln1, 1)
            pool.wait_ge(rel_pair, 2)
            for i, c0 in ((0, 2 * HD), (1, HD)):
                o = stat[i][0:S, :, c0:c0 + 2 * S].rearrange("p x (i l r) -> p x i l r", l=2, r=R3)
                for l in range(2):
                    nc.gpsimd.tensor_copy(o[:, :, :, l, :], rel_hi[i][:, :, :].rearrange("p x (i r) -> p x i r", r=R3))\
                      .then_inc(stat_done, 1)
                    norm_root(pool, nc, rstd, ln1, 2 + 2 * i + l)
            pool.wait_ge(op_ps, 2 * S)
            nc.gpsimd.memset(v_ext[:, :, :, HD:HD + 1], 1.0)
            nc.gpsimd.memset(v_ext[:, :, :, HD + 1:32], 0.0).then_inc(v_one, 1)
            pool.wait_ge(v_ok, 3 * NC)

            def copy_v(n, p):
                nc.gpsimd.tensor_copy(v_ext[:, p, :, 0:HD],
                                      v_all[:, ds(n, 1), :, :].rearrange("p o j c -> p (o j) c")).then_inc(v_in, 1)

            copy_v(0, 0)
            copy_v(1, 1)
            with pool.Fori(1, NH // 2) as i:
                for p in range(2):
                    pool.wait_ge(pv_ps, (2 * i + p - 1) * PAIRS)
                    copy_v(2 * i + p, p)

            wait_consts(pool)
            def residual(c):
                pool.wait_ge(xr_in, 16 * (c + 1))
                wait_used(pool, x1_ok, c)
                nc.gpsimd.tensor_tensor(xb[:, :, :], xin[:, :, :],
                                        rows[:, 0:1, :].to_broadcast([T, CT, C]), ALU.add).then_inc(xb_ok, 1)
                norm_root(pool, nc, rstd, ln2, c)
                bias_into(c, 1, ln2, x1b_ok)

            def bias_into(c, row, norm, done):
                pool.wait_ge(norm["out"], c + 1)
                x1_c = x1[:, ds(c * CT, CT), :]
                nc.gpsimd.tensor_tensor(x1_c, x1_c, rows[:, row:row + 1, :].to_broadcast([T, CT, C]),
                                        ALU.add).then_inc(done, 1)

            def block0(c, more):
                if more:
                    residual(c + 1)
                norm_root(pool, nc, rstd, ln3, c)
                pool.wait_ge(h1_ok, c + 1)
                nc.gpsimd.tensor_tensor(r3[:, ds(c * CT, CT), :], h1[:, :, :], y_sb[:, :, :],
                                        ALU.add).then_inc(r3_ok, 1)

            residual(0)
            chunks(pool, block0)

            def block1(c):
                norm_root(pool, nc, rstd, ln4, c)
                bias_into(c, 4, ln4, x3b_ok)

            rounds(pool, NC, block1)

        @block.scalar
        def _(act):
            act.dma_start(rel[0][:, :, :], d["c_rel_h"]).then_inc(rel_in, 16)
            act.dma_start(rel[1][:, :, :], d["c_rel_w"]).then_inc(rel_in, 16)
            act.dma_start(esel[:, :], d["c_esel"]).then_inc(rel_in, 16)
            act.wait_ge(first_in, FIRST)
            nc.scalar.activation(w_qkv[0:C2, :, C:2 * C], w_qkv[0:C2, :, C:2 * C], ACT.Copy, scale=SCALE)
            nc.scalar.activation(w_qkv[C2:C2 + 1, 1, C:2 * C], w_qkv[C2:C2 + 1, 1, C:2 * C], ACT.Copy,
                                 scale=SCALE).then_inc(wk_ok, 1)

            def in_key_order(x):
                return x.rearrange("p (j a b) -> p a j b", j=3, b=R3)

            def gain_bias(c):
                act.wait_ge(t1_ps, c + 1)
                wait_used(act, v_ps, c - 1)
                for k in range(2):
                    nc.scalar.activation(xnt[c % 2][0:C2, k, :], ps[0:C2, k, 0:CW], ACT.Identity,
                                         bias=shift[0][:, k:k + 1], scale=gain[0][:, k:k + 1])
                    nc.scalar.activation(in_key_order(xnk[c % 2][0:C2, k, :]),
                                         ps[0:C2, k, 0:CW].rearrange("p (a j b) -> p a j b", j=3, b=R3),
                                         ACT.Identity, bias=shift[0][:, k:k + 1],
                                         scale=gain[0][:, k:k + 1]).then_inc(xnt_ok, 1)

            gain_bias(0)
            act.wait_ge(rel_in, 48)
            for i in range(2):
                nc.scalar.activation(rel_hi[i][:, :, :], rel[i][:, :, :], ACT.Copy).then_inc(rel_h16, 1)
            for c in range(NC):
                if c + 1 < NC:
                    gain_bias(c + 1)
                wait_used(act, kq_out[c % 2], 64 * (c // 2))
                for i in range(4):
                    act.wait_ge(kq_ps, 4 * c + i + 1)
                    nc.scalar.activation(khl[:, c % 2, i, 0, :], ps[0:C2, 2 + i, 0:CW], ACT.Copy).then_inc(kq_hi, 1)

            def op_hi_of(i, ab, par, first):
                act.wait_ge(op_ps, i + 1)
                if not first:
                    act.wait_ge(op_out, i - 3)
                nc.scalar.activation(tmp16[:, par, :].rearrange("p (a b) -> p a b", a=2),
                                     ps[:, 2 * par:2 * par + 2, 0:NG * S], ACT.Copy,
                                     scale=mask[:, ab:ab + 1]).then_inc(op_hi, 1)

            for par in range(4):
                op_hi_of(par, 0, par, True)
            for s in range(4):
                with act.Fori(s * S // 8 + (s == 0), (s + 1) * S // 8) as i:
                    for par in range(4):
                        op_hi_of(4 * i + par, s % 2, par, False)

            def attn_chunk(c):
                wait_used(act, at_ps, c)
                nc.scalar.activation(at_c[:, :, :], attn[:, ds(c * CT, CT), :], ACT.Copy).then_inc(at_ok, 1)

            def attn_transposed(c, bank=4):
                act.wait_ge(at_ps, c + 1)
                wait_used(act, pr_ps, c)
                nc.scalar.activation(at_t[:, :, :], ps[0:C2, bank:bank + 2, 0:CW], ACT.Copy).then_inc(att_ok, 1)

            def norm_transposed(c, i, ps_sem, done, bank=4):
                act.wait_ge(ps_sem, c + 1)
                for k in range(2):
                    nc.scalar.activation(xnt_all[:, k, ds(c * CW, CW)], ps[0:C2, bank + k, 0:CW], ACT.Identity,
                                         bias=shift[1 + i][:, k:k + 1], scale=gain[1 + i][:, k:k + 1])\
                      .then_inc(done, 1)

            def period(n, p):
                for s in range(STEPS):
                    act.wait_ge(s_ps, n * STEPS + s + 1)
                    if not (is_at(n, 0) and s < 4):
                        act.wait_ge(pv_ps, n * PAIRS + (s - 4) // 2 + 1)
                    nc.scalar.activation(prob[:, s4(p, s), :].rearrange("p (a b) -> p a b", a=2),
                                         ps[:, 3 + 2 * (s % 2):5 + 2 * (s % 2), 0:CW],
                                         ACT.Exp).then_inc(p_ok, 1)
                    if s == 1 and not is_at(n, 0):
                        out_group(n - 1, 1 - p, NQ - 1)
                    elif s % GS == 1 and s > 1:
                        out_group(n, p, s // GS - 1)
                    if is_at(n, NH - 1):
                        if s == AT_SLOT // 2 - 3:
                            act.wait_ge(unit_ok, units_to(n, "out", 0))
                            attn_chunk(0)
                        if s == AT_SLOT // 2 + 1:
                            attn_transposed(0, 0)
                        if s == NORM_SLOT // 2 + 1:
                            norm_transposed(0, 0, t2_ps, xn2_ok, 0)

            def out_group(n, p, q):
                par = (NQ * p + q) % 2
                act.wait_ge(pv_ps, n * PAIRS + (q + 1) * (GS // 2))
                if q == 2:
                    act.wait_ge(unit_ps, units_to(n, "out", 0))
                elif q == 1 and not is_at(n, 0):
                    act.wait_ge(unit_ps, units_to(n, "out", -1))
                elif q == 0 and not is_at(n, 0):
                    act.wait_ge(unit_ps, units_to(n - 1, "out", 1))
                nc.scalar.activation(o_sb[:, par, :], ps[:, 7, 0:CW], ACT.Copy).then_inc(o_ok, 1)

            wait_consts(act)
            nc.scalar.activation(f_wn[:, :, :], f_w[:, 0, :, 1, :], ACT.Copy, scale=-1.0).then_inc(fw_neg, 1)
            period(0, 0)
            period(1, 1)
            with act.Fori(1, NH // 2 - 1) as i:
                period(2 * i, 0)
                period(2 * i + 1, 1)
            period(NH - 2, 0)
            period(NH - 1, 1)
            out_group(NH - 1, 1, NQ - 1)


            def gelus(c, i, sems, between):
                wait_used(act, sems["dn_ps"], c)
                for m in range(HM):
                    if m == 2:
                        between()
                    act.wait_ge(sems["up_ps"], c * HM + m + 1)
                    nc.scalar.activation(hid[:, m, :], ps[:, m % 2, 0:CW], ACT.Gelu,
                                         bias=b_up[i][:, m:m + 1]).then_inc(sems["act"], 1)

            def spectrum(c):
                act.wait_ge(fw_ps, c + 1)
                wait_used(act, u_out, 16 * c)
                nc.scalar.activation(u_sb[:, :, :].rearrange("p (a b) c -> p a (b c)", a=2),
                                     ps[0:4 * KF, 6:8, 0:2 * C], ACT.Copy).then_inc(u_ok, 1)

            def block0(c, more):
                if more:
                    if is_at(c, 1):
                        act.wait_ge(unit_ok, U_ALL)
                    attn_chunk(c + 1)
                gelus(c, 0, up0, lambda: attn_transposed(c + 1) if more else None)
                if more:
                    norm_transposed(c + 1, 0, t2_ps, xn2_ok)
                if not is_at(c, 0):
                    spectrum(c - 1)

            chunks(act, block0)
            spectrum(NC - 1)

            def f_transformed(g):
                act.wait_ge(fh_ps, g + 1)
                wait_used(act, f1_ps, g)
                nc.scalar.activation(f_x[:, :, :, :, :].rearrange("p a k r h -> p a (k r h)"),
                                     ps[0:C2, 0:2, 0:KG * 2 * S], ACT.Copy).then_inc(fx_ok, 1)

            def f_inverse(g):
                act.wait_ge(fi_ps, g + 1)
                wait_used(act, fu_out, 32 * g)
                nc.scalar.activation(f_u[:, 0:4, :].rearrange("p (a b) c -> p a (b c)", a=2),
                                     ps[0:2 * S, 4:6, 0:2 * C], ACT.Copy)
                nc.scalar.activation(f_u[:, 4, :], ps[0:2 * S, 6, 0:C], ACT.Copy).then_inc(fu_ok, 1)

            f_transformed(0)
            for g in range(G):
                act.wait_ge(f1_ps, g + 1)
                wait_used(act, f2_ps, g)
                for k in range(2):
                    for r in range(2):
                        ins = nc.scalar.activation(
                            f_a[:, k, :, r, :],
                            ps[0:C2, 2 + k, r * KG * S:(r + 1) * KG * S].rearrange("p (k h) -> p k h", h=S),
                            ACT.Relu, bias=f_b1[:, r, k:k + 1])
                ins.then_inc(fa_ok, 1)
                if g > 0:
                    f_inverse(g - 1)
                if g + 1 < G:
                    f_transformed(g + 1)
            f_inverse(G - 1)

            def block1(c, more):
                gelus(c, 1, up1, lambda: None)
                if more:
                    norm_transposed(c + 1, 1, t4_ps, xn4_ok)

            norm_transposed(0, 1, t4_ps, xn4_ok)
            chunks(act, block1)

        @block.tensor
        def _(pe):
            def mm(o, l, r, start=True, stop=True):
                return nc.tensor.matmul(o, l, r, start=start, stop=stop)

            def transposes(src, bank):
                for k in range(2):
                    for t in range(CT):
                        ins = nc.tensor.transpose(ps[0:C2, bank + k, t * T:(t + 1) * T],
                                                  src[:, t, k * C2:(k + 1) * C2], ident[0:T, 0:T])
                return ins

            pe.wait_ge(first_in, FIRST)

            def transpose_chunk(c):
                pe.wait_ge(ln1["out"], c + 1)
                wait_used(pe, xnt_ok, 2 * c)
                transposes(xh2[c % 2], 0).then_inc(t1_ps, 1)

            transpose_chunk(0)
            pe.wait_ge(ones_row, 1)
            pe.wait_ge(wk_ok, 1)
            for c in range(NC):
                if c + 1 < NC:
                    transpose_chunk(c + 1)
                pe.wait_ge(xnt_ok, 2 * c + 2)
                for i in range(4):
                    wait_used(pe, kq_lo, 4 * (c - 1) + i + 1)
                    col = (C if i < 2 else 0) + (i % 2) * C2
                    xn = (xnk if i < 2 else xnt)[c % 2]
                    mm(ps[0:C2, 2 + i, 0:CW], w_qkv[0:C2, 0, col:col + C2], xn[0:C2, 0, :], stop=False)
                    mm(ps[0:C2, 2 + i, 0:CW], w_qkv[:, 1, col:col + C2], xn[:, 1, :],
                       start=False).then_inc(kq_ps, 1)
                wait_used(pe, v_ok, 3 * c)
                xk = xnk[c % 2]
                for j in range(3):
                    o = ps[:, 6 + j // 2, (j % 2) * C:(j % 2 + 1) * C]
                    mm(o, xk[0:C2, 0, j * 128:(j + 1) * 128], w_qkv[0:C2, 0, 2 * C:3 * C], stop=False)
                    ins = mm(o, xk[:, 1, j * 128:(j + 1) * 128], w_qkv[:, 1, 2 * C:3 * C], start=False)
                ins.then_inc(v_ps, 1)

            pe.wait_ge(q48_in, 48 * NC)
            pe.wait_ge(stat_done, 4)
            pe.wait_ge(stat_sel, 1)
            pe.wait_ge(zeroed, 1)
            pe.wait_ge(v_ok, 3 * NC)
            pe.wait_ge(kq_lo, 4 * NC)

            def op_tile(s, i, tile, par, first):
                g, ab = s // 2, s % 2
                if not first:
                    pe.wait_ge(op_out, tile - 3)
                for j in range(2):
                    r = 2 * i + j
                    if ab == 0:
                        q = q48[0:S, g * NG:(g + 1) * NG, ds(r * S, S)]
                    else:
                        q = q48[0:S, g * NG:(g + 1) * NG, :].rearrange("p n (h w) -> p n w h", w=S)[:, :, ds(r, 1), :]
                        q = q.rearrange("p n o h -> p n (o h)")
                    ins = mm(ps[:, 2 * par + j, 0:NG * S].rearrange("p (n w) -> p n w", n=NG),
                             stat[ab][0:S, ds(r, 1), :].rearrange("p o m -> p (o m)"), q)
                ins.then_inc(op_ps, 1)

            for s in range(4):
                base = s * S // 2
                if s == 0:
                    for par in range(4):
                        op_tile(0, par, par, par, True)
                with pe.Fori(1 if s == 0 else 0, S // 8) as i:
                    for par in range(4):
                        op_tile(s, 4 * i + par, 4 * i + par + base, par, False)

            pe.wait_ge(op_out, 2 * S)
            pe.wait_ge(onehot_in[1], 32)

            def ring_unit(n, p, unit, count, slot):
                kind, group, k = unit
                other = group // NQ % 2 if group > 0 else 0
                hp, q = (p + other) % 2, group % NQ
                if kind == "max" and q == 0 and k == 0:
                    pe.wait_ge(c_in[hp], 128 * (heads_like(n, p) + 1 + (p if other else 0)))
                if not (isinstance(count, int) and count < RING):
                    ends = is_at(n, NH - 1) and kind == "out" and group > 0
                    pe.wait_ge(unit_ok, count - (0 if ends else RING - 1))
                if kind == "max":
                    qt, w = q * GT + k // MP, k % MP * MW
                    end = min(w + MW, N)
                    mm(ps[:, slot, 0:end - w], qc[0:HD + 2 * S, hp, qt * 128:(qt + 1) * 128],
                       kc[0:HD + 2 * S, hp, w:end]).then_inc(unit_ps, 1)
                elif kind == "mt":
                    pe.wait_ge(mx_red, n * NQ + group + 1)
                    nc.tensor.transpose(ps[0:GT, slot, 0:128], mx[:, q * GT:(q + 1) * GT], ident[:, :])\
                      .then_inc(unit_ps, 1)
                else:
                    pe.wait_ge(o_ok, n * NQ + group + 1)
                    for t in range(CT):
                        ins = mm(ps[0:T, slot, t * 2 * (HD + 1):(t + 1) * 2 * (HD + 1)],
                                 o_sb[:, (NQ * p + group) % 2, t * T:(t + 1) * T],
                                 sel[:, :, :].rearrange("p h c -> p (h c)"))
                    ins.then_inc(unit_ps, 1)

            def attn_transposed(c, bank=4):
                pe.wait_ge(at_ok, c + 1)
                wait_used(pe, xn2_ok, 2 * c)
                transposes(at_c, bank).then_inc(at_ps, 1)

            def project(c, bank=6):
                pe.wait_ge(att_ok, c + 1)
                for t in range(CT):
                    for k in range(2):
                        ins = mm(ps[0:T, bank + t // 2, (t % 2) * C:(t % 2 + 1) * C],
                                 at_t[:, k, t * T:(t + 1) * T], w_proj[:, k, :], start=(k == 0), stop=(k == 1))
                ins.then_inc(pr_ps, 1)

            def norm_transposed(c, norm, done, bank=4):
                pe.wait_ge(norm["out"], c + 1)
                transposes(xh2[0], bank).then_inc(done, 1)

            def heads_like(n, p):
                return half[0] if half[0] is not None else n // 2

            half = [None]
            for u, unit in enumerate(before):
                ring_unit(0, 0, unit, u, u % RING)
            pe.wait_ge(v_one, 1)
            pe.wait_ge(onehot_in[0], 32)
            wait_consts(pe)

            def scores(n, p, s, j):
                k0, q = (s % GS) * 128, s // GS
                if j == 0 and (s >= 2 or not is_at(n, 0)):
                    pe.wait_ge(p_ok, n * STEPS + s - 1)
                v = (2 - s % GS // 6) * 3 + 2 - s % 3
                if s % GS == 0 and j == 0:
                    pe.wait_ge(qv_in[(p + q) % 2], 144 * (3 * heads_like(n, p) + (3 * p + q) // 2 + 1))
                ins = mm(ps[:, 3 + 2 * (s % 2) + j, 0:CW], ka[0:QR + 1, p, k0:k0 + 128],
                         qv[0:QR + 1, (p + q) % 2, v, j * CW:(j + 1) * CW])
                if j == 1:
                    ins.then_inc(s_ps, 1)

            def values(n, p, s):
                q = s // GS
                pe.wait_ge(p_ok, n * STEPS + s + 2)
                if s % GS == 0 and not (is_at(n, 0) and q == 0):
                    pe.wait_ge(o_ok, n * NQ + q)
                for e in range(2):
                    for j in range(2):
                        r = 32 * (2 * e + j)
                        ins = nc.tensor.matmul(ps[r:r + 32, 7, 0:CW], v_ext[:, p, (s + e) % GS, :],
                                               prob[:, s4(p, s + e), j * CW:(j + 1) * CW],
                                               start=(s % GS == 0), stop=(s % GS == GS - 2),
                                               tile_position=(0, r))
                ins.then_inc(pv_ps, 1)

            def period(n, p):
                at, u = units_of(n), 0
                pe.wait_ge(k_in[p], 48 * (heads_like(n, p) + 1))

                def slot_units(x):
                    nonlocal u
                    if is_at(n, NH - 1):
                        if x == AT_SLOT:
                            pe.wait_ge(unit_ok, units_before(n) + u)
                            attn_transposed(0, 0)
                        if x == PROJECT_SLOT:
                            project(0, 0)
                        if x == NORM_SLOT:
                            pe.wait_ge(x1_ok, 1)
                            norm_transposed(0, ln2, t2_ps, 0)
                    for unit in at[x]:
                        ring_unit(n, p, unit, units_before(n) + u, ring_slot(n, p, u))
                        u += 1

                for s in range(0, STEPS, 2):
                    scores(n, p, s, 0)
                    scores(n, p, s, 1)
                    slot_units(2 * s)
                    scores(n, p, s + 1, 0)
                    slot_units(2 * s + 1)
                    scores(n, p, s + 1, 1)
                    slot_units(2 * s + 2)
                    if s == 0 and not is_at(n, 0):
                        values(n - 1, 1 - p, STEPS - 2)
                    if s == 0:
                        pe.wait_ge(v_in, n + 1)
                    else:
                        values(n, p, s - 2)
                    slot_units(2 * s + 3)

            period(0, 0)
            period(1, 1)
            with pe.Fori(1, NH // 2 - 1) as i:
                half[0] = i
                period(2 * i, 0)
                period(2 * i + 1, 1)
            half[0] = None
            period(NH - 2, 0)
            period(NH - 1, 1)
            values(NH - 1, 1, STEPS - 2)
            def up(c, i, sems, xn_ok, between):
                pe.wait_ge(xn_ok, 2 * c + 2)
                for m in range(HM):
                    if m == 2:
                        between()
                    if m >= 2:
                        pe.wait_ge(sems["act"], c * HM + m - 1)
                    else:
                        wait_used(pe, sems["act"], c * HM)
                    for k in range(2):
                        ins = mm(ps[:, m % 2, 0:CW], w_up[i][:, k, m * 128:(m + 1) * 128],
                                 xnt_all[:, k, ds(c * CW, CW)], start=(k == 0), stop=(k == 1))
                    ins.then_inc(sems["up_ps"], 1)

            def down(c, i, sems):
                pe.wait_ge(sems["act"], (c + 1) * HM)
                wait_used(pe, sems["sum"], c)
                for t in range(CT):
                    for m in range(HM):
                        ins = mm(ps[0:T, 2 + t // 2, (t % 2) * C:(t % 2 + 1) * C],
                                 hid[:, m, t * T:(t + 1) * T], w_dn[i][:, m, :],
                                 start=(m == 0), stop=(m == HM - 1))
                ins.then_inc(sems["dn_ps"], 1)

            def dft(c):
                pe.wait_ge(h1_ok, c + 1)
                for j in range(2):
                    ins = mm(ps[0:4 * KF, 6 + j, 0:2 * C], dft_w[:, :],
                             h1[:, 2 * j:2 * j + 2, :].rearrange("p t c -> p (t c)"))
                ins.then_inc(fw_ps, 1)

            def block0(c, more):
                up(c, 0, up0, xn2_ok, lambda: attn_transposed(c + 1) if more else None)
                if is_at(c, 0):
                    ring_unit(NH - 1, 1, ("out", NQ - 1, 0), U_ALL - 1, FREE_BANK)
                if more:
                    wait_used(pe, u_ok, c - 1)
                    project(c + 1)
                if is_at(c, 0):
                    pe.wait_ge(unit_ok, U_ALL)
                down(c, 0, up0)
                if more:
                    norm_transposed(c + 1, ln2, t2_ps)
                if not is_at(c, 0):
                    if more:
                        pe.wait_ge(x1_ok, c + 2)
                    else:
                        wait_used(pe, u_ok, c - 1)
                    dft(c - 1)

            chunks(pe, block0)
            pe.wait_ge(u_ok, NC - 1)
            dft(NC - 1)

            def transform(g):
                pe.wait_ge(f_in_ok[g % 2], 32 * (g // 2 + 1))
                wait_used(pe, fx_ok, g)
                for k in range(2):
                    for f in range(KG):
                        ins = mm(ps[0:C2, k, f * 2 * S:(f + 1) * 2 * S], f_in[:, g % 2, f, k * C2:(k + 1) * C2],
                                 dft_h[:, 0, :])
                ins.then_inc(fh_ps, 1)

            def layer1(g):
                pe.wait_ge(fx_ok, g + 1)
                wait_used(pe, fa_ok, g)
                for k in range(2):
                    for r in range(2):
                        o = ps[0:C2, 2 + k, r * KG * S:(r + 1) * KG * S].rearrange("p (k h) -> p k h", h=S)
                        w_r, w_i = f_w[:, 0, k, 0, :], f_w[:, 0, k, 1, :]
                        mm(o, w_r, f_x[:, k, :, r, :], stop=False)
                        ins = mm(o, f_wn[:, k, :] if r == 0 else w_i, f_x[:, k, :, 1 - r, :], start=False)
                ins.then_inc(f1_ps, 1)

            def layer2(g):
                pe.wait_ge(fr_ok, g + 1)
                wait_used(pe, fu_ok, g)
                for f in range(KG):
                    for k in range(2):
                        o = ps[0:2 * S, 4 + f // 2, (f % 2) * C + k * C2:(f % 2) * C + (k + 1) * C2]
                        mm(o, f_a[:, k, f, :, :].rearrange("p r h -> p (r h)"), f_w[:, 1, k, 0, :], stop=False)
                        ins = mm(o, f_r[:, k, f, :, :].rearrange("p r h -> p (r h)"), f_w[:, 1, k, 1, :],
                                 start=False)
                ins.then_inc(f2_ps, 1)

            def inverse(g):
                pe.wait_ge(fo_ok, g + 1)
                for j in range(-(-KG // 2)):
                    w = min(2, KG - 2 * j)
                    ins = mm(ps[0:2 * S, 4 + j, 0:w * C], dft_h[:, 1, :],
                             f_o[:, 2 * j:2 * j + w, :].rearrange("p f c -> p (f c)"))
                ins.then_inc(fi_ps, 1)

            pe.wait_ge(fw_neg, 1)
            pe.wait_ge(up0["sum"], NC)
            pe.wait_ge(u_ok, NC)
            transform(0)
            for g in range(G):
                layer1(g)
                if g > 0:
                    inverse(g - 1)
                if g + 1 < G:
                    transform(g + 1)
                layer2(g)
            inverse(G - 1)

            def inverse_w(c):
                pe.wait_ge(u2_in, 16 * (c + 1))
                wait_used(pe, x3_ok, c)
                for j in range(2):
                    ins = mm(ps[0:T, 6 + j, 0:2 * C], idft_w[:, :],
                             u_sb[:, 2 * j:2 * j + 2, :].rearrange("p t c -> p (t c)"))
                ins.then_inc(iw_ps, 1)

            def block1(c, more):
                up(c, 1, up1, xn4_ok, lambda: inverse_w(c + 1) if more else None)
                down(c, 1, up1)
                if more:
                    norm_transposed(c + 1, ln4, t4_ps)

            pe.wait_ge(fu_ok, G)
            inverse_w(0)
            norm_transposed(0, ln4, t4_ps)
            pe.wait_ge(w1_in, 32)
            chunks(pe, block1)

        @block.vector
        def _(dve):
            def norm1(c):
                dve.wait_ge(x_in[c % 2], 16 * (c // 2 + 1))
                norm_chunk(dve, nc, xin2[c % 2], stats, mv, rstd, xh2[c % 2], ln1, c,
                           lambda: wait_used(dve, t1_ps, c - 1))

            norm1(0)
            norm1(1)
            dve.wait_ge(rel_h16, 2)
            dve.wait_ge(first_in, FIRST)
            for i in range(2):
                nc.vector.scalar_tensor_tensor(out=rel_hi[i][:, :, :], in0=rel_hi[i][:, :, :],
                                               scalar=mask[0:S, 2:3], in1=rel[i][:, :, :],
                                               op0=ALU.mult, op1=ALU.add).then_inc(rel_pair, 1)
            for c in range(NC):
                if c + 2 < NC:
                    norm1(c + 2)
                for i in range(4):
                    dve.wait_ge(kq_hi, 4 * c + i + 1)
                    lo, hi, x = khl[:, c % 2, i, 1, :], khl[:, c % 2, i, 0, :], ps[0:C2, 2 + i, 0:CW]
                    nc.vector.tensor_tensor(lo, x, hi, ALU.subtract).then_inc(kq_lo, 1)
                dve.wait_ge(v_ps, c + 1)
                for j in range(3):
                    nc.vector.tensor_copy(v_all[:, :, ds(c * 3 + j, 1), :].rearrange("p n o c -> p n (o c)"),
                                          ps[:, 6 + j // 2, (j % 2) * C:(j % 2 + 1) * C]
                                          .rearrange("p (n c) -> p n c", c=HD)).then_inc(v_ok, 1)

            def operand(s, i, tile, par):
                g, ab = s // 2, s % 2
                dve.wait_ge(op_hi, tile + 1)
                st = stage[s % 2]
                if ab == 0:
                    o = st[:, :, ds(i * 2 * S, 2 * S)].rearrange("p n (r w) -> p r n w", r=2)
                else:
                    o = st[:, :, :].rearrange("p n (h w) -> p w n h", w=S)[:, ds(i * 2, 2), :, :]
                nc.vector.tensor_tensor(o, ps[:, 2 * par:2 * par + 2, 0:NG * S].rearrange("p r (n w) -> p r n w", n=NG),
                                        tmp16[:, par, :].rearrange("p (r n w) -> p r n w", r=2, n=NG),
                                        ALU.subtract).then_inc(op_out, 1)

            for p in range(2):
                dve.wait_ge(kq_out[p], 64 * NC // 2)
            dve.wait_ge(stat_done, 4)
            for s in range(4):
                if s >= 2:
                    dve.wait_ge(q_out[s % 2], 16)
                base = s * S // 2
                with dve.Fori(0, S // 8) as i:
                    for par in range(4):
                        operand(s, 4 * i + par, 4 * i + par + base, par)

            def projected(c, bank=6):
                dve.wait_ge(pr_ps, c + 1)
                dve.wait_ge(xb_ok, c + 1)
                x1_c = x1[:, ds(c * CT, CT), :]
                nc.vector.tensor_tensor(x1_c.rearrange("p (a b) c -> p a (b c)", a=2), ps[0:T, bank:bank + 2, 0:2 * C],
                                        xb[:, :, :].rearrange("p (a b) c -> p a (b c)", a=2),
                                        ALU.add).then_inc(x1_ok, 1)
                dve.wait_ge(x1_ok, c + 1)
                norm_chunk(dve, nc, x1_c, stats, mv, rstd, xh2[0], ln2, c,
                           lambda: wait_used(dve, t2_ps, c))

            def ring_unit(n, p, unit, count, slot):
                kind, group, k = unit
                q = group % NQ
                dve.wait_ge(unit_ps, count + 1)
                if kind == "max":
                    if k == 0:
                        wait_used(dve, mx_red, 0 if is_at(n, 0) and group < NQ else n * NQ + group - 2)
                    nc.vector.tensor_reduce(mx_p[:, q * GT + k // MP, k % MP:k % MP + 1], ps[:, slot, 0:min(MW, N - k % MP * MW)], AX,
                                            ALU.max).then_inc(unit_ok, 1)
                    if k == GU - 1:
                        dve.wait_ge(unit_ok, count + 1)
                        nc.vector.tensor_reduce(mx[:, q * GT:(q + 1) * GT], mx_p[:, q * GT:(q + 1) * GT, :], AX,
                                                ALU.max).then_inc(mx_red, 1)
                elif kind == "mt":
                    if not (is_at(n, 0) and group == 0):
                        dve.wait_ge(m_out, 16 * (n * NQ + group))
                    nc.vector.tensor_scalar(mneg[:, :], ps[0:GT, slot, 0:128], -1.0, None,
                                            ALU.mult).then_inc(unit_ok, 1)
                else:
                    o = ps[0:T, slot, 0:2 * CT * (HD + 1)].rearrange("p (t h c) -> p h t c", h=2, c=HD + 1)
                    r = rden[:, :].rearrange("p (h t) -> p h t", h=2)
                    head = n - 1 if group < 0 else n
                    dve.wait_ge(unit_ok, count)
                    nc.vector.reciprocal(r, o[:, :, :, HD]).then_inc(den_ok, 1)
                    dve.wait_ge(den_ok, n * NQ + group + 1)
                    a = attn[:, 2 * CT * q:2 * CT * (q + 1), ds(head * HD, HD)]
                    nc.vector.tensor_tensor(a.rearrange("p (h t) c -> p h t c", h=2), o[:, :, :, 0:HD],
                                            r.unsqueeze(3).to_broadcast([T, 2, CT, HD]),
                                            ALU.mult).then_inc(unit_ok, 1)

            def period(n, p):
                for u, unit in enumerate(flat(n)):
                    if is_at(n, NH - 1) and unit[:2] == ("out", 1):
                        projected(0, 0)
                    ring_unit(n, p, unit, units_before(n) + u, ring_slot(n, p, u))

            for u, unit in enumerate(before):
                ring_unit(0, 0, unit, u, u % RING)
            period(0, 0)
            period(1, 1)
            with dve.Fori(1, NH // 2 - 1) as i:
                period(2 * i, 0)
                period(2 * i + 1, 1)
            period(NH - 2, 0)
            period(NH - 1, 1)
            ring_unit(NH - 1, 1, ("out", NQ - 1, 0), U_ALL - 1, FREE_BANK)
            wait_consts(dve)

            def mlp_sum(c, sems, res_ok, free):
                dve.wait_ge(sems["dn_ps"], c + 1)
                dve.wait_ge(res_ok, c + 1)
                free()
                nc.vector.tensor_tensor(y_sb[:, :, :].rearrange("p (a b) c -> p a (b c)", a=2),
                                        ps[0:T, 2:4, 0:2 * C],
                                        x1[:, ds(c * CT, CT), :].rearrange("p (a b) c -> p a (b c)", a=2),
                                        ALU.add).then_inc(sems["sum"], 1)

            def block0(c, more):
                if more:
                    projected(c + 1)
                mlp_sum(c, up0, x1b_ok, lambda: wait_used(dve, r3_ok, c))
                dve.wait_ge(up0["sum"], c + 1)
                norm_chunk(dve, nc, y_sb, stats, mv, rstd, xh2[1], ln3, c, lambda: None)
                dve.wait_ge(ln3["out"], c + 1)
                wait_used(dve, fw_ps, c)
                wait_used(dve, r3_ok, c)
                nc.vector.tensor_tensor(h1[:, :, :], xh2[1][:, :, :],
                                        rows[:, 2:3, :].to_broadcast([T, CT, C]), ALU.mult).then_inc(h1_mul, 1)
                dve.wait_ge(h1_mul, c + 1)
                nc.vector.tensor_tensor(h1[:, :, :], h1[:, :, :],
                                        rows[:, 3:4, :].to_broadcast([T, CT, C]), ALU.add).then_inc(h1_ok, 1)

            chunks(dve, block0)

            for g in range(G):
                dve.wait_ge(fa_ok, g + 1)
                wait_used(dve, f2_ps, g)
                nc.vector.tensor_scalar(f_r[:, :, :, 0, :], f_a[:, :, :, 1, :], -1.0, None, ALU.mult)
                nc.vector.tensor_copy(f_r[:, :, :, 1, :], f_a[:, :, :, 0, :]).then_inc(fr_ok, 1)
                dve.wait_ge(f2_ps, g + 1)
                nc.vector.tensor_tensor(f_y[:, 0:4, :].rearrange("p (a b) c -> p a b c", a=2),
                                        ps[0:2 * S, 4:6, 0:2 * C].rearrange("p a (b c) -> p a b c", b=2),
                                        f_b2[:, :].unsqueeze(1).unsqueeze(1).to_broadcast([2 * S, 2, 2, C]), ALU.add)
                nc.vector.tensor_tensor(f_y[:, 4, :], ps[0:2 * S, 6, 0:C], f_b2[:, :], ALU.add).then_inc(fy_ok, 1)
                dve.wait_ge(fy_ok, g + 1)
                nc.vector.tensor_scalar(f_c[:, :, :], f_y[:, :, :], -LAM, LAM, ALU.max, ALU.min).then_inc(fc_ok, 1)
                dve.wait_ge(fc_ok, g + 1)
                wait_used(dve, fi_ps, g)
                nc.vector.tensor_tensor(f_o[:, :, :], f_y[:, :, :], f_c[:, :, :], ALU.subtract).then_inc(fo_ok, 1)

            dve.wait_ge(r3_ok, NC)
            def inverse(c):
                dve.wait_ge(iw_ps, c + 1)
                x3_c = x1[:, ds(c * CT, CT), :]
                nc.vector.tensor_tensor(x3_c.rearrange("p (a b) c -> p a (b c)", a=2), ps[0:T, 6:8, 0:2 * C],
                                        r3[:, ds(c * CT, CT), :].rearrange("p (a b) c -> p a (b c)", a=2),
                                        ALU.add).then_inc(x3_ok, 1)
                dve.wait_ge(x3_ok, c + 1)
                norm_chunk(dve, nc, x3_c, stats, mv, rstd, xh2[0], ln4, c,
                           lambda: wait_used(dve, t4_ps, c))

            def block1(c, more):
                if more:
                    inverse(c + 1)
                mlp_sum(c, up1, x3b_ok, lambda: wait_used(dve, y_out, 16 * c))

            inverse(0)
            chunks(dve, block1)

        assert NCONST[0] == ALL_CONSTS, (NCONST[0], ALL_CONSTS)


_FLAT = ("L0_conv_qkv_w", "L0_conv_proj_w", "L0_conv_proj_b", "L0_conv_ln1_g", "L0_conv_ln1_b", "L0_conv_ln2_g",
         "L0_conv_ln2_b", "L0_conv_mlp_w1", "L0_conv_mlp_b1", "L0_conv_mlp_w2", "L0_conv_mlp_b2", "L1_conv_g1",
         "L1_conv_be1", "L1_conv_g2", "L1_conv_be2", "L1_conv_fc1_w", "L1_conv_fc1_b", "L1_conv_fc2_w",
         "L1_conv_fc2_b")


def constants():
    import numpy as np

    r = np.arange(S)
    c = {"c_ident": np.eye(128, dtype=np.float32)}
    mask = np.zeros((128, 3), np.float32)
    mask[HD:2 * HD, 0] = 1.0
    for i in range(3):
        mask[2 * HD + (2 * i + 1) * R3:2 * HD + (2 * i + 2) * R3, 0] = 1.0
        mask[HD + (2 * i + 1) * R3:HD + (2 * i + 2) * R3, 1] = 1.0
    mask[2 * HD:3 * HD, 2] = -1.0
    c["c_mask"] = mask
    rh = S - 1 - (np.arange(6)[:, None, None, None] * 8 + np.arange(8)[:, None]) + np.zeros((6, 3, 8, R3), int)
    rw = S - 1 - (np.arange(3)[:, None, None] * R3 + np.arange(R3)) + np.zeros((6, 3, 8, R3), int)
    rh, rw = rh.reshape(N), rw.reshape(N)
    x = np.arange(R3)[:, None]
    row, col = rh % R3 == x, rw % R3 == x
    c["c_onehot"] = np.concatenate([row, row, col, col, np.ones((1, N))]).astype(np.float16)
    c["c_onehot_c"] = np.concatenate([rh == r[:, None], rw == r[:, None]]).astype(np.float16)
    esel = np.zeros((S, 2 * HD), np.float16)
    for j in range(HD):
        for a in range(2):
            for b in range(2):
                esel[a * HD + j, b * HD + j] = 1.0
    c["c_esel"] = esel
    sel = np.zeros((128, 2, HD + 1), np.float32)
    for half in range(2):
        for e in range(2):
            for j in range(HD + 1):
                sel[32 * (2 * e + half) + j, half, j] = 1.0
    c["c_sel"] = sel
    ang = 2 * np.pi * (np.outer(r, np.arange(KF)) % S) / S
    dw, iw = np.zeros((2, S, 2, 2, KF)), np.zeros((2, 2, KF, 2, S))
    wt = np.where((np.arange(KF) == 0) | (np.arange(KF) == S // 2), 1.0, 2.0)[:, None]
    for a in range(2):
        dw[a, :, a, 0], dw[a, :, a, 1] = np.cos(ang), -np.sin(ang)
        iw[a, 0, :, a], iw[a, 1, :, a] = wt * np.cos(ang).T / S, -wt * np.sin(ang).T / S
    c["c_dft_w"] = (dw / S).reshape(T, 4 * KF).astype(np.float32)
    c["c_idft_w"] = iw.reshape(4 * KF, T).astype(np.float32)
    ang = 2 * np.pi * (np.outer(r, r) % S) / S
    co, si = np.cos(ang), np.sin(ang)
    fwd = np.block([[co, -si], [si, co]])
    inv = np.block([[co, si], [-si, co]])
    c["c_dft_h"] = np.stack([fwd, inv], 1).astype(np.float32)
    return c


def kernel(**inputs):
    import numpy as np
    import concourse.bacc as bacc
    from concourse.bass_utils import run_bass_kernel_spmd as run

    nc = bacc.Bacc("TRN2", target_bir_lowering=False, num_devices=1)
    arrays = {"x": np.ascontiguousarray(inputs["x"]).reshape(N, C),
              "L0_conv_qkv_b": np.ascontiguousarray(inputs["L0_conv_qkv_b"]).reshape(1, 3 * C)}
    for name in _FLAT:
        arrays[name] = np.ascontiguousarray(inputs[name])
    for short, name in (("c_rel_h", "L0_conv_rel_pos_h"), ("c_rel_w", "L0_conv_rel_pos_w")):
        table = np.ascontiguousarray(inputs[name])
        win = np.stack([table[i:i + S] for i in range(S)])
        arrays[short] = np.ascontiguousarray(np.concatenate([win.transpose(2, 0, 1)] * 3))
    arrays["f_w"] = np.ascontiguousarray(np.stack([np.ascontiguousarray(inputs[n]).transpose(3, 0, 1, 2)
                                                   for n in ("L1_conv_w1", "L1_conv_w2")]))
    for short, name in (("f_b1", "L1_conv_b1"), ("f_b2", "L1_conv_b2")):
        arrays[short] = np.ascontiguousarray(np.ascontiguousarray(inputs[name]).transpose(2, 0, 1).reshape(2, C))
    arrays.update(constants())
    d = {k: nc.dram_tensor(f"in_{k}", a.shape, mybir.dt.from_np(a.dtype), kind="ExternalInput").ap()
         for k, a in arrays.items()}
    out = nc.dram_tensor("out_0", (N, C), F32, kind="ExternalOutput").ap()
    build(nc, d, out)
    r = run(nc, [{f"in_{k}": a for k, a in arrays.items()}], core_ids=[0])
    return r.results[0]["out_0"].reshape(1, S, S, C)
```

```python
from contextlib import ExitStack

import concourse.bass as bass
from concourse import mybir

F32 = mybir.dt.float32
F16 = mybir.dt.float16
ALU = mybir.AluOpType
ACT = mybir.ActivationFunctionType
AX = mybir.AxisListType.X
ds = bass.ds

S = 48
N = S * S
C = 192
C2 = C // 2
NH = 12
HD = C // NH
SCALE = HD ** -0.5
T = 96
NT = N // T
CT = 4
NC = NT // CT
CW = CT * T
HID = 4 * C
HM = HID // 128
KT = N // 128
QW = 2 * CW
NQ = N // QW
STEPS = NQ * KT
GS = STEPS // NQ
MP = 5
MW = 464
GT = KT // NQ
GU = GT * MP
LEAD = 15
NG = 6
KF = S // 2 + 1
NB = 8
BS = C // NB
R3 = S // 3
NV = 9
QR = 3 * HD + 4 * R3
LAM = 0.01
KG = 5
G = KF // KG
EPS = 1e-5
WS = 256.0


def rounds(eng, count, body):
    body(0)
    with eng.Fori(1, count) as c:
        body(c)


def chunks(eng, body):
    body(0, True)
    body(1, True)
    with eng.Fori(2, NC - 1) as c:
        body(c, True)
    body(NC - 1, False)


def wait_used(eng, sem, count):
    if not (isinstance(count, int) and count <= 0):
        eng.wait_ge(sem, count)


def norm_chunk(dve, nc, src, stats, mv, rstd, dst, sem, n, dst_free, beside_root=lambda: None):
    dve.nop(nofuse=True)
    for t in range(CT):
        ins = nc.vector.bn_stats(stats[:, t, :], src[:, t, :])
    ins.then_inc(sem["stats"], 1)
    dve.wait_ge(sem["stats"], n + 1)
    dve.nop(nofuse=True)
    for t in range(CT):
        ins = nc.vector.bn_aggr(mv[:, t, :], stats[:, t, :])
    ins.then_inc(sem["mean"], 1)
    dve.wait_ge(sem["mean"], n + 1)
    nc.vector.tensor_scalar(rstd[:, 0, :], mv[:, :, 1], EPS, None, ALU.add).then_inc(sem["var"], 1)
    beside_root()
    dve.wait_ge(sem["rstd"], n + 1)
    dst_free()
    for t in range(CT):
        ins = nc.vector.tensor_scalar(dst[:, t, :], src[:, t, :], mv[:, t, 0:1], rstd[:, 1, t:t + 1],
                                      ALU.subtract, ALU.mult)
    ins.then_inc(sem["out"], 1)


def norm_root(pool, nc, rstd, sem, n):
    pool.wait_ge(sem["var"], n + 1)
    nc.gpsimd.tensor_tensor(rstd[:, 1, :], rstd[:, 0, :], rstd[:, 2, :], ALU.pow).then_inc(sem["rstd"], 1)


def build(nc, d, out):
    ctx = ExitStack()
    with ctx:
        def sb(name, shape, dt=F32, where=ctx):
            return where.enter_context(nc.sbuf_tensor(name, shape, dt))

        def sem(name):
            return ctx.enter_context(nc.semaphore(name))

        def norm_sems(name):
            return {k: sem(f"{name}_{k}") for k in ("stats", "mean", "var", "rstd", "out")}

        kq_d = nc.dram_tensor("kq_d", (2, 2, C, N), F16).ap()
        q_d = nc.dram_tensor("q_d", (2, NH, 128, N), F16).ap()
        m_d = nc.dram_tensor("m_d", (2, QW), F16).ap()
        u1_d = nc.dram_tensor("u1_d", (S, 2, KF, C), F32).ap()
        u2_d = nc.dram_tensor("u2_d", (S, 2, KF, C), F32).ap()

        attn = sb("attn", [T, NT, C])
        v_all = sb("v_all", [128, NH, KT, HD])
        w_qkv = sb("w_qkv", [C2 + 1, 2, 3 * C])
        w_proj = sb("w_proj", [C2, 2, C])
        w_up = [sb("w_up0", [C2, 2, 2, HID], F16)]
        w_dn = [sb("w_dn0", [128, 2, HM, C], F16)]
        b_up = [sb(f"b_up{i}", [128, HM]) for i in range(2)]
        gain = [sb(f"gain{i}", [C2, 2]) for i in range(3)]
        shift = [sb(f"shift{i}", [C2, 2]) for i in range(3)]
        rows = sb("rows", [T, 5, C])
        ident = sb("ident", [128, 128])
        mask = sb("mask", [128, 3])
        sel = sb("sel", [128, 2, HD + 1])
        dft_w = sb("dft_w", [T, 4 * KF])
        idft_w = sb("idft_w", [4 * KF, T])
        dft_h = sb("dft_h", [2 * S, 2, 2 * S])
        f_w = sb("f_w", [C2, 2, 2, 2, C2])
        f_wn = sb("f_wn", [C2, 2, C2])
        f_b1 = sb("f_b1", [C2, 2, 2])
        f_b2 = sb("f_b2", [2 * S, C])
        xin = sb("xin", [T, CT, C])
        xh2 = [sb(f"xh{i}", [T, CT, C]) for i in range(2)]
        stats = sb("stats", [T, CT, 6])
        mv = sb("mv", [T, CT, 2])
        rstd = sb("rstd", [T, 3, CT])

        tmp16 = sb("tmp16", [128, 4, 2 * NG * S], F16)
        mx_p = sb("mx_p", [128, KT, MP])
        mx = sb("mx", [128, KT])
        mneg = sb("mneg", [GT, 128], F16)
        rden = sb("rden", [T, 2 * CT])
        esel = sb("esel", [S, 2 * HD], F16)

        with ExitStack() as r:
            khl = sb("khl", [C2, 2, 4, 2, CW], F16, r)
            rel = [sb(f"rel{i}", [S, S, S], F32, r) for i in range(2)]
            rel_hi = [sb(f"rel_hi{i}", [S, S, S], F16, r) for i in range(2)]
            xnt = [sb(f"xnt{i}", [C2 + 1, 2, CW], F32, r) for i in range(2)]
            xnk = [sb(f"xnk{i}", [C2 + 1, 2, CW], F32, r) for i in range(2)]
            xin2 = [xin, sb("xin1", [T, CT, C], F32, r)]
        with ExitStack() as r:
            stage = [sb(f"stage{i}", [128, NG, N], F16, r) for i in range(2)]
        with ExitStack() as r:
            x1 = sb("x1", [T, NT, C], F32, r)
            xnt_all = sb("xnt_all", [C2, NC, 2, 2, CW], F16, r)
            r3 = sb("r3", [T, NT, C], F32, r)
        qc, kc = (sb(n, [128, 2, N], F16) for n in ("qc", "kc"))
        qv = sb("qv", [128, 2, NV, QW], F16)
        ka = sb("ka", [128, 2, N], F16)

        with ExitStack() as r:
            q48 = sb("q48", [128, NH, N], F16, r)
            stat = [sb(f"stat{i}", [128, S, 128], F16, r) for i in range(2)]
        with ExitStack() as r:
            v_ext = sb("v_ext", [128, 2, KT, 32], F32, r)
            prob = sb("prob", [128, 4, QW], F32, r)
            o_sb = sb("o_sb", [128, 2, CW], F32, r)
            w_up_f = [sb(f"w_up_f{i}", [C2, 2, HID], F32, r) for i in range(2)]
            w_dn_f = [sb(f"w_dn_f{i}", [128, HM, C], F32, r) for i in range(2)]
        with ExitStack() as r:
            hid_f = sb("hid_f", [128, HM, CW], F32, r)
        f_x = sb("f_x", [C2, 2, KG, 2, S])
        f_a = sb("f_a", [C2, 2, KG, 2, S])
        f_r = sb("f_r", [C2, 2, KG, 2, S])
        f_y = sb("f_y", [2 * S, KG, C])
        f_c = sb("f_c", [2 * S, KG, C])
        f_o = sb("f_o", [2 * S, KG, C])
        f_u = sb("f_u", [2 * S, KG, C])
        h1 = sb("h1", [T, CT, C])
        hid = sb("hid", [128, HM, 2, CW], F16)
        u_sb = sb("u_sb", [4 * KF, CT, C])
        w_up.append(sb("w_up1", [C2, 2, 2, HID], F16))
        w_dn.append(sb("w_dn1", [128, 2, HM, C], F16))
        xnt_f = sb("xnt_f", [C2, 2, CW])
        y_sb = sb("y_sb", [T, CT, C])
        f_in = sb("f_in", [2 * S, 2, KG, C])
        at_c = sb("at_c", [T, CT, C])
        at_t = sb("at_t", [C2, 2, CW])
        xb = sb("xb", [T, CT, C])

        ps = ctx.enter_context(nc.psum_tensor("ps", [128, 8, 512], F32))

        first_in = sem("first_in")
        consts = sem("consts")
        fw_zero = sem("fw_zero")
        fw_neg = sem("fw_neg")
        w_mlp_in = sem("w_mlp_in")
        w_scaled = sem("w_scaled")
        w_hi = sem("w_hi")
        w_pair = sem("w_pair")
        x_hi = sem("x_hi")
        x_lo = sem("x_lo")
        exponent = sem("exponent")
        ones_row = sem("ones_row")
        rel_in = sem("rel_in")
        zeroed = sem("zeroed")
        stat_sel = sem("stat_sel")
        rel_h16 = sem("rel_h16")
        stat_done = sem("stat_done")
        x_in = [sem("x_in0"), sem("x_in1")]
        ln1 = norm_sems("ln1")
        t1_ps = sem("t1_ps")
        xnt_ok = sem("xnt_ok")
        kq_ps = sem("kq_ps")
        kq_hi = sem("kq_hi")
        kq_lo = sem("kq_lo")
        v_ps = sem("v_ps")
        v_ok = sem("v_ok")
        kq_out = [sem("kq_out0"), sem("kq_out1")]
        q48_in = [sem("q48_in"), sem("q48_in_last")]
        op_ps = sem("op_ps")
        op_hi = sem("op_hi")
        op_out = sem("op_out")
        q_out = [sem("q_out0"), sem("q_out1")]
        onehot_in = [sem("onehot_in_k"), sem("onehot_in_c")]
        c_in = [sem("c_in0"), sem("c_in1")]
        k_in = [sem("k_in0"), sem("k_in1")]
        qv_in = [sem("qv_in0"), sem("qv_in1")]
        wk_ok = sem("wk_ok")
        rel_pair = sem("rel_pair")
        v_one = sem("v_one")
        v_in = sem("v_in")
        unit_ps = sem("unit_ps")
        unit_ok = sem("unit_ok")
        mx_red = sem("mx_red")
        m_out = sem("m_out")
        s_ps = sem("s_ps")
        p_ok = sem("p_ok")
        pv_ps = sem("pv_ps")
        o_ok = sem("o_ok")
        den_ok = sem("den_ok")
        at_ok = sem("at_ok")
        at_ps = sem("at_ps")
        att_ok = sem("att_ok")
        xr_in = sem("xr_in")
        xb_ok = sem("xb_ok")
        pr_ps = sem("pr_ps")
        x1_ok = sem("x1_ok")
        x1b_ok = sem("x1b_ok")
        ln2 = norm_sems("ln2")
        t2_ps = sem("t2_ps")
        xn2_ok = sem("xn2_ok")
        up0 = {k: sem(f"mlp0_{k}") for k in ("up_ps", "act", "hi", "lo", "dn_ps", "sum")}
        up1 = {k: sem(f"mlp1_{k}") for k in ("up_ps", "act", "hi", "lo", "dn_ps", "sum")}
        ln3 = norm_sems("ln3")
        h1_mul = sem("h1_mul")
        h1_ok = sem("h1_ok")
        r3_ok = sem("r3_ok")
        fw_ps = sem("fw_ps")
        u_ok = sem("u_ok")
        u_out = sem("u_out")
        f_in_ok = [sem("f_in0"), sem("f_in1")]
        fh_ps = sem("fh_ps")
        fx_ok = sem("fx_ok")
        f1_ps = sem("f1_ps")
        fa_ok = sem("fa_ok")
        fr_ok = sem("fr_ok")
        f2_ps = sem("f2_ps")
        fy_ok = sem("fy_ok")
        fc_ok = sem("fc_ok")
        fo_ok = sem("fo_ok")
        fi_ps = sem("fi_ps")
        fu_ok = sem("fu_ok")
        fu_out = sem("fu_out")
        u2_in = sem("u2_in")
        iw_ps = sem("iw_ps")
        x3_ok = sem("x3_ok")
        x3b_ok = sem("x3b_ok")
        ln4 = norm_sems("ln4")
        t4_ps = sem("t4_ps")
        xn4_ok = sem("xn4_ok")
        y_out = sem("y_out")

        block = ctx.enter_context(nc.Block())
        x_t = d["x"].rearrange("(t p) c -> p t c", p=T)
        out_t = out.rearrange("(t p) c -> p t c", p=T)
        NCONST = [0]
        FIRST = 16 * 6

        def load(eng, dst, src):
            eng.dma_start(dst, src, allow_slow_non_contiguous=True).then_inc(consts, 16)
            NCONST[0] += 16

        def load_consts(eng):
            load(eng, w_proj[:, :, :], d["L0_conv_proj_w"].rearrange("(k p) n -> p k n", p=C2))
            for i, bu in enumerate(("L0_conv_mlp_b1", "L1_conv_fc1_b")):
                load(eng, b_up[i][:, :], d[bu].rearrange("(m p) -> p m", p=128))
            load(eng, gain[1][:, :], d["L0_conv_ln2_g"].rearrange("(k p) -> p k", p=C2))
            load(eng, shift[1][:, :], d["L0_conv_ln2_b"].rearrange("(k p) -> p k", p=C2))
            load(eng, gain[2][:, :], d["L1_conv_g2"].rearrange("(k p) -> p k", p=C2))
            load(eng, shift[2][:, :], d["L1_conv_be2"].rearrange("(k p) -> p k", p=C2))
            for i, nm in enumerate(("L0_conv_proj_b", "L0_conv_mlp_b2", "L1_conv_g1", "L1_conv_be1", "L1_conv_fc2_b")):
                load(eng, rows[:, i, :], d[nm].rearrange("(o c) -> o c", o=1).to_broadcast([T, C]))
            load(eng, sel[:, :, :], d["c_sel"])
            load(eng, dft_w[:, :], d["c_dft_w"])
            load(eng, idft_w[:, :], d["c_idft_w"])
            load(eng, dft_h[:, :, :], d["c_dft_h"])
            load(eng, f_b1[:, :, :].rearrange("p r k -> p (r k)"), d["f_b1"].rearrange("r (k p) -> p (r k)", p=C2))
            for r in range(2):
                load(eng, f_b2[r * S:(r + 1) * S, :], d["f_b2"][r:r + 1, :].to_broadcast([S, C]))
            eng.wait_ge(fw_zero, 1)
            for layer in range(2):
                for b in range(NB):
                    p0 = (b % 4) * BS
                    load(eng, f_w[p0:p0 + BS, layer, b // 4, :, p0:p0 + BS],
                         d["f_w"][layer, :, b].rearrange("r k o -> k r o"))

        def wait_consts(eng):
            eng.wait_ge(consts, ALL_CONSTS)

        ALL_CONSTS = 16 * (1 + 4 + 2 + 5 + 4 + 1 + 2 + 2 * NB)

        assert GU * 6 == 2 * GS * 5
        GROUP_K = LEAD % 5 + 5

        def units(first, last):
            at = {x: [] for x in range(2 * STEPS)}
            for x in range(2 * STEPS):
                k = x // 6 * 5 + x % 6 + LEAD
                if x % 6 < 5:
                    if not (last and k // GU >= NQ - 1):
                        at[x].append(("max", k // GU + 1, k % GU))
                elif k % GU == GROUP_K and not (last and k // GU >= NQ):
                    at[x].append(("mt", k // GU, 0))
            for q in range(NQ):
                if not (first and q == 0):
                    at[2 * q * GS + 11].append(("out", q - 1, 0))
            return at

        def chunk_of(x, c):
            return x[:, ds(c, 1), :, :, :].rearrange("p o k l t -> p (o k) l t")

        def is_at(n, head):
            return isinstance(n, int) and n == head

        def units_of(n):
            return units(is_at(n, 0), is_at(n, NH - 1))

        def flat(n):
            return [u for x in range(2 * STEPS) for u in units_of(n)[x]]

        before = [("max", 0, k) for k in range(GU)] + [("max", 1, k) for k in range(LEAD)]
        before.insert(GU + GROUP_K, ("mt", 0, 0))
        U_HEAD = len(flat(1))
        U_ALL = len(before) + len(flat(0)) + (NH - 2) * U_HEAD + len(flat(NH - 1)) + 1
        PAIRS = STEPS // 2

        def units_before(n):
            return len(before) + (0 if is_at(n, 0) else n * U_HEAD - 1)

        def units_to(n, kind, group):
            return units_before(n) + [u[:2] for u in flat(n)].index((kind, group)) + 1

        FREE_BANK = 2

        def ring_slot(n, p, u):
            if is_at(n, NH - 1) and flat(n)[u][:2] == ("out", 1):
                return FREE_BANK
            return (len(before) + (0 if is_at(n, 0) else p * U_HEAD - 1) + u) % RING

        def s4(p, s):
            return (p * STEPS + s) % 4

        RING = 3
        assert U_HEAD % RING == 0 and MW * (MP - 1) < N <= MW * MP <= 512 * MP

        POOL_TILES = 4
        AT_SLOT, PROJECT_SLOT, NORM_SLOT = 64, 72, 92

        @block.sync
        def _(sp):
            def load_x(c):
                wait_used(sp, ln1["out"], c - 1)
                sp.dma_start(xin2[c % 2][:, :, :], x_t[:, c * CT:(c + 1) * CT, :]).then_inc(x_in[c % 2], 16)

            def load_q48(c):
                sp.wait_ge(kq_out[c % 2], 64 * (c // 2 + 1))
                for r, part in enumerate((0, 1, 0)):
                    sp.dma_start(q48[r * HD:(r + 1) * HD, :, c * CW:(c + 1) * CW],
                                 kq_d[1, part, :, c * CW:(c + 1) * CW].rearrange("(n c) t -> c n t", c=HD))\
                      .then_inc(q48_in[c == NC - 1], 16)

            def first(dst, src):
                sp.dma_start(dst, src, allow_slow_non_contiguous=True).then_inc(first_in, 16)

            load_x(0)
            first(w_qkv[0:C2, :, :], d["L0_conv_qkv_w"].rearrange("(k p) n -> p k n", p=C2))
            first(w_qkv[C2:C2 + 1, 1, :], d["L0_conv_qkv_b"])
            first(gain[0][:, :], d["L0_conv_ln1_g"].rearrange("(k p) -> p k", p=C2))
            first(shift[0][:, :], d["L0_conv_ln1_b"].rearrange("(k p) -> p k", p=C2))
            first(ident[:, :], d["c_ident"])
            first(mask[:, :], d["c_mask"])
            load_x(1)
            load_x(2)
            for c in range(NC):
                if c + 3 < NC:
                    load_x(c + 3)
                sp.wait_ge(kq_lo, c * 4 + 4)
                for i in range(4):
                    dst = kq_d[i // 2, :, (i % 2) * C2:(i % 2 + 1) * C2, c * CW:(c + 1) * CW]
                    sp.dma_start(dst.rearrange("l p t -> p l t"), khl[:, c % 2, i, :, :]).then_inc(kq_out[c % 2], 16)
                if c > 0:
                    load_q48(c - 1)
            load_q48(NC - 1)
            load_consts(sp)

            def load_c(n, p):
                parts = [(qc[0:HD, p, :], q_d[0, ds(n, 1), 0:HD, :]),
                         (kc[0:HD, p, :], kq_d[0, 0:1, ds(n * HD, HD), :])]
                for i in range(3):
                    r = HD + i * R3
                    parts.append((qc[r:r + R3, p, :], q_d[0, ds(n, 1), 2 * HD + 2 * i * R3:2 * HD + (2 * i + 1) * R3, :]))
                    r += S
                    parts.append((qc[r:r + R3, p, :], q_d[1, ds(n, 1), HD + 2 * i * R3:HD + (2 * i + 1) * R3, :]))
                for dst, src in parts:
                    sp.dma_start(dst, src.rearrange("o p t -> (o p) t")).then_inc(c_in[p], 16)

            def load_k(n, p):
                for r, part in enumerate((0, 0, 1)):
                    sp.dma_start(ka[r * HD:(r + 1) * HD, p, :],
                                 kq_d[0, part:part + 1, ds(n * HD, HD), :].rearrange("o p t -> (o p) t"))\
                      .then_inc(k_in[p], 16)

            def load_qv(n, q, b):
                def rows(ab, r0, r1):
                    return q_d[ab, ds(n, 1), r0:r1, q * QW:(q + 1) * QW].rearrange("o p t -> p o t")

                v3 = qv[:, b, :, :].rearrange("p (i j) t -> p i j t", j=3)
                parts = [(qv[0:2 * HD, b, :, :], rows(0, 0, 2 * HD).to_broadcast([2 * HD, NV, QW])),
                         (qv[2 * HD:3 * HD, b, :, :], rows(1, 0, HD).to_broadcast([HD, NV, QW]))]
                for i in range(3):
                    r = 3 * HD
                    parts.append((v3[r:r + 2 * R3, i, :, :],
                                  rows(0, 2 * HD + 2 * i * R3, 2 * HD + 2 * (i + 1) * R3).to_broadcast([2 * R3, 3, QW])))
                    r += 2 * R3
                    parts.append((v3[r:r + 2 * R3, :, i, :],
                                  rows(1, HD + 2 * i * R3, HD + 2 * (i + 1) * R3).to_broadcast([2 * R3, 3, QW])))
                for dst, src in parts:
                    sp.dma_start(dst, src).then_inc(qv_in[b], 16)

            def m_through_dram(n, p, q, count):
                b = (p + q) % 2
                sp.wait_ge(unit_ok, count)
                sp.dma_start(m_d[b].rearrange("(k t) -> k t", t=128), mneg[:, :]).then_inc(m_out, 16)
                sp.wait_ge(m_out, 16 * (n * NQ + q + 1))
                sp.dma_start(qv[QR:QR + 1, b, :, :],
                             m_d[b:b + 1, :].unsqueeze(1).to_broadcast([1, NV, QW])).then_inc(qv_in[b], 16)

            def period(n, p):
                last = is_at(n, NH - 1)
                for q in range(1, NQ):
                    wait_used(sp, s_ps, n * STEPS + (q - 1) * GS)
                    load_qv(n, q, (p + q) % 2)
                    if q == 1 and not last:
                        load_k(n + 1, 1 - p)
                    m_through_dram(n, p, q, units_to(n, "mt", q))
                if last:
                    return
                if not is_at(n, NH - 2):
                    load_c(n + 2, p)
                sp.wait_ge(s_ps, n * STEPS + (NQ - 1) * GS)
                load_qv(n + 1, 0, 1 - p)
                m_through_dram(n + 1, 1 - p, 0, units_to(n, "mt", NQ))

            for s in range(4):
                g, ab = s // 2, s % 2
                if s == 3:
                    sp.wait_ge(q_out[0], 32)
                    for p in range(2):
                        sp.dma_start(kc[HD:HD + 2 * S, p, :], d["c_onehot_c"]).then_inc(onehot_in[1], 16)
                    sp.wait_ge(q_out[1], 16)
                    load_c(0, 0)
                sp.wait_ge(op_out, (s + 1) * S // 2)
                sp.dma_start(q_d[ab, g * NG:(g + 1) * NG].rearrange("n p t -> p n t"),
                             stage[s % 2][:, :, :]).then_inc(q_out[s % 2], 16)

            sp.wait_ge(q_out[1], 32)
            for p in range(2):
                sp.dma_start(ka[3 * HD:QR + 1, p, :], d["c_onehot"]).then_inc(onehot_in[0], 16)
            load_k(0, 0)
            load_qv(0, 0, 0)
            m_through_dram(0, 0, 0, before.index(("mt", 0, 0)) + 1)
            load_c(1, 1)
            for i, (up, dn) in enumerate((("L0_conv_mlp_w1", "L0_conv_mlp_w2"), ("L1_conv_fc1_w", "L1_conv_fc2_w"))):
                sp.dma_start(w_up_f[i][:, :, :], d[up].rearrange("(k p) n -> p k n", p=C2)).then_inc(w_mlp_in, 16)
                sp.dma_start(w_dn_f[i][:, :, :], d[dn].rearrange("(k p) n -> p k n", p=128)).then_inc(w_mlp_in, 16)

            def two_periods(i):
                period(2 * i, 0)
                period(2 * i + 1, 1)

            rounds(sp, NH // 2 - 1, two_periods)
            period(NH - 2, 0)
            period(NH - 1, 1)

            def load_xr(c):
                wait_used(sp, xb_ok, c)
                sp.dma_start(xin[:, :, :], x_t[:, ds(c * CT, CT), :]).then_inc(xr_in, 16)

            u1_t = u1_d.rearrange("(t a) r k c -> (a r k) t c", a=2)
            u2_t = u2_d.rearrange("(t a) r k c -> (a r k) t c", a=2)

            def store_u1(c):
                sp.wait_ge(u_ok, c + 1)
                sp.dma_start(u1_t[:, ds(c * CT, CT), :], u_sb[:, :, :]).then_inc(u_out, 16)

            def block0(c, more):
                if more:
                    load_xr(c + 1)
                if not is_at(c, 0):
                    store_u1(c - 1)

            load_xr(0)
            chunks(sp, block0)
            store_u1(NC - 1)
            sp.wait_ge(u_out, 16 * NC)

            def f_load(g):
                for r in range(2):
                    sp.dma_start(f_in[r * S:(r + 1) * S, g % 2, :, :],
                                 u1_d[:, r, ds(g * KG, KG), :]).then_inc(f_in_ok[g % 2], 16)

            def f_store(g):
                sp.wait_ge(fu_ok, g + 1)
                for r in range(2):
                    sp.dma_start(u2_d[:, r, ds(g * KG, KG), :],
                                 f_u[r * S:(r + 1) * S, :, :]).then_inc(fu_out, 16)

            f_load(0)
            f_load(1)
            for g in range(G):
                if g + 2 < G:
                    sp.wait_ge(fh_ps, g + 1)
                    f_load(g + 2)
                f_store(g)
            sp.wait_ge(fu_out, 32 * G)

            def load_u2(c):
                wait_used(sp, iw_ps, c)
                sp.dma_start(u_sb[:, :, :], u2_t[:, ds(c * CT, CT), :]).then_inc(u2_in, 16)

            def store_out(c):
                sp.wait_ge(up1["sum"], c + 1)
                sp.dma_start(out_t[:, ds(c * CT, CT), :], y_sb[:, :, :]).then_inc(y_out, 16)

            def block1(c, more):
                if more:
                    load_u2(c + 1)
                if not is_at(c, 0):
                    store_out(c - 1)

            load_u2(0)
            chunks(sp, block1)
            store_out(NC - 1)
            sp.wait_ge(y_out, 16 * NC)

        @block.gpsimd
        def _(pool):
            nc.gpsimd.memset(rstd[:, 2, :], -0.5).then_inc(exponent, 1)
            pool.wait_ge(exponent, 1)
            for i in range(2):
                nc.gpsimd.memset(xnk[i][C2:C2 + 1, :, :], 1.0)
                ins = nc.gpsimd.memset(xnt[i][C2:C2 + 1, :, :], 1.0)
            ins.then_inc(ones_row, 1)
            pool.wait_ge(ones_row, 1)
            nc.gpsimd.memset(f_w[:, :, :, :, :], 0.0).then_inc(fw_zero, 1)
            nc.gpsimd.memset(stat[1][0:S, :, HD + 2 * S:], 0.0).then_inc(zeroed, 1)
            for c in range(NC):
                norm_root(pool, nc, rstd, ln1, c)
            pool.wait_ge(op_ps, 2 * S)
            nc.gpsimd.memset(v_ext[:, :, :, HD:HD + 1], 1.0)
            nc.gpsimd.memset(v_ext[:, :, :, HD + 1:32], 0.0).then_inc(v_one, 1)
            pool.wait_ge(v_ok, 3 * NC)

            def copy_v(n, p):
                nc.gpsimd.tensor_copy(v_ext[:, p, :, 0:HD],
                                      v_all[:, ds(n, 1), :, :].rearrange("p o j c -> p (o j) c")).then_inc(v_in, 1)

            copy_v(0, 0)
            copy_v(1, 1)
            pool.wait_ge(w_mlp_in, 64)
            for w in w_up_f + w_dn_f:
                nc.gpsimd.tensor_scalar(w[:, :, :], w[:, :, :], WS, None, ALU.mult).then_inc(w_scaled, 1)
            pool.wait_ge(w_scaled, 4)
            for i in range(2):
                for f, hi in ((w_up_f[i], w_up[i][:, :, 0, :]), (w_dn_f[i], w_dn[i][:, 0, :, :])):
                    nc.gpsimd.tensor_copy(hi, f[:, :, :]).then_inc(w_hi, 1)
            pool.wait_ge(w_hi, 4)
            for i in range(2):
                for f, hi, lo in ((w_up_f[i], w_up[i][:, :, 0, :], w_up[i][:, :, 1, :]),
                                  (w_dn_f[i], w_dn[i][:, 0, :, :], w_dn[i][:, 1, :, :])):
                    nc.gpsimd.tensor_tensor(lo, f[:, :, :], hi, ALU.subtract).then_inc(w_pair, 1)
            with pool.Fori(1, NH // 2) as i:
                for p in range(2):
                    pool.wait_ge(pv_ps, (2 * i + p - 1) * PAIRS)
                    copy_v(2 * i + p, p)

            wait_consts(pool)

            def lo_of_hidden(c, sems, tiles=range(HM)):
                for m in tiles:
                    pool.wait_ge(sems["hi"], c * HM + m + 1)
                    nc.gpsimd.tensor_tensor(hid[:, m, 1, :], hid_f[:, m, :], hid[:, m, 0, :],
                                            ALU.subtract).then_inc(sems["lo"], 1)

            def residual(c):
                pool.wait_ge(xr_in, 16 * (c + 1))
                wait_used(pool, x1_ok, c)
                nc.gpsimd.tensor_tensor(xb[:, :, :], xin[:, :, :],
                                        rows[:, 0:1, :].to_broadcast([T, CT, C]), ALU.add).then_inc(xb_ok, 1)

            def bias_into(c, row, norm, done):
                pool.wait_ge(norm["out"], c + 1)
                x1_c = x1[:, ds(c * CT, CT), :]
                nc.gpsimd.tensor_tensor(x1_c, x1_c, rows[:, row:row + 1, :].to_broadcast([T, CT, C]),
                                        ALU.add).then_inc(done, 1)

            def block0(c, more):
                if more:
                    residual(c + 1)
                lo_of_hidden(c, up0)
                if more:
                    norm_root(pool, nc, rstd, ln2, c + 1)
                if not is_at(c, 0):
                    skip(c - 1)
                if more:
                    bias_into(c + 1, 1, ln2, x1b_ok)
                norm_root(pool, nc, rstd, ln3, c)

            def skip(c):
                pool.wait_ge(h1_ok, c + 1)
                nc.gpsimd.tensor_tensor(r3[:, ds(c * CT, CT), :], h1[:, :, :], y_sb[:, :, :],
                                        ALU.add).then_inc(r3_ok, 1)

            residual(0)
            norm_root(pool, nc, rstd, ln2, 0)
            bias_into(0, 1, ln2, x1b_ok)
            chunks(pool, block0)
            skip(NC - 1)

            def block1(c, more):
                lo_of_hidden(c, up1, range(POOL_TILES))
                if more:
                    norm_root(pool, nc, rstd, ln4, c + 1)
                    bias_into(c + 1, 4, ln4, x3b_ok)

            norm_root(pool, nc, rstd, ln4, 0)
            bias_into(0, 4, ln4, x3b_ok)
            chunks(pool, block1)

        @block.scalar
        def _(act):
            act.dma_start(rel[0][:, :, :], d["c_rel_h"]).then_inc(rel_in, 16)
            act.dma_start(rel[1][:, :, :], d["c_rel_w"]).then_inc(rel_in, 16)
            act.dma_start(esel[:, :], d["c_esel"]).then_inc(rel_in, 16)
            act.wait_ge(first_in, FIRST)
            nc.scalar.activation(w_qkv[0:C2, :, C:2 * C], w_qkv[0:C2, :, C:2 * C], ACT.Copy, scale=SCALE)
            nc.scalar.activation(w_qkv[C2:C2 + 1, 1, C:2 * C], w_qkv[C2:C2 + 1, 1, C:2 * C], ACT.Copy,
                                 scale=SCALE).then_inc(wk_ok, 1)

            def in_key_order(x):
                return x.rearrange("p (j a b) -> p a j b", j=3, b=R3)

            def gain_bias(c):
                act.wait_ge(t1_ps, c + 1)
                wait_used(act, v_ps, c - 1)
                for k in range(2):
                    nc.scalar.activation(xnt[c % 2][0:C2, k, :], ps[0:C2, k, 0:CW], ACT.Identity,
                                         bias=shift[0][:, k:k + 1], scale=gain[0][:, k:k + 1])
                    nc.scalar.activation(in_key_order(xnk[c % 2][0:C2, k, :]),
                                         ps[0:C2, k, 0:CW].rearrange("p (a j b) -> p a j b", j=3, b=R3),
                                         ACT.Identity, bias=shift[0][:, k:k + 1],
                                         scale=gain[0][:, k:k + 1]).then_inc(xnt_ok, 1)

            gain_bias(0)
            act.wait_ge(rel_in, 48)
            for i in range(2):
                nc.scalar.activation(rel_hi[i][:, :, :], rel[i][:, :, :], ACT.Copy).then_inc(rel_h16, 1)

            def selectors():
                nc.scalar.activation(stat[0][0:S, :, 0:2 * HD],
                                     esel[:, :].unsqueeze(1).to_broadcast([S, S, 2 * HD]), ACT.Copy)
                nc.scalar.activation(stat[1][0:S, :, 0:HD],
                                     esel[:, 0:HD].unsqueeze(1).to_broadcast([S, S, HD]), ACT.Copy)\
                  .then_inc(stat_sel, 1)

            def table(i, l):
                c0 = (2 * HD, HD)[i]
                act.wait_ge(rel_pair, 2)
                o = stat[i][0:S, :, c0:c0 + 2 * S].rearrange("p x (i l r) -> p x i l r", l=2, r=R3)
                nc.scalar.activation(o[:, :, :, l, :], rel_hi[i][:, :, :].rearrange("p x (i r) -> p x i r", r=R3),
                                     ACT.Copy).then_inc(stat_done, 1)

            for c in range(NC):
                if c + 1 < NC:
                    gain_bias(c + 1)
                if c == 1:
                    selectors()
                elif c > 1:
                    table((c - 2) // 2, c % 2)
                wait_used(act, kq_out[c % 2], 64 * (c // 2))
                for i in range(4):
                    act.wait_ge(kq_ps, 4 * c + i + 1)
                    nc.scalar.activation(khl[:, c % 2, i, 0, :], ps[0:C2, 2 + i, 0:CW], ACT.Copy).then_inc(kq_hi, 1)

            def op_hi_of(i, ab, par, first):
                act.wait_ge(op_ps, i + 1)
                if not first:
                    act.wait_ge(op_out, i - 3)
                nc.scalar.activation(tmp16[:, par, :].rearrange("p (a b) -> p a b", a=2),
                                     ps[:, 2 * par:2 * par + 2, 0:NG * S], ACT.Copy,
                                     scale=mask[:, ab:ab + 1]).then_inc(op_hi, 1)

            for par in range(4):
                op_hi_of(par, 0, par, True)
            for s in range(4):
                with act.Fori(s * S // 8 + (s == 0), (s + 1) * S // 8) as i:
                    for par in range(4):
                        op_hi_of(4 * i + par, s % 2, par, False)

            def attn_chunk(c):
                wait_used(act, at_ps, c)
                nc.scalar.activation(at_c[:, :, :], attn[:, ds(c * CT, CT), :], ACT.Copy).then_inc(at_ok, 1)

            def attn_transposed(c, bank=4):
                act.wait_ge(at_ps, c + 1)
                wait_used(act, pr_ps, c)
                nc.scalar.activation(at_t[:, :, :], ps[0:C2, bank:bank + 2, 0:CW], ACT.Copy).then_inc(att_ok, 1)

            def norm_transposed(c, i, ps_sem, done, bank=4):
                act.wait_ge(ps_sem, c + 1)
                wait_used(act, x_lo, c + i * NC)
                for k in range(2):
                    nc.scalar.activation(xnt_f[:, k, :], ps[0:C2, bank + k, 0:CW], ACT.Identity,
                                         bias=shift[1 + i][:, k:k + 1], scale=gain[1 + i][:, k:k + 1])\
                      .then_inc(done, 1)
                act.wait_ge(done, 2 * c + 2)
                nc.scalar.activation(chunk_of(xnt_all, c)[:, :, 0, :], xnt_f[:, :, :], ACT.Copy).then_inc(x_hi, 1)

            def period(n, p):
                for s in range(STEPS):
                    act.wait_ge(s_ps, n * STEPS + s + 1)
                    if not (is_at(n, 0) and s < 4):
                        act.wait_ge(pv_ps, n * PAIRS + (s - 4) // 2 + 1)
                    nc.scalar.activation(prob[:, s4(p, s), :].rearrange("p (a b) -> p a b", a=2),
                                         ps[:, 3 + 2 * (s % 2):5 + 2 * (s % 2), 0:CW],
                                         ACT.Exp).then_inc(p_ok, 1)
                    if s == 1 and not is_at(n, 0):
                        out_group(n - 1, 1 - p, NQ - 1)
                    elif s % GS == 1 and s > 1:
                        out_group(n, p, s // GS - 1)
                    if is_at(n, NH - 1):
                        if s == AT_SLOT // 2 - 3:
                            act.wait_ge(unit_ok, units_to(n, "out", 0))
                            attn_chunk(0)
                        if s == AT_SLOT // 2 + 1:
                            attn_transposed(0, 0)
                        if s == NORM_SLOT // 2 + 1:
                            norm_transposed(0, 0, t2_ps, xn2_ok, 0)

            def out_group(n, p, q):
                par = (NQ * p + q) % 2
                act.wait_ge(pv_ps, n * PAIRS + (q + 1) * (GS // 2))
                if q == 2:
                    act.wait_ge(unit_ps, units_to(n, "out", 0))
                elif q == 1 and not is_at(n, 0):
                    act.wait_ge(unit_ps, units_to(n, "out", -1))
                elif q == 0 and not is_at(n, 0):
                    act.wait_ge(unit_ps, units_to(n - 1, "out", 1))
                nc.scalar.activation(o_sb[:, par, :], ps[:, 7, 0:CW], ACT.Copy).then_inc(o_ok, 1)

            wait_consts(act)
            nc.scalar.activation(f_wn[:, :, :], f_w[:, 0, :, 1, :], ACT.Copy, scale=-1.0).then_inc(fw_neg, 1)
            period(0, 0)
            period(1, 1)
            with act.Fori(1, NH // 2 - 1) as i:
                period(2 * i, 0)
                period(2 * i + 1, 1)
            period(NH - 2, 0)
            period(NH - 1, 1)
            out_group(NH - 1, 1, NQ - 1)


            def gelus(c, i, sems, between):
                wait_used(act, sems["lo"], c * HM)

                def hi(m):
                    act.wait_ge(sems["act"], c * HM + m + 1)
                    nc.scalar.activation(hid[:, m, 0, :], hid_f[:, m, :], ACT.Copy).then_inc(sems["hi"], 1)

                for m in range(HM):
                    if m == 2:
                        between()
                    act.wait_ge(sems["up_ps"], c * HM + m + 1)
                    nc.scalar.activation(hid_f[:, m, :], ps[:, m % 2, 0:CW], ACT.Gelu,
                                         bias=b_up[i][:, m:m + 1], scale=1 / WS).then_inc(sems["act"], 1)
                    if m == 1:
                        wait_used(act, sems["dn_ps"], c)
                    if m > 0:
                        hi(m - 1)
                hi(HM - 1)

            def spectrum(c):
                act.wait_ge(fw_ps, c + 1)
                wait_used(act, u_out, 16 * c)
                nc.scalar.activation(u_sb[:, :, :].rearrange("p (a b) c -> p a (b c)", a=2),
                                     ps[0:4 * KF, 6:8, 0:2 * C], ACT.Copy).then_inc(u_ok, 1)

            def block0(c, more):
                if more:
                    if is_at(c, 1):
                        act.wait_ge(unit_ok, U_ALL)
                    attn_chunk(c + 1)
                gelus(c, 0, up0, lambda: attn_transposed(c + 1) if more else None)
                if not is_at(c, 0):
                    spectrum(c - 1)
                if more:
                    norm_transposed(c + 1, 0, t2_ps, xn2_ok)

            chunks(act, block0)
            spectrum(NC - 1)

            def f_transformed(g):
                act.wait_ge(fh_ps, g + 1)
                wait_used(act, f1_ps, g)
                nc.scalar.activation(f_x[:, :, :, :, :].rearrange("p a k r h -> p a (k r h)"),
                                     ps[0:C2, 0:2, 0:KG * 2 * S], ACT.Copy).then_inc(fx_ok, 1)

            def f_inverse(g):
                act.wait_ge(fi_ps, g + 1)
                wait_used(act, fu_out, 32 * g)
                nc.scalar.activation(f_u[:, 0:4, :].rearrange("p (a b) c -> p a (b c)", a=2),
                                     ps[0:2 * S, 4:6, 0:2 * C], ACT.Copy)
                nc.scalar.activation(f_u[:, 4, :], ps[0:2 * S, 6, 0:C], ACT.Copy).then_inc(fu_ok, 1)

            f_transformed(0)
            for g in range(G):
                act.wait_ge(f1_ps, g + 1)
                wait_used(act, f2_ps, g)
                for k in range(2):
                    for r in range(2):
                        ins = nc.scalar.activation(
                            f_a[:, k, :, r, :],
                            ps[0:C2, 2 + k, r * KG * S:(r + 1) * KG * S].rearrange("p (k h) -> p k h", h=S),
                            ACT.Relu, bias=f_b1[:, r, k:k + 1])
                ins.then_inc(fa_ok, 1)
                if g > 0:
                    f_inverse(g - 1)
                if g + 1 < G:
                    f_transformed(g + 1)
            f_inverse(G - 1)

            def block1(c, more):
                gelus(c, 1, up1, lambda: None)
                if more:
                    norm_transposed(c + 1, 1, t4_ps, xn4_ok)

            norm_transposed(0, 1, t4_ps, xn4_ok)
            chunks(act, block1)

        @block.tensor
        def _(pe):
            def mm(o, l, r, start=True, stop=True):
                return nc.tensor.matmul(o, l, r, start=start, stop=stop)

            def transposes(src, bank):
                for k in range(2):
                    for t in range(CT):
                        ins = nc.tensor.transpose(ps[0:C2, bank + k, t * T:(t + 1) * T],
                                                  src[:, t, k * C2:(k + 1) * C2], ident[0:T, 0:T])
                return ins

            pe.wait_ge(first_in, FIRST)

            def transpose_chunk(c):
                pe.wait_ge(ln1["out"], c + 1)
                wait_used(pe, xnt_ok, 2 * c)
                transposes(xh2[c % 2], 0).then_inc(t1_ps, 1)

            transpose_chunk(0)
            pe.wait_ge(ones_row, 1)
            pe.wait_ge(wk_ok, 1)
            for c in range(NC):
                if c + 1 < NC:
                    transpose_chunk(c + 1)
                pe.wait_ge(xnt_ok, 2 * c + 2)
                for i in range(4):
                    wait_used(pe, kq_lo, 4 * (c - 1) + i + 1)
                    col = (C if i < 2 else 0) + (i % 2) * C2
                    xn = (xnk if i < 2 else xnt)[c % 2]
                    mm(ps[0:C2, 2 + i, 0:CW], w_qkv[0:C2, 0, col:col + C2], xn[0:C2, 0, :], stop=False)
                    mm(ps[0:C2, 2 + i, 0:CW], w_qkv[:, 1, col:col + C2], xn[:, 1, :],
                       start=False).then_inc(kq_ps, 1)
                wait_used(pe, v_ok, 3 * c)
                xk = xnk[c % 2]
                for j in range(3):
                    o = ps[:, 6 + j // 2, (j % 2) * C:(j % 2 + 1) * C]
                    mm(o, xk[0:C2, 0, j * 128:(j + 1) * 128], w_qkv[0:C2, 0, 2 * C:3 * C], stop=False)
                    ins = mm(o, xk[:, 1, j * 128:(j + 1) * 128], w_qkv[:, 1, 2 * C:3 * C], start=False)
                ins.then_inc(v_ps, 1)

            pe.wait_ge(q48_in[0], 48 * (NC - 1))
            pe.wait_ge(stat_done, 4)
            pe.wait_ge(stat_sel, 1)
            pe.wait_ge(zeroed, 1)
            pe.wait_ge(v_ok, 3 * NC)
            pe.wait_ge(kq_lo, 4 * NC)

            def op_tile(s, i, tile, par, first):
                g, ab = s // 2, s % 2
                if not first:
                    pe.wait_ge(op_out, tile - 3)
                for j in range(2):
                    r = 2 * i + j
                    if ab == 0:
                        q = q48[0:S, g * NG:(g + 1) * NG, ds(r * S, S)]
                    else:
                        q = q48[0:S, g * NG:(g + 1) * NG, :].rearrange("p n (h w) -> p n w h", w=S)[:, :, ds(r, 1), :]
                        q = q.rearrange("p n o h -> p n (o h)")
                    ins = mm(ps[:, 2 * par + j, 0:NG * S].rearrange("p (n w) -> p n w", n=NG),
                             stat[ab][0:S, ds(r, 1), :].rearrange("p o m -> p (o m)"), q)
                ins.then_inc(op_ps, 1)

            for s in range(4):
                base = s * S // 2
                if s == 0:
                    for par in range(4):
                        op_tile(0, par, par, par, True)
                with pe.Fori(1 if s == 0 else 0, NC - (s == 0)) as i:
                    for par in range(4):
                        op_tile(s, 4 * i + par, 4 * i + par + base, par, False)
                if s == 0:
                    pe.wait_ge(q48_in[1], 48)
                    for par in range(4):
                        tile = 4 * (NC - 1) + par
                        op_tile(s, tile, tile, par, False)

            pe.wait_ge(op_out, 2 * S)
            pe.wait_ge(onehot_in[1], 32)

            def ring_unit(n, p, unit, count, slot):
                kind, group, k = unit
                other = group // NQ % 2 if group > 0 else 0
                hp, q = (p + other) % 2, group % NQ
                if kind == "max" and q == 0 and k == 0:
                    pe.wait_ge(c_in[hp], 128 * (heads_like(n, p) + 1 + (p if other else 0)))
                if not (isinstance(count, int) and count < RING):
                    ends = is_at(n, NH - 1) and kind == "out" and group > 0
                    pe.wait_ge(unit_ok, count - (0 if ends else RING - 1))
                if kind == "max":
                    qt, w = q * GT + k // MP, k % MP * MW
                    end = min(w + MW, N)
                    mm(ps[:, slot, 0:end - w], qc[0:HD + 2 * S, hp, qt * 128:(qt + 1) * 128],
                       kc[0:HD + 2 * S, hp, w:end]).then_inc(unit_ps, 1)
                elif kind == "mt":
                    pe.wait_ge(mx_red, n * NQ + group + 1)
                    nc.tensor.transpose(ps[0:GT, slot, 0:128], mx[:, q * GT:(q + 1) * GT], ident[:, :])\
                      .then_inc(unit_ps, 1)
                else:
                    pe.wait_ge(o_ok, n * NQ + group + 1)
                    for t in range(CT):
                        ins = mm(ps[0:T, slot, t * 2 * (HD + 1):(t + 1) * 2 * (HD + 1)],
                                 o_sb[:, (NQ * p + group) % 2, t * T:(t + 1) * T],
                                 sel[:, :, :].rearrange("p h c -> p (h c)"))
                    ins.then_inc(unit_ps, 1)

            def attn_transposed(c, bank=4):
                pe.wait_ge(at_ok, c + 1)
                wait_used(pe, xn2_ok, 2 * c)
                transposes(at_c, bank).then_inc(at_ps, 1)

            def project(c, bank=6):
                pe.wait_ge(att_ok, c + 1)
                for t in range(CT):
                    for k in range(2):
                        ins = mm(ps[0:T, bank + t // 2, (t % 2) * C:(t % 2 + 1) * C],
                                 at_t[:, k, t * T:(t + 1) * T], w_proj[:, k, :], start=(k == 0), stop=(k == 1))
                ins.then_inc(pr_ps, 1)

            def norm_transposed(c, norm, done, bank=4):
                pe.wait_ge(norm["out"], c + 1)
                transposes(xh2[0], bank).then_inc(done, 1)

            def heads_like(n, p):
                return half[0] if half[0] is not None else n // 2

            half = [None]
            for u, unit in enumerate(before):
                ring_unit(0, 0, unit, u, u % RING)
            pe.wait_ge(v_one, 1)
            pe.wait_ge(onehot_in[0], 32)
            wait_consts(pe)

            def scores(n, p, s, j):
                k0, q = (s % GS) * 128, s // GS
                if j == 0 and (s >= 2 or not is_at(n, 0)):
                    pe.wait_ge(p_ok, n * STEPS + s - 1)
                v = (2 - s % GS // 6) * 3 + 2 - s % 3
                if s % GS == 0 and j == 0:
                    pe.wait_ge(qv_in[(p + q) % 2], 144 * (3 * heads_like(n, p) + (3 * p + q) // 2 + 1))
                ins = mm(ps[:, 3 + 2 * (s % 2) + j, 0:CW], ka[0:QR + 1, p, k0:k0 + 128],
                         qv[0:QR + 1, (p + q) % 2, v, j * CW:(j + 1) * CW])
                if j == 1:
                    ins.then_inc(s_ps, 1)

            def values(n, p, s):
                q = s // GS
                pe.wait_ge(p_ok, n * STEPS + s + 2)
                if s % GS == 0 and not (is_at(n, 0) and q == 0):
                    pe.wait_ge(o_ok, n * NQ + q)
                for e in range(2):
                    for j in range(2):
                        r = 32 * (2 * e + j)
                        ins = nc.tensor.matmul(ps[r:r + 32, 7, 0:CW], v_ext[:, p, (s + e) % GS, :],
                                               prob[:, s4(p, s + e), j * CW:(j + 1) * CW],
                                               start=(s % GS == 0), stop=(s % GS == GS - 2),
                                               tile_position=(0, r))
                ins.then_inc(pv_ps, 1)

            def period(n, p):
                at, u = units_of(n), 0
                pe.wait_ge(k_in[p], 48 * (heads_like(n, p) + 1))

                def slot_units(x):
                    nonlocal u
                    if is_at(n, NH - 1):
                        if x == AT_SLOT:
                            pe.wait_ge(unit_ok, units_before(n) + u)
                            attn_transposed(0, 0)
                        if x == PROJECT_SLOT:
                            project(0, 0)
                        if x == NORM_SLOT:
                            pe.wait_ge(x1_ok, 1)
                            norm_transposed(0, ln2, t2_ps, 0)
                    for unit in at[x]:
                        ring_unit(n, p, unit, units_before(n) + u, ring_slot(n, p, u))
                        u += 1

                for s in range(0, STEPS, 2):
                    scores(n, p, s, 0)
                    scores(n, p, s, 1)
                    slot_units(2 * s)
                    scores(n, p, s + 1, 0)
                    slot_units(2 * s + 1)
                    scores(n, p, s + 1, 1)
                    slot_units(2 * s + 2)
                    if s == 0 and not is_at(n, 0):
                        values(n - 1, 1 - p, STEPS - 2)
                    if s == 0:
                        pe.wait_ge(v_in, n + 1)
                    else:
                        values(n, p, s - 2)
                    slot_units(2 * s + 3)

            period(0, 0)
            period(1, 1)
            with pe.Fori(1, NH // 2 - 1) as i:
                half[0] = i
                period(2 * i, 0)
                period(2 * i + 1, 1)
            half[0] = None
            period(NH - 2, 0)
            period(NH - 1, 1)
            values(NH - 1, 1, STEPS - 2)

            def up(c, i, sems, before_tile):
                x = chunk_of(xnt_all, c)

                def hi_products(m):
                    wait_used(pe, sems["act"], c * HM + m - 1 if m > 1 or not is_at(c, 0) else 0)
                    for k in range(2):
                        for part in range(2):
                            mm(ps[:, m % 2, 0:CW], w_up[i][:, k, part, m * 128:(m + 1) * 128], x[:, k, 0, :],
                               start=(k == 0 and part == 0), stop=False)

                def lo_products(m):
                    for k in range(2):
                        ins = mm(ps[:, m % 2, 0:CW], w_up[i][:, k, 0, m * 128:(m + 1) * 128], x[:, k, 1, :],
                                 start=False, stop=(k == 1))
                    ins.then_inc(sems["up_ps"], 1)

                pe.wait_ge(x_hi, i * NC + c + 1)
                hi_products(0)
                hi_products(1)
                pe.wait_ge(x_lo, i * NC + c + 1)
                lo_products(0)
                lo_products(1)
                for m in range(2, HM):
                    if m in before_tile:
                        before_tile[m]()
                    hi_products(m)
                    lo_products(m)

            def down(c, i, sems, half_way):
                def hi_products(t, tiles):
                    for m in tiles:
                        for part in range(2):
                            mm(down_tile(t), hid[:, m, 0, t * T:(t + 1) * T], w_dn[i][:, part, m, :],
                               start=(m == 0 and part == 0), stop=False)

                def lo_products(t):
                    for m in range(HM):
                        ins = mm(down_tile(t), hid[:, m, 1, t * T:(t + 1) * T], w_dn[i][:, 0, m, :],
                                 start=False, stop=(m == HM - 1))
                    return ins

                def down_tile(t):
                    return ps[0:T, 2 + t // 2, (t % 2) * C:(t % 2 + 1) * C]

                pe.wait_ge(sems["hi"], (c + 1) * HM - 1)
                wait_used(pe, sems["sum"], c)
                for t in (0, 2):
                    hi_products(t, range(HM - 1))
                pe.wait_ge(sems["hi"], (c + 1) * HM)
                for t in (0, 2):
                    hi_products(t, range(HM - 1, HM))
                pe.wait_ge(sems["lo"], (c + 1) * HM)
                for t in (0, 2):
                    lo_products(t)
                half_way()
                for t in (1, 3):
                    hi_products(t, range(HM))
                    ins = lo_products(t)
                ins.then_inc(sems["dn_ps"], 1)

            def dft(c):
                pe.wait_ge(h1_ok, c + 1)
                for j in range(2):
                    ins = mm(ps[0:4 * KF, 6 + j, 0:2 * C], dft_w[:, :],
                             h1[:, 2 * j:2 * j + 2, :].rearrange("p t c -> p (t c)"))
                ins.then_inc(fw_ps, 1)

            def block0(c, more):
                def project_next():
                    if is_at(c, 0):
                        ring_unit(NH - 1, 1, ("out", NQ - 1, 0), U_ALL - 1, FREE_BANK)
                    wait_used(pe, u_ok, c - 1)
                    project(c + 1)

                up(c, 0, up0, {2: lambda: attn_transposed(c + 1), 4: project_next} if more else {})
                if is_at(c, 0):
                    pe.wait_ge(unit_ok, U_ALL)
                else:
                    if more:
                        pe.wait_ge(x1_ok, c + 2)
                    else:
                        pe.wait_ge(u_ok, c - 1)
                    dft(c - 1)
                down(c, 0, up0, lambda: norm_transposed(c + 1, ln2, t2_ps) if more else None)

            pe.wait_ge(w_pair, 4)
            chunks(pe, block0)
            pe.wait_ge(u_ok, NC - 1)
            dft(NC - 1)

            def transform(g):
                pe.wait_ge(f_in_ok[g % 2], 32 * (g // 2 + 1))
                wait_used(pe, fx_ok, g)
                for k in range(2):
                    for f in range(KG):
                        ins = mm(ps[0:C2, k, f * 2 * S:(f + 1) * 2 * S], f_in[:, g % 2, f, k * C2:(k + 1) * C2],
                                 dft_h[:, 0, :])
                ins.then_inc(fh_ps, 1)

            def layer1(g):
                pe.wait_ge(fx_ok, g + 1)
                wait_used(pe, fa_ok, g)
                for k in range(2):
                    for r in range(2):
                        o = ps[0:C2, 2 + k, r * KG * S:(r + 1) * KG * S].rearrange("p (k h) -> p k h", h=S)
                        w_r, w_i = f_w[:, 0, k, 0, :], f_w[:, 0, k, 1, :]
                        mm(o, w_r, f_x[:, k, :, r, :], stop=False)
                        ins = mm(o, f_wn[:, k, :] if r == 0 else w_i, f_x[:, k, :, 1 - r, :], start=False)
                ins.then_inc(f1_ps, 1)

            def layer2(g):
                pe.wait_ge(fr_ok, g + 1)
                wait_used(pe, fu_ok, g)
                for f in range(KG):
                    for k in range(2):
                        o = ps[0:2 * S, 4 + f // 2, (f % 2) * C + k * C2:(f % 2) * C + (k + 1) * C2]
                        mm(o, f_a[:, k, f, :, :].rearrange("p r h -> p (r h)"), f_w[:, 1, k, 0, :], stop=False)
                        ins = mm(o, f_r[:, k, f, :, :].rearrange("p r h -> p (r h)"), f_w[:, 1, k, 1, :],
                                 start=False)
                ins.then_inc(f2_ps, 1)

            def inverse(g):
                pe.wait_ge(fo_ok, g + 1)
                for j in range(-(-KG // 2)):
                    w = min(2, KG - 2 * j)
                    ins = mm(ps[0:2 * S, 4 + j, 0:w * C], dft_h[:, 1, :],
                             f_o[:, 2 * j:2 * j + w, :].rearrange("p f c -> p (f c)"))
                ins.then_inc(fi_ps, 1)

            pe.wait_ge(fw_neg, 1)
            pe.wait_ge(up0["sum"], NC)
            pe.wait_ge(u_ok, NC)
            transform(0)
            for g in range(G):
                layer1(g)
                if g > 0:
                    inverse(g - 1)
                if g + 1 < G:
                    transform(g + 1)
                layer2(g)
            inverse(G - 1)

            def inverse_w(c):
                pe.wait_ge(u2_in, 16 * (c + 1))
                wait_used(pe, x3_ok, c)
                for j in range(2):
                    ins = mm(ps[0:T, 6 + j, 0:2 * C], idft_w[:, :],
                             u_sb[:, 2 * j:2 * j + 2, :].rearrange("p t c -> p (t c)"))
                ins.then_inc(iw_ps, 1)

            def block1(c, more):
                up(c, 1, up1, {2: lambda: inverse_w(c + 1)} if more else {})
                down(c, 1, up1, lambda: norm_transposed(c + 1, ln4, t4_ps) if more else None)

            pe.wait_ge(fu_ok, G)
            inverse_w(0)
            norm_transposed(0, ln4, t4_ps)
            chunks(pe, block1)

        @block.vector
        def _(dve):
            def norm1(c):
                dve.wait_ge(x_in[c % 2], 16 * (c // 2 + 1))
                norm_chunk(dve, nc, xin2[c % 2], stats, mv, rstd, xh2[c % 2], ln1, c,
                           lambda: wait_used(dve, t1_ps, c - 1))

            norm1(0)
            norm1(1)
            dve.wait_ge(rel_h16, 2)
            dve.wait_ge(first_in, FIRST)
            for i in range(2):
                nc.vector.scalar_tensor_tensor(out=rel_hi[i][:, :, :], in0=rel_hi[i][:, :, :],
                                               scalar=mask[0:S, 2:3], in1=rel[i][:, :, :],
                                               op0=ALU.mult, op1=ALU.add).then_inc(rel_pair, 1)
            for c in range(NC):
                if c + 2 < NC:
                    norm1(c + 2)
                for i in range(4):
                    dve.wait_ge(kq_hi, 4 * c + i + 1)
                    lo, hi, x = khl[:, c % 2, i, 1, :], khl[:, c % 2, i, 0, :], ps[0:C2, 2 + i, 0:CW]
                    nc.vector.tensor_tensor(lo, x, hi, ALU.subtract).then_inc(kq_lo, 1)
                dve.wait_ge(v_ps, c + 1)
                for j in range(3):
                    nc.vector.tensor_copy(v_all[:, :, ds(c * 3 + j, 1), :].rearrange("p n o c -> p n (o c)"),
                                          ps[:, 6 + j // 2, (j % 2) * C:(j % 2 + 1) * C]
                                          .rearrange("p (n c) -> p n c", c=HD)).then_inc(v_ok, 1)

            def operand(s, i, tile, par):
                g, ab = s // 2, s % 2
                dve.wait_ge(op_hi, tile + 1)
                st = stage[s % 2]
                if ab == 0:
                    o = st[:, :, ds(i * 2 * S, 2 * S)].rearrange("p n (r w) -> p r n w", r=2)
                else:
                    o = st[:, :, :].rearrange("p n (h w) -> p w n h", w=S)[:, ds(i * 2, 2), :, :]
                nc.vector.tensor_tensor(o, ps[:, 2 * par:2 * par + 2, 0:NG * S].rearrange("p r (n w) -> p r n w", n=NG),
                                        tmp16[:, par, :].rearrange("p (r n w) -> p r n w", r=2, n=NG),
                                        ALU.subtract).then_inc(op_out, 1)

            for p in range(2):
                dve.wait_ge(kq_out[p], 64 * NC // 2)
            dve.wait_ge(stat_done, 4)
            for s in range(4):
                if s >= 2:
                    dve.wait_ge(q_out[s % 2], 16)
                base = s * S // 2
                with dve.Fori(0, S // 8) as i:
                    for par in range(4):
                        operand(s, 4 * i + par, 4 * i + par + base, par)

            def lo_of_input(c, i):
                dve.wait_ge(x_hi, i * NC + c + 1)
                x = chunk_of(xnt_all, c)
                nc.vector.tensor_tensor(x[:, :, 1, :], xnt_f[:, :, :], x[:, :, 0, :], ALU.subtract).then_inc(x_lo, 1)

            def projected(c, bank=6):
                dve.wait_ge(pr_ps, c + 1)
                dve.wait_ge(xb_ok, c + 1)
                x1_c = x1[:, ds(c * CT, CT), :]
                nc.vector.tensor_tensor(x1_c.rearrange("p (a b) c -> p a (b c)", a=2), ps[0:T, bank:bank + 2, 0:2 * C],
                                        xb[:, :, :].rearrange("p (a b) c -> p a (b c)", a=2),
                                        ALU.add).then_inc(x1_ok, 1)
                dve.wait_ge(x1_ok, c + 1)
                norm_chunk(dve, nc, x1_c, stats, mv, rstd, xh2[0], ln2, c,
                           lambda: wait_used(dve, t2_ps, c))

            def ring_unit(n, p, unit, count, slot):
                kind, group, k = unit
                q = group % NQ
                dve.wait_ge(unit_ps, count + 1)
                if kind == "max":
                    if k == 0:
                        wait_used(dve, mx_red, 0 if is_at(n, 0) and group < NQ else n * NQ + group - 2)
                    nc.vector.tensor_reduce(mx_p[:, q * GT + k // MP, k % MP:k % MP + 1], ps[:, slot, 0:min(MW, N - k % MP * MW)], AX,
                                            ALU.max).then_inc(unit_ok, 1)
                    if k == GU - 1:
                        dve.wait_ge(unit_ok, count + 1)
                        nc.vector.tensor_reduce(mx[:, q * GT:(q + 1) * GT], mx_p[:, q * GT:(q + 1) * GT, :], AX,
                                                ALU.max).then_inc(mx_red, 1)
                elif kind == "mt":
                    if not (is_at(n, 0) and group == 0):
                        dve.wait_ge(m_out, 16 * (n * NQ + group))
                    nc.vector.tensor_scalar(mneg[:, :], ps[0:GT, slot, 0:128], -1.0, None,
                                            ALU.mult).then_inc(unit_ok, 1)
                else:
                    o = ps[0:T, slot, 0:2 * CT * (HD + 1)].rearrange("p (t h c) -> p h t c", h=2, c=HD + 1)
                    r = rden[:, :].rearrange("p (h t) -> p h t", h=2)
                    head = n - 1 if group < 0 else n
                    dve.wait_ge(unit_ok, count)
                    nc.vector.reciprocal(r, o[:, :, :, HD]).then_inc(den_ok, 1)
                    dve.wait_ge(den_ok, n * NQ + group + 1)
                    a = attn[:, 2 * CT * q:2 * CT * (q + 1), ds(head * HD, HD)]
                    nc.vector.tensor_tensor(a.rearrange("p (h t) c -> p h t c", h=2), o[:, :, :, 0:HD],
                                            r.unsqueeze(3).to_broadcast([T, 2, CT, HD]),
                                            ALU.mult).then_inc(unit_ok, 1)

            def period(n, p):
                for u, unit in enumerate(flat(n)):
                    if is_at(n, NH - 1) and unit[:2] == ("out", 1):
                        projected(0, 0)
                    ring_unit(n, p, unit, units_before(n) + u, ring_slot(n, p, u))

            for u, unit in enumerate(before):
                ring_unit(0, 0, unit, u, u % RING)
            period(0, 0)
            period(1, 1)
            with dve.Fori(1, NH // 2 - 1) as i:
                period(2 * i, 0)
                period(2 * i + 1, 1)
            period(NH - 2, 0)
            period(NH - 1, 1)
            lo_of_input(0, 0)
            ring_unit(NH - 1, 1, ("out", NQ - 1, 0), U_ALL - 1, FREE_BANK)
            wait_consts(dve)

            def mlp_sum(c, sems, res_ok, free):
                dve.wait_ge(sems["dn_ps"], c + 1)
                dve.wait_ge(res_ok, c + 1)
                free()
                nc.vector.scalar_tensor_tensor(out=y_sb[:, :, :].rearrange("p (a b) c -> p a (b c)", a=2),
                                               in0=ps[0:T, 2:4, 0:2 * C], scalar=1 / WS,
                                               in1=x1[:, ds(c * CT, CT), :].rearrange("p (a b) c -> p a (b c)", a=2),
                                               op0=ALU.mult, op1=ALU.add).then_inc(sems["sum"], 1)

            def block0(c, more):
                if more:
                    projected(c + 1)
                    lo_of_input(c + 1, 0)
                mlp_sum(c, up0, x1b_ok, lambda: wait_used(dve, r3_ok, c))
                dve.wait_ge(up0["sum"], c + 1)
                norm_chunk(dve, nc, y_sb, stats, mv, rstd, xh2[1], ln3, c, lambda: None)
                dve.wait_ge(ln3["out"], c + 1)
                wait_used(dve, fw_ps, c)
                wait_used(dve, r3_ok, c)
                nc.vector.tensor_tensor(h1[:, :, :], xh2[1][:, :, :],
                                        rows[:, 2:3, :].to_broadcast([T, CT, C]), ALU.mult).then_inc(h1_mul, 1)
                dve.wait_ge(h1_mul, c + 1)
                nc.vector.tensor_tensor(h1[:, :, :], h1[:, :, :],
                                        rows[:, 3:4, :].to_broadcast([T, CT, C]), ALU.add).then_inc(h1_ok, 1)

            chunks(dve, block0)

            for g in range(G):
                dve.wait_ge(fa_ok, g + 1)
                wait_used(dve, f2_ps, g)
                nc.vector.tensor_scalar(f_r[:, :, :, 0, :], f_a[:, :, :, 1, :], -1.0, None, ALU.mult)
                nc.vector.tensor_copy(f_r[:, :, :, 1, :], f_a[:, :, :, 0, :]).then_inc(fr_ok, 1)
                dve.wait_ge(f2_ps, g + 1)
                nc.vector.tensor_tensor(f_y[:, 0:4, :].rearrange("p (a b) c -> p a b c", a=2),
                                        ps[0:2 * S, 4:6, 0:2 * C].rearrange("p a (b c) -> p a b c", b=2),
                                        f_b2[:, :].unsqueeze(1).unsqueeze(1).to_broadcast([2 * S, 2, 2, C]), ALU.add)
                nc.vector.tensor_tensor(f_y[:, 4, :], ps[0:2 * S, 6, 0:C], f_b2[:, :], ALU.add).then_inc(fy_ok, 1)
                dve.wait_ge(fy_ok, g + 1)
                nc.vector.tensor_scalar(f_c[:, :, :], f_y[:, :, :], -LAM, LAM, ALU.max, ALU.min).then_inc(fc_ok, 1)
                dve.wait_ge(fc_ok, g + 1)
                wait_used(dve, fi_ps, g)
                nc.vector.tensor_tensor(f_o[:, :, :], f_y[:, :, :], f_c[:, :, :], ALU.subtract).then_inc(fo_ok, 1)

            dve.wait_ge(r3_ok, NC)

            def lo_of_hidden(c, tiles):
                for m in tiles:
                    dve.wait_ge(up1["hi"], c * HM + m + 1)
                    nc.vector.tensor_tensor(hid[:, m, 1, :], hid_f[:, m, :], hid[:, m, 0, :],
                                            ALU.subtract).then_inc(up1["lo"], 1)

            def inverse(c, beside_root):
                dve.wait_ge(iw_ps, c + 1)
                x3_c = x1[:, ds(c * CT, CT), :]
                nc.vector.tensor_tensor(x3_c.rearrange("p (a b) c -> p a (b c)", a=2), ps[0:T, 6:8, 0:2 * C],
                                        r3[:, ds(c * CT, CT), :].rearrange("p (a b) c -> p a (b c)", a=2),
                                        ALU.add).then_inc(x3_ok, 1)
                dve.wait_ge(x3_ok, c + 1)
                norm_chunk(dve, nc, x3_c, stats, mv, rstd, xh2[0], ln4, c,
                           lambda: wait_used(dve, t4_ps, c), beside_root)
                lo_of_input(c, 1)

            def block1(c, more):
                tiles = range(POOL_TILES, HM)
                if more:
                    inverse(c + 1, lambda: lo_of_hidden(c, tiles))
                else:
                    lo_of_hidden(c, tiles)
                mlp_sum(c, up1, x3b_ok, lambda: wait_used(dve, y_out, 16 * c))

            inverse(0, lambda: None)
            chunks(dve, block1)

        assert NCONST[0] == ALL_CONSTS, (NCONST[0], ALL_CONSTS)


_FLAT = ("L0_conv_qkv_w", "L0_conv_proj_w", "L0_conv_proj_b", "L0_conv_ln1_g", "L0_conv_ln1_b", "L0_conv_ln2_g",
         "L0_conv_ln2_b", "L0_conv_mlp_w1", "L0_conv_mlp_b1", "L0_conv_mlp_w2", "L0_conv_mlp_b2", "L1_conv_g1",
         "L1_conv_be1", "L1_conv_g2", "L1_conv_be2", "L1_conv_fc1_w", "L1_conv_fc1_b", "L1_conv_fc2_w",
         "L1_conv_fc2_b")


def constants():
    import numpy as np

    r = np.arange(S)
    c = {"c_ident": np.eye(128, dtype=np.float32)}
    mask = np.zeros((128, 3), np.float32)
    mask[HD:2 * HD, 0] = 1.0
    for i in range(3):
        mask[2 * HD + (2 * i + 1) * R3:2 * HD + (2 * i + 2) * R3, 0] = 1.0
        mask[HD + (2 * i + 1) * R3:HD + (2 * i + 2) * R3, 1] = 1.0
    mask[2 * HD:3 * HD, 2] = -1.0
    c["c_mask"] = mask
    rh = S - 1 - (np.arange(6)[:, None, None, None] * 8 + np.arange(8)[:, None]) + np.zeros((6, 3, 8, R3), int)
    rw = S - 1 - (np.arange(3)[:, None, None] * R3 + np.arange(R3)) + np.zeros((6, 3, 8, R3), int)
    rh, rw = rh.reshape(N), rw.reshape(N)
    x = np.arange(R3)[:, None]
    row, col = rh % R3 == x, rw % R3 == x
    c["c_onehot"] = np.concatenate([row, row, col, col, np.ones((1, N))]).astype(np.float16)
    c["c_onehot_c"] = np.concatenate([rh == r[:, None], rw == r[:, None]]).astype(np.float16)
    esel = np.zeros((S, 2 * HD), np.float16)
    for j in range(HD):
        for a in range(2):
            for b in range(2):
                esel[a * HD + j, b * HD + j] = 1.0
    c["c_esel"] = esel
    sel = np.zeros((128, 2, HD + 1), np.float32)
    for half in range(2):
        for e in range(2):
            for j in range(HD + 1):
                sel[32 * (2 * e + half) + j, half, j] = 1.0
    c["c_sel"] = sel
    ang = 2 * np.pi * (np.outer(r, np.arange(KF)) % S) / S
    dw, iw = np.zeros((2, S, 2, 2, KF)), np.zeros((2, 2, KF, 2, S))
    wt = np.where((np.arange(KF) == 0) | (np.arange(KF) == S // 2), 1.0, 2.0)[:, None]
    for a in range(2):
        dw[a, :, a, 0], dw[a, :, a, 1] = np.cos(ang), -np.sin(ang)
        iw[a, 0, :, a], iw[a, 1, :, a] = wt * np.cos(ang).T / S, -wt * np.sin(ang).T / S
    c["c_dft_w"] = (dw / S).reshape(T, 4 * KF).astype(np.float32)
    c["c_idft_w"] = iw.reshape(4 * KF, T).astype(np.float32)
    ang = 2 * np.pi * (np.outer(r, r) % S) / S
    co, si = np.cos(ang), np.sin(ang)
    fwd = np.block([[co, -si], [si, co]])
    inv = np.block([[co, si], [-si, co]])
    c["c_dft_h"] = np.stack([fwd, inv], 1).astype(np.float32)
    return c


def kernel(**inputs):
    import numpy as np
    import concourse.bacc as bacc
    from concourse.bass_utils import run_bass_kernel_spmd as run

    nc = bacc.Bacc("TRN2", target_bir_lowering=False, num_devices=1)
    arrays = {"x": np.ascontiguousarray(inputs["x"]).reshape(N, C),
              "L0_conv_qkv_b": np.ascontiguousarray(inputs["L0_conv_qkv_b"]).reshape(1, 3 * C)}
    for name in _FLAT:
        arrays[name] = np.ascontiguousarray(inputs[name])
    for short, name in (("c_rel_h", "L0_conv_rel_pos_h"), ("c_rel_w", "L0_conv_rel_pos_w")):
        table = np.ascontiguousarray(inputs[name])
        win = np.stack([table[i:i + S] for i in range(S)])
        arrays[short] = np.ascontiguousarray(np.concatenate([win.transpose(2, 0, 1)] * 3))
    arrays["f_w"] = np.ascontiguousarray(np.stack([np.ascontiguousarray(inputs[n]).transpose(3, 0, 1, 2)
                                                   for n in ("L1_conv_w1", "L1_conv_w2")]))
    for short, name in (("f_b1", "L1_conv_b1"), ("f_b2", "L1_conv_b2")):
        arrays[short] = np.ascontiguousarray(np.ascontiguousarray(inputs[name]).transpose(2, 0, 1).reshape(2, C))
    arrays.update(constants())
    d = {k: nc.dram_tensor(f"in_{k}", a.shape, mybir.dt.from_np(a.dtype), kind="ExternalInput").ap()
         for k, a in arrays.items()}
    out = nc.dram_tensor("out_0", (N, C), F32, kind="ExternalOutput").ap()
    build(nc, d, out)
    r = run(nc, [{f"in_{k}": a for k, a in arrays.items()}], core_ids=[0])
    return r.results[0]["out_0"].reshape(1, S, S, C)
```
